# Optimizing a Trainium2 kernel written in Bass

```python
import numpy as np
import jax
import jax.numpy as jnp

def _softmax(x, axis=-1):
    return jax.nn.softmax(x, axis=axis)

def _gelu(x):
    return jax.nn.gelu(x, approximate=True)

def _silu(x):
    return jax.nn.silu(x)

def _sigmoid(x):
    return jax.nn.sigmoid(x)

def _layernorm(x, axis=-1, eps=1e-05):
    m = jnp.mean(x, axis=axis, keepdims=True)
    v = jnp.var(x, axis=axis, keepdims=True)
    return (x - m) / jnp.sqrt(v + eps)

def _scatter_add(tgt, idx, src, axis=0):
    return tgt.at[idx].add(src)

def _segment_sum(src, seg, n):
    return jax.ops.segment_sum(src, seg, n)
kernel_name = 'mk_flamingo_gated_d1_seqx_r8_7c6253'

def setup_inputs(seed: int=0):
    np.random.seed(seed)
    _w = jnp.asarray

    def _rec_inputs():
        import jax
        import jax.numpy as jnp
        _rk = jax.random.key(seed)
        x = -0.0005207 + 1.001 * jax.random.normal(jax.random.fold_in(_rk, 1), (64, 64, 256), jnp.float32)
        _lenS = 64 - jax.random.randint(jax.random.fold_in(_rk, 7), (64,), 0, max(1, 64 // 4) + 1, jnp.int32)
        _lenS2 = 64 - jax.random.randint(jax.random.fold_in(_rk, 8), (64,), 0, max(1, 64 // 4) + 1, jnp.int32)
        _ctx_2048P = jax.random.normal(jax.random.fold_in(_rk, 11), (64, 16, 256), jnp.float32)
        _ctx_2048c = jax.random.dirichlet(jax.random.fold_in(_rk, 511), 0.3 * jnp.ones((16,), jnp.float32), (64, 64))
        _ctx_2048t = jnp.einsum('bsk,bkd->bsd', _ctx_2048c, _ctx_2048P)
        _ctx_2048t = _ctx_2048t * jax.lax.rsqrt(jnp.mean(jnp.square(_ctx_2048t)) + 1e-12) * 0.953939
        ctx_2048 = 2.81802e-05 + 1.00001 * (_ctx_2048t + 0.3 * jax.random.normal(jax.random.fold_in(_rk, 611), (64, 64, 256), jnp.float32))
        pos_BxS2 = jnp.broadcast_to(jnp.arange(64, dtype=jnp.int32), (64, 64))
        itok_BxS_4096_4607 = jax.random.randint(jax.random.fold_in(_rk, 13), (64, 64), 512, 576, jnp.int32)
        _g = jax.random.normal(jax.random.fold_in(_rk, 9001), (2, 1), jnp.float32)
        _g = jnp.sign(_g) * jnp.maximum(jnp.abs(_g), 1.0) + (_g == 0) * 1.0
        g_xattn = _g[0]
        g_ffn = _g[1]
        return (x, ctx_2048, pos_BxS2, itok_BxS_4096_4607, g_xattn, g_ffn)
    x, ctx_2048, pos_BxS2, itok_BxS_4096_4607, g_xattn, g_ffn = _rec_inputs()

    def _L0_xattn_setup():
        import jax, jax.numpy as jnp
        import numpy as np
        B, CTX, DRAFT, D = (2, 512, 64, 256)
        H, KVH, HD = (16, 4, 128)
        N_REP = H // KVH
        EPS = 1e-06
        THETA = 10000.0
        SCALE = 1.0 / np.sqrt(HD).astype(np.float32)

        def _rms_norm(x, w):
            v = jnp.mean(jnp.square(x.astype(jnp.float32)), axis=-1, keepdims=True)
            return (w * (x.astype(jnp.float32) * jax.lax.rsqrt(v + EPS))).astype(x.dtype)

        def _rotate_half(x):
            x1, x2 = jnp.split(x, 2, axis=-1)
            return jnp.concatenate((-x2, x1), axis=-1)

        def _rope(x, pos):
            inv_freq = 1.0 / THETA ** (jnp.arange(0, HD, 2, dtype=jnp.float32) / HD)
            freqs = pos.astype(jnp.float32)[:, None, :, None] * inv_freq
            emb = jnp.concatenate((freqs, freqs), axis=-1)
            return x * jnp.cos(emb) + _rotate_half(x) * jnp.sin(emb)
        key = jax.random.key(seed)
        ks = jax.random.split(key, 6)
        return {'draft_hidden': jax.random.normal(ks[0], (B, DRAFT, D), jnp.float32), 'context_hidden': jax.random.normal(ks[1], (B, CTX, D), jnp.float32), 'Wq': jax.random.normal(ks[2], (H * HD, D), jnp.float32) * 0.02, 'Wk': jax.random.normal(ks[3], (KVH * HD, D), jnp.float32) * 0.02, 'Wv': jax.random.normal(ks[4], (KVH * HD, D), jnp.float32) * 0.02, 'Wo': jax.random.normal(ks[5], (D, H * HD), jnp.float32) * 0.02, 'q_norm_w': jnp.ones((HD,), jnp.float32), 'k_norm_w': jnp.ones((HD,), jnp.float32), 'context_position_ids': jnp.broadcast_to(jnp.arange(CTX, dtype=jnp.int32), (B, CTX)), 'draft_position_ids': jnp.broadcast_to(CTX + jnp.arange(DRAFT, dtype=jnp.int32), (B, DRAFT))}
    _L0_xattn_all = _L0_xattn_setup()
    _L0_xattn_in = {k: v for k, v in _L0_xattn_all.items() if k in ('Wq', 'Wk', 'Wv', 'Wo', 'q_norm_w', 'k_norm_w')}
    del _L0_xattn_all

    def _L0_ffn_setup():
        import jax, jax.numpy as jnp
        import numpy as np
        HID = 256
        E = 8
        TOP_K = 2
        F = 176
        FS = 352
        SCALE = 2.5
        key = jax.random.key(seed)
        ks = jax.random.split(key, 8)
        s = 0.02
        return {'hidden_states': jax.random.normal(ks[0], (1, 256, HID), jnp.float32), 'w_router': jax.random.normal(ks[1], (HID, E), jnp.float32) * s, 'w_gate': jax.random.normal(ks[2], (E, HID, F), jnp.float32) * s, 'w_up': jax.random.normal(ks[3], (E, HID, F), jnp.float32) * s, 'w_down': jax.random.normal(ks[4], (E, F, HID), jnp.float32) * s, 'ws_gate': jax.random.normal(ks[5], (HID, FS), jnp.float32) * s, 'ws_up': jax.random.normal(ks[6], (HID, FS), jnp.float32) * s, 'ws_down': jax.random.normal(ks[7], (FS, HID), jnp.float32) * s}
    _L0_ffn_all = _L0_ffn_setup()
    _L0_ffn_in = {k: v for k, v in _L0_ffn_all.items() if k in ('w_router', 'w_gate', 'w_up', 'w_down', 'ws_gate', 'ws_up', 'ws_down')}
    del _L0_ffn_all
    return {'x': x, 'ctx_2048': ctx_2048, 'pos_BxS2': pos_BxS2, 'itok_BxS_4096_4607': itok_BxS_4096_4607, 'g_xattn': g_xattn, 'g_ffn': g_ffn, 'L0_xattn_Wq': _L0_xattn_in['Wq'], 'L0_xattn_Wk': _L0_xattn_in['Wk'], 'L0_xattn_Wv': _L0_xattn_in['Wv'], 'L0_xattn_Wo': _L0_xattn_in['Wo'], 'L0_xattn_q_norm_w': _L0_xattn_in['q_norm_w'], 'L0_xattn_k_norm_w': _L0_xattn_in['k_norm_w'], 'L0_ffn_w_router': _L0_ffn_in['w_router'], 'L0_ffn_w_gate': _L0_ffn_in['w_gate'], 'L0_ffn_w_up': _L0_ffn_in['w_up'], 'L0_ffn_w_down': _L0_ffn_in['w_down'], 'L0_ffn_ws_gate': _L0_ffn_in['ws_gate'], 'L0_ffn_ws_up': _L0_ffn_in['ws_up'], 'L0_ffn_ws_down': _L0_ffn_in['ws_down']}

def reference(x, ctx_2048, pos_BxS2, itok_BxS_4096_4607, g_xattn, g_ffn, L0_xattn_Wq, L0_xattn_Wk, L0_xattn_Wv, L0_xattn_Wo, L0_xattn_q_norm_w, L0_xattn_k_norm_w, L0_ffn_w_router, L0_ffn_w_gate, L0_ffn_w_up, L0_ffn_w_down, L0_ffn_ws_gate, L0_ffn_ws_up, L0_ffn_ws_down):
    import jax
    import jax.numpy as jnp

    def _L0_xattn_ref(draft_hidden, context_hidden, Wq, Wk, Wv, Wo, q_norm_w, k_norm_w, context_position_ids, draft_position_ids):
        import jax, jax.numpy as jnp
        import numpy as np
        B, CTX, DRAFT, D = (2, 512, 64, 256)
        H, KVH, HD = (16, 4, 128)
        N_REP = H // KVH
        EPS = 1e-06
        THETA = 10000.0
        SCALE = 1.0 / np.sqrt(HD).astype(np.float32)

        def _rms_norm(x, w):
            v = jnp.mean(jnp.square(x.astype(jnp.float32)), axis=-1, keepdims=True)
            return (w * (x.astype(jnp.float32) * jax.lax.rsqrt(v + EPS))).astype(x.dtype)

        def _rotate_half(x):
            x1, x2 = jnp.split(x, 2, axis=-1)
            return jnp.concatenate((-x2, x1), axis=-1)

        def _rope(x, pos):
            inv_freq = 1.0 / THETA ** (jnp.arange(0, HD, 2, dtype=jnp.float32) / HD)
            freqs = pos.astype(jnp.float32)[:, None, :, None] * inv_freq
            emb = jnp.concatenate((freqs, freqs), axis=-1)
            return x * jnp.cos(emb) + _rotate_half(x) * jnp.sin(emb)
        bsz, draft_len, _ = draft_hidden.shape
        ctx_len = context_hidden.shape[1]
        total_len = ctx_len + draft_len
        q = (draft_hidden @ Wq.T).reshape(bsz, draft_len, H, HD)
        q = _rms_norm(q, q_norm_w).transpose(0, 2, 1, 3)
        kv_in = jnp.concatenate([context_hidden, draft_hidden], axis=1)
        k = (kv_in @ Wk.T).reshape(bsz, total_len, KVH, HD)
        v = (kv_in @ Wv.T).reshape(bsz, total_len, KVH, HD).transpose(0, 2, 1, 3)
        k = _rms_norm(k, k_norm_w).transpose(0, 2, 1, 3)
        full_position_ids = jnp.concatenate([context_position_ids, draft_position_ids], axis=1)
        q = _rope(q, draft_position_ids)
        k = _rope(k, full_position_ids)
        k = jnp.repeat(k, N_REP, axis=1)
        v = jnp.repeat(v, N_REP, axis=1)
        scores = jnp.einsum('bhqd,bhkd->bhqk', q, k) * SCALE
        probs = jax.nn.softmax(scores, axis=-1)
        attn = jnp.einsum('bhqk,bhkd->bhqd', probs, v)
        attn = attn.transpose(0, 2, 1, 3).reshape(bsz, draft_len, H * HD)
        return attn @ Wo.T

    def _L0_ffn_ref(hidden_states, w_router, w_gate, w_up, w_down, ws_gate, ws_up, ws_down):
        import jax, jax.numpy as jnp
        import numpy as np
        HID = 256
        E = 8
        TOP_K = 2
        F = 176
        FS = 352
        SCALE = 2.5
        B, S, D = hidden_states.shape
        x = hidden_states.reshape(-1, D)
        T = x.shape[0]
        probs = jax.nn.softmax(x @ w_router, axis=-1)
        top_v, top_i = jax.lax.top_k(probs, TOP_K)
        top_v = top_v / jnp.sum(top_v, axis=-1, keepdims=True)
        combine = jnp.zeros((T, E), x.dtype).at[jnp.arange(T)[:, None], top_i].set(top_v)
        g = jax.nn.silu(jnp.einsum('td,edf->etf', x, w_gate))
        u = jnp.einsum('td,edf->etf', x, w_up)
        y = jnp.einsum('etf,efd->etd', g * u, w_down)
        routed = jnp.einsum('etd,te->td', y, combine) * SCALE
        shared = jax.nn.silu(x @ ws_gate) * (x @ ws_up) @ ws_down
        return (routed + shared).reshape(B, S, D)
    x = x + jnp.tanh(g_xattn[0]) * _L0_xattn_ref(_layernorm(x, axis=-1), ctx_2048, L0_xattn_Wq, L0_xattn_Wk, L0_xattn_Wv, L0_xattn_Wo, L0_xattn_q_norm_w, L0_xattn_k_norm_w, pos_BxS2, itok_BxS_4096_4607)
    x = x + jnp.tanh(g_ffn[0]) * _L0_ffn_ref(_layernorm(x, axis=-1), L0_ffn_w_router, L0_ffn_w_gate, L0_ffn_w_up, L0_ffn_w_down, L0_ffn_ws_gate, L0_ffn_ws_up, L0_ffn_ws_down)
    return x

_drawn_inputs = setup_inputs


def setup_inputs(seed=0):
    import zlib

    import numpy as np

    out = dict(_drawn_inputs(seed))
    spreads = {'L0_xattn_q_norm_w': (1.0, 0.6), 'L0_xattn_k_norm_w': (1.0, 0.6)}
    factors = {'L0_ffn_w_router': 8.733,
     'L0_ffn_ws_gate': 3.065,
     'L0_ffn_ws_up': 3.034,
     'L0_ffn_ws_down': 3.031,
     'L0_ffn_w_gate': 2.76,
     'L0_ffn_w_up': 2.728,
     'L0_ffn_w_down': 2.725}
    for name, (base, spread) in spreads.items():
        noise = np.random.default_rng([zlib.crc32(name.encode()), seed]).standard_normal(out[name].shape)
        drawn = base * np.exp(spread * noise) if base else spread * noise
        out[name] = jnp.asarray(drawn.astype(out[name].dtype))
    for name, factor in factors.items():
        out[name] = (out[name] * factor).astype(out[name].dtype)
    return out
```

```python
import concourse.bass as bass
from concourse import mybir
from contextlib import ExitStack
import numpy as np

F32 = mybir.dt.float32
F32R = mybir.dt.float32r
I32 = mybir.dt.int32
U32 = mybir.dt.uint32
BF16 = mybir.dt.bfloat16
ALU = mybir.AluOpType
ACT = mybir.ActivationFunctionType
AX = mybir.AxisListType

P = 128
B, S, D = 64, 64, 256
H, KVH, HD = 16, 4, 128
REP = H // KVH
NB = P // S
TILES = B * S // P
PAIRS = TILES // 2
DC = D // P
HALF = HD // 2
E, TOPK, F, FS = 8, 2, 176, 352
BLOCKS = 1 + E // 2
FB = FS
FC = -(-FB // P)
FW = FC * P
ROUTED_SCALE = 2.5
SCALE = float(np.float32(1.0) / np.sqrt(np.float32(HD)))
RMS_EPS, LN_EPS = 1e-6, 1e-5
TWO_PI = (6.28125, 0.0019350051879882812, 2 * np.pi - 6.28125 - 0.0019350051879882812)
ROUND = 1.5 * 2.0 ** 23
PI_BELOW = 3.1415925
PASSES = ((0, 0), (0, 1), (1, 0))
HI, LO = 0, 1


def need(eng, sem, count):
    if not isinstance(count, int) or count > 0:
        eng.wait_ge(sem, count)


def walk(eng, body):
    body(0, True, False)
    with eng.Fori(1, PAIRS - 1) as i:
        body(i, False, False)
    body(PAIRS - 1, False, True)


def flamingo(nc, x, ctxT, posx, posc, invf, g_xattn, g_ffn, q_w, k_w, wq, wkv, wo, wr, wg, wd, out):
    ctx = ExitStack()
    with ctx:
        cursor = [-(-nc.sbuf_base // 64) * 64]

        def sb(name, shape, dt, at=None):
            size = int(np.prod(shape[1:])) * mybir.dt.size(dt)
            where = cursor if at is None else at
            t = nc.alloc_sbuf_tensor_at(name, shape, dt, offset=where[0])
            where[0] += -(-size // 64) * 64
            return t

        def parts(name, shape, at=None):
            return [sb(f"{name}_{p}", shape, F32R, at) for p in ("hi", "lo")]

        ident = sb("ident", [P, P], F32)
        gates = sb("gates", [P, 2], F32)
        gates_raw = sb("gates_raw", [P, 2], F32)
        minus_half = sb("minus_half", [P, 8], F32)
        eps_rms = sb("eps_rms", [P, 8], F32)
        eps_ln = sb("eps_ln", [P, 1], F32)
        half_pi = sb("half_pi", [P, 1], F32)
        expert_no = sb("expert_no", [P, E], F32)
        ln_stats = sb("ln_stats", [P, 6], F32)
        ln_mv = sb("ln_mv", [P, 2, 2], F32)
        ln_ve = sb("ln_ve", [P, 2], F32)
        ln_rstd = sb("ln_rstd", [P, 2], F32)
        stage_at = list(cursor)
        wg_raw = sb("wg_raw", [P, DC, BLOCKS, 2 * FB], F32)
        wd_raw = sb("wd_raw", [P, BLOCKS, FC, D], F32)
        wr_raw = sb("wr_raw", [P, DC, E], F32)
        wq_raw = sb("wq_raw", [P, DC, H * HD], F32, stage_at)
        wkv_raw = sb("wkv_raw", [P, DC, KVH, 2 * HD], F32, stage_at)
        wo_raw = sb("wo_raw", [P, H, D], F32, stage_at)
        assert stage_at[0] <= cursor[0]
        phase_at = list(cursor)
        wq_s = parts("wq", [P, DC, H * HD])
        wkv_s = parts("wkv", [P, DC, KVH, 2 * HD])
        wo_s = parts("wo", [P, H, D])
        w_cos = sb("w_cos", [P, 3, 2, HALF], F32)
        w_sin = sb("w_sin", [P, 3, 2, HALF], F32)
        trig_raw = [sb(f"trig_raw{p}", [P, 3, 2, HALF], F32) for p in range(2)]
        cos_w = [sb(f"cos_w{p}", [P, 3, 2, HALF], F32) for p in range(2)]
        sin_w = [sb(f"sin_w{p}", [P, 3, 2, HALF], F32) for p in range(2)]
        x_in = [sb(f"x_in{p}", [P, D], F32) for p in range(2)]
        x_res = [sb(f"x_res{p}", [P, D], F32) for p in range(2)]
        x1_out = [sb(f"x1_out{p}", [P, D], F32) for p in range(2)]
        ctx_raw = [sb(f"ctx_raw{p}", [P, DC, P], F32) for p in range(2)]
        x_n = sb("x_n", [P, D], F32)
        kv_in = [parts(f"kv_in{p}", [P, DC, 4, S]) for p in range(2)]
        junk = sb("junk", [P, REP + NB, HD], BF16)
        q_ms = [sb(f"q_ms{p}", [P, REP], F32) for p in range(2)]
        k_ms = [sb(f"k_ms{p}", [P, NB], F32) for p in range(2)]
        q_me = sb("q_me", [P, REP], F32)
        k_me = sb("k_me", [P, NB], F32)
        q_r = [sb(f"q_r{p}", [P, REP], F32) for p in range(2)]
        k_r = [sb(f"k_r{p}", [P, NB], F32) for p in range(2)]
        q_rot = [sb(f"q_rot{p}", [P, REP, HD], F32) for p in range(2)]
        q_sin = [sb(f"q_sin{p}", [P, REP, HD], F32) for p in range(2)]
        k_rot = [sb(f"k_rot{p}", [P, NB, HD], F32) for p in range(2)]
        k_sin = [sb(f"k_sin{p}", [P, NB, HD], F32) for p in range(2)]
        v_s = [parts(f"v{g}", [P, NB, HD]) for g in range(KVH)]
        early_at = list(cursor)
        qT = parts("qT", [P, NB, REP, S])
        kT = parts("kT", [P, NB, P])
        probs = sb("probs", [P, REP, P], F32)
        pT = parts("pT", [P, NB, REP * S])
        aT = parts("aT", [P, REP, NB, S])
        early_end = cursor[0]
        row_max = sb("row_max", [P, REP], F32)
        neg_max = [sb(f"neg_max{p}", [P, REP], F32) for p in range(2)]
        row_sum = [sb(f"row_sum{p}", [P, REP], F32) for p in range(2)]
        row_inv = [sb(f"row_inv{p}", [P, REP], F32) for p in range(2)]
        NCH = 4
        CH = 2 * TILES // NCH
        ang = [sb(f"ang{p}", [P, CH, HALF], F32, early_at) for p in range(2)]
        sincos = sb("sincos", [P, CH, 2, HALF], F32, early_at)
        turn = sb("turn", [P, CH, HALF], F32)
        invf_s = sb("invf_s", [P, HALF], F32)
        pos_i = sb("pos_i", [P, 2 * TILES], I32)
        pos_f = sb("pos_f", [P, 2 * TILES], F32)
        assert early_at[0] <= early_end and cursor[0] <= nc.sbuf_usable_end, cursor
        wg_s = parts("wg", [P, DC, BLOCKS, 2 * FB], phase_at)
        wd_s = parts("wd", [P, BLOCKS, FC, D], phase_at)
        wr_s = parts("wr", [P, DC, E], phase_at)
        y_in = [sb(f"y_in{p}", [P, D], F32, phase_at) for p in range(2)]
        y_res = [sb(f"y_res{p}", [P, D], F32, phase_at) for p in range(2)]
        y_n = sb("y_n", [P, D], F32, phase_at)
        yT = [parts(f"yT{p}", [P, DC, P], phase_at) for p in range(2)]
        logits = sb("logits", [P, E], F32, phase_at)
        top_v = sb("top_v", [P, 8], F32, phase_at)
        top_i = sb("top_i", [P, 8], U32, phase_at)
        top_f = sb("top_f", [P, TOPK], F32, phase_at)
        lead = sb("lead", [P, 1], F32, phase_at)
        lead_t = sb("lead_t", [P, 1], F32, phase_at)
        share = sb("share", [P, TOPK], F32, phase_at)
        pick = sb("pick", [P, TOPK, E], F32, phase_at)
        combine = [sb(f"combine{p}", [P, E], F32, phase_at) for p in range(2)]
        silu = [sb(f"silu{p}", [P, FB], F32, phase_at) for p in range(2)]
        hid = [sb(f"hid{p}", [P, FW], F32, phase_at) for p in range(2)]
        hT = parts("hT", [P, FC, P], phase_at)
        o_out = [sb(f"o_out{p}", [P, D], F32, phase_at) for p in range(2)]
        assert phase_at[0] <= cursor[0]

        trig = nc.dram_tensor("trig_scratch", (2, TILES, P, 2, HALF), F32, kind="Internal").ap()
        x1_dram = nc.dram_tensor("x1_scratch", (TILES, P, D), F32, kind="Internal").ap()

        def bank(name):
            return ctx.enter_context(nc.psum_tensor(name, [P, 512], F32))

        b_q, b_kv, b_qT, b_kT, b_sc, b_pT, b_aT, b_o = [
            bank(n) for n in ("b_q", "b_kv", "b_qT", "b_kT", "b_sc", "b_pT", "b_aT", "b_o")]
        b_gate, b_up, b_hT, b_yT, b_y = [b_q, b_kv], [b_qT, b_kT], b_sc, b_pT, [b_aT, b_o]

        def sem(name):
            return ctx.enter_context(nc.semaphore(name))

        ld_const, ld_wq, ld_wkv, ld_wo, ld_w2 = map(sem, ("ld_const", "ld_wq", "ld_wkv", "ld_wo", "ld_w2"))
        ld_x, ld_ctx, ld_trig, ld_res, ld_y, ld_yres = [[sem(f"{n}{p}") for p in range(2)] for n in
                                               ("ld_x", "ld_ctx", "ld_trig", "ld_res", "ld_y", "ld_yres")]
        st_trig, = map(sem, ("st_trig",))
        st_x1, st_out = [[sem(f"{n}{p}") for p in range(2)] for n in ("st_x1", "st_out")]
        consts_set, ident_done, pos_ready, wsin_ready, angle_step, angle_ready, sin_ready, gates_ready = map(sem, (
            "consts_set", "ident_done", "pos_ready", "wsin_ready", "angle_step", "angle_ready", "sin_ready",
            "gates_ready"))
        abs_ready = sem("abs_ready")
        w_hi, w_lo = sem("w_hi"), sem("w_lo")
        q_done, kv_done, qT_done, kT_done, sc_done, pT_done, aT_done, o_done, xT_done = map(sem, (
            "q_done", "kv_done", "qT_done", "kT_done", "sc_done", "pT_done", "aT_done", "o_done", "xT_done"))
        q_sq, k_sq, q_hi, k_hi, exp_done, pT_hi, aT_hi, x_hi, ctx_hi = map(sem, (
            "q_sq", "k_sq", "q_hi", "k_hi", "exp_done", "pT_hi", "aT_hi", "x_hi", "ctx_hi"))
        (v_lo, k_lo, q_lo, k_turned, q_turned, max_found, max_ready, pT_lo, inv_ready, aT_lo, stats_done, ln_var,
         x_normed, x_lo, ctx_lo, x1_ready) = map(sem, (
             "v_lo", "k_lo", "q_lo", "k_turned", "q_turned", "max_found", "max_ready", "pT_lo", "inv_ready", "aT_lo",
             "stats_done", "ln_var", "x_normed", "x_lo", "ctx_lo", "x1_ready"))
        p_normed, k_me_done, k_r_ready, q_me_done, q_r_ready, q_summed, q_ready, k_ready, ve_done, rstd_ready, \
            cos_ready, sin_w_ready = map(sem, (
                "p_normed", "k_me_done", "k_r_ready", "q_me_done", "q_r_ready", "q_summed", "q_ready", "k_ready",
                "ve_done", "rstd_ready", "cos_ready", "sin_w_ready"))
        w2_hi, w2_lo, pad_done = map(sem, ("w2_hi", "w2_lo", "pad_done"))
        gu_done, hT_done, y_done, yT_done, lg_done = map(sem, ("gu_done", "hT_done", "y_done", "yT_done", "lg_done"))
        silu_done, hT_hi, yT_hi, lead_done = map(sem, ("silu_done", "hT_hi", "yT_hi", "lead_done"))
        (stats2, var2, y_normed, yT_lo, lg_copied, top_found, idx_found, lead_ready, share_ready, pick_ready,
         combine_ready, hid_ready, hT_lo, out_ready) = map(sem, (
             "stats2", "var2", "y_normed", "yT_lo", "lg_copied", "top_found", "idx_found", "lead_ready",
             "share_ready", "pick_ready", "combine_ready", "hid_ready", "hT_lo", "out_ready"))
        ve2_done, rstd2_ready = sem("ve2_done"), sem("rstd2_ready")

        SPLITS = 4 + 2 + 4
        N_CONST = 13

        block = ctx.enter_context(nc.Block())

        def split_pieces():
            for c in range(4):
                yield tuple(w[:, :, 512 * c:512 * c + 512] for w in (wq_raw, *wq_s)) + (ld_wq,)
                if c % 2 == 0:
                    yield tuple(w[:, c // 2, :, :] for w in (wkv_raw, *wkv_s)) + (ld_wkv,)
            for c in range(4):
                yield tuple(w[:, 4 * c:4 * c + 4, :] for w in (wo_raw, *wo_s)) + (ld_wo,)

        def split2_pieces():
            yield wr_raw[:], wr_s[HI][:], wr_s[LO][:]
            for k in range(BLOCKS):
                for c in range(DC):
                    yield tuple(w[:, c, k, :] for w in (wg_raw, *wg_s))
                yield tuple(w[:, k, :, :] for w in (wd_raw, *wd_s))

        W2_READY = [1 + 3 * (k + 1) for k in range(BLOCKS)]

        @block.sync
        def _(sp):
            sp.dma_start(pos_i[:, 0:TILES], posc).then_inc(ld_const, 16)
            sp.dma_start(pos_i[:, TILES:2 * TILES], posx).then_inc(ld_const, 16)
            sp.dma_start(invf_s[:], invf).then_inc(ld_const, 16)
            sp.dma_start(wq_raw[:], wq).then_inc(ld_wq, 16)
            sp.dma_start(wkv_raw[:], wkv).then_inc(ld_wkv, 16)
            for n, w in ((0, q_w), (1, k_w), (2, k_w)):
                row = w.rearrange("(a n) -> a n", a=1)
                sp.dma_start(w_cos[:, n, :, :].rearrange("p a b -> p (a b)"),
                             row.to_broadcast([P, HD])).then_inc(ld_const, 16)
                sp.dma_start(w_sin[:, n, 0, :], row[:, HALF:HD].to_broadcast([P, HALF])).then_inc(ld_const, 16)
                sp.dma_start(w_sin[:, n, 1, :], row[:, 0:HALF].to_broadcast([P, HALF])).then_inc(ld_const, 16)
            sp.dma_start(gates_raw[:, 0:1], g_xattn.rearrange("(a n) -> a n", a=1).to_broadcast([P, 1])) \
              .then_inc(ld_const, 16)
            sp.dma_start(wo_raw[:], wo).then_inc(ld_wo, 16)

            def load_tile(t, i, p):
                need(sp, x_normed, t - 1)
                sp.dma_start(x_in[p][:], x[bass.ds(t, 1), :, :].rearrange("a p n -> p (a n)")).then_inc(ld_x[p], 16)
                need(sp, ctx_lo, t - 1)
                sp.dma_start(ctx_raw[p][:], ctxT[bass.ds(t, 1), :, :, :].rearrange("a p c n -> p (a c) n")) \
                  .then_inc(ld_ctx[p], 16)
                need(sp, sin_w_ready, t - 1)
                t_x = trig[1, bass.ds(t, 1), :, :, :].rearrange("a p c n -> p (a c n)")
                t_c = trig[0, bass.ds(t, 1), :, :, :].rearrange("a p c n -> p (a c n)")
                sp.dma_start(trig_raw[p][:, 0, :, :].rearrange("p c n -> p (c n)"), t_x).then_inc(ld_trig[p], 16)
                for b in range(NB):
                    first, second = (t_c, t_x) if b == 0 else (t_x, t_c)
                    sp.dma_start(trig_raw[p][0:S, 1 + b, :, :].rearrange("p c n -> p (c n)"),
                                 first[b * S:(b + 1) * S, :]).then_inc(ld_trig[p], 16)
                    sp.dma_start(trig_raw[p][S:P, 1 + b, :, :].rearrange("p c n -> p (c n)"),
                                 second[b * S:(b + 1) * S, :]).then_inc(ld_trig[p], 16)

            def load_residual(t, p):
                need(sp, x1_ready, t - 1)
                sp.dma_start(x_res[p][:], x[bass.ds(t, 1), :, :].rearrange("a p n -> p (a n)")).then_inc(ld_res[p], 16)

            def store_x1(t, p):
                need(sp, x1_ready, t + 1)
                sp.dma_start(x1_dram[bass.ds(t, 1), :, :].rearrange("a p n -> p (a n)"), x1_out[p][:]) \
                  .then_inc(st_x1[p], 16)

            sp.wait_ge(st_trig, 16 * NCH)
            load_tile(0, 0, 0)

            def pair(i, first, last):
                for p in range(2):
                    t = 2 * i + p
                    if not (last and p == 1):
                        load_tile(t + 1, i, 1 - p)
                    load_residual(t, p)
                    if not (first and p == 0):
                        store_x1(t - 1, 1 - p)

            body = pair

            def with_w2(i, first, last):
                body(i, first, last)
                if first:
                    sp.wait_ge(w_lo, SPLITS)
                    sp.dma_start(wg_raw[:], wg).then_inc(ld_w2, 16)
                    sp.dma_start(wd_raw[:], wd).then_inc(ld_w2, 16)
                    sp.dma_start(wr_raw[:], wr).then_inc(ld_w2, 16)

            walk(sp, with_w2)
            store_x1(TILES - 1, 1)

            for p in range(2):
                sp.wait_ge(st_x1[p], 16 * PAIRS)

            def load_y(t, p):
                need(sp, y_normed, t - 1)
                sp.dma_start(y_in[p][:], x1_dram[bass.ds(t, 1), :, :].rearrange("a p n -> p (a n)")) \
                  .then_inc(ld_y[p], 16)

            def load_y_residual(t, p):
                need(sp, out_ready, t - 1)
                sp.dma_start(y_res[p][:], x1_dram[bass.ds(t, 1), :, :].rearrange("a p n -> p (a n)")) \
                  .then_inc(ld_yres[p], 16)

            def store_out(t, p):
                need(sp, out_ready, t + 1)
                sp.dma_start(out[bass.ds(t, 1), :, :].rearrange("a p n -> p (a n)"), o_out[p][:]) \
                  .then_inc(st_out[p], 16)

            load_y(0, 0)

            def pair2(i, first, last):
                for p in range(2):
                    t = 2 * i + p
                    if not (last and p == 1):
                        load_y(t + 1, 1 - p)
                    load_y_residual(t, p)
                    if not (first and p == 0):
                        store_out(t - 1, 1 - p)

            walk(sp, pair2)
            store_out(TILES - 1, 1)
            for p in range(2):
                sp.wait_ge(st_out[p], 16 * PAIRS)

        @block.gpsimd
        def _(pool):
            nc.gpsimd.memset(ident[:], 0.0).then_inc(consts_set, 1)
            nc.gpsimd.memset(minus_half[:], -0.5).then_inc(consts_set, 1)
            nc.gpsimd.memset(eps_rms[:], RMS_EPS).then_inc(consts_set, 1)
            nc.gpsimd.memset(eps_ln[:], LN_EPS).then_inc(consts_set, 1)
            nc.gpsimd.memset(half_pi[:], np.pi / 2).then_inc(consts_set, 1)
            nc.gpsimd.iota(expert_no[:], pattern=[[1, E]], base=0, channel_multiplier=0,
                           allow_small_or_imprecise_dtypes=True).then_inc(consts_set, 1)
            pool.wait_ge(consts_set, 6)
            nc.gpsimd.affine_select(out=ident[:], in_=ident[:], compare_op=ALU.not_equal, fill=1.0, base=0,
                                    pattern=[[-1, P]], channel_multiplier=1).then_inc(ident_done, 1)
            pool.wait_ge(wsin_ready, 1)

            def trig_tables(t, i, p):
                pool.wait_ge(ld_trig[p], 80 * (i + 1))
                shape = [P, 3, 2, HALF]
                nc.gpsimd.tensor_tensor(cos_w[p][:], trig_raw[p][:, :, 0:1, :].to_broadcast(shape), w_cos[:],
                                        ALU.mult).then_inc(cos_ready, 1)
                nc.gpsimd.tensor_tensor(sin_w[p][:], trig_raw[p][:, :, 1:2, :].to_broadcast(shape), w_sin[:],
                                        ALU.mult).then_inc(sin_w_ready, 1)

            def layer_rstd(t, p):
                need(pool, ln_var, t + 1)
                nc.gpsimd.tensor_tensor(ln_ve[:, p:p + 1], ln_mv[:, p, 1:2], eps_ln[:], ALU.add).then_inc(ve_done, 1)
                need(pool, ve_done, t + 1)
                nc.gpsimd.tensor_tensor(ln_rstd[:, p:p + 1], ln_ve[:, p:p + 1], minus_half[:, 0:1], ALU.pow) \
                  .then_inc(rstd_ready, 1)

            def normalize_probs(n, g):
                need(pool, inv_ready, n + 1)
                nc.gpsimd.tensor_tensor(probs[:], probs[:], row_inv[g % 2][:].unsqueeze(2).to_broadcast([P, REP, P]),
                                        ALU.mult).then_inc(p_normed, 1)

            def key_scale(n, g):
                need(pool, k_sq, n + 1)
                nc.gpsimd.tensor_tensor(k_me[:], k_ms[g % 2][:], eps_rms[:, 0:NB], ALU.add).then_inc(k_me_done, 1)
                need(pool, k_me_done, n + 1)
                nc.gpsimd.tensor_tensor(k_r[g % 2][:], k_me[:], minus_half[:, 0:NB], ALU.pow).then_inc(k_r_ready, 1)

            def query_scale(n, g):
                need(pool, q_sq, n + 1)
                nc.gpsimd.tensor_tensor(q_me[:], q_ms[g % 2][:], eps_rms[:, 0:REP], ALU.add).then_inc(q_me_done, 1)
                need(pool, q_me_done, n + 1)
                nc.gpsimd.tensor_tensor(q_r[g % 2][:], q_me[:], minus_half[:, 0:REP], ALU.pow).then_inc(q_r_ready, 1)

            def query_sum(n, g):
                need(pool, q_turned, n + 1)
                nc.gpsimd.tensor_tensor(q_rot[g % 2][:], q_rot[g % 2][:], q_sin[g % 2][:], ALU.add) \
                  .then_inc(q_summed, 1)
                need(pool, q_r_ready, n + 1)
                need(pool, q_summed, n + 1)
                nc.gpsimd.tensor_tensor(q_rot[g % 2][:], q_rot[g % 2][:],
                                        q_r[g % 2][:].unsqueeze(2).to_broadcast([P, REP, HD]), ALU.mult) \
                  .then_inc(q_ready, 1)

            def key_sum(n, g):
                need(pool, k_turned, n + 1)
                nc.gpsimd.tensor_tensor(k_rot[g % 2][:], k_rot[g % 2][:], k_sin[g % 2][:], ALU.add) \
                  .then_inc(k_ready, 1)

            layer_rstd(0, 0)
            trig_tables(0, 0, 0)
            query_scale(0, 0)
            key_scale(0, 0)
            query_sum(0, 0)
            key_sum(0, 0)
            query_scale(1, 1)

            def pair(i, first, last):
                for u in range(2 * KVH):
                    p, g = divmod(u, KVH)
                    t, n = 2 * i + p, 8 * i + u
                    end = last and p == 1
                    if not (first and u == 0):
                        normalize_probs(n - 1, g - 1)
                    if not (end and g == 3):
                        key_scale(n + 1, g + 1)
                        query_sum(n + 1, g + 1)
                    if not (end and g >= 2):
                        query_scale(n + 2, g)
                    if not (end and g == 3):
                        key_sum(n + 1, g + 1)
                    if g == 0 and not end:
                        layer_rstd(t + 1, 1 - p)
                        trig_tables(t + 1, i + p, 1 - p)

            walk(pool, pair)
            normalize_probs(4 * TILES - 1, 3)

            def layer_rstd2(t, p):
                need(pool, var2, t + 1)
                nc.gpsimd.tensor_tensor(ln_ve[:, p:p + 1], ln_mv[:, p, 1:2], eps_ln[:], ALU.add).then_inc(ve2_done, 1)
                need(pool, ve2_done, t + 1)
                nc.gpsimd.tensor_tensor(ln_rstd[:, p:p + 1], ln_ve[:, p:p + 1], minus_half[:, 0:1], ALU.pow) \
                  .then_inc(rstd2_ready, 1)

            def pair2(i, first, last):
                for p in range(2):
                    layer_rstd2(2 * i + p, p)

            walk(pool, pair2)

        @block.scalar
        def _(act):
            act.dma_start(gates_raw[:, 1:2], g_ffn.rearrange("(a n) -> a n", a=1).to_broadcast([P, 1])) \
               .then_inc(ld_const, 16)
            act.wait_ge(consts_set, 6)
            for c in range(NCH):
                act.wait_ge(angle_ready, c + 1)
                if c >= 1:
                    act.wait_ge(st_trig, 16 * c)
                nc.scalar.activation(sincos[:, :, 1, :], ang[c % 2][:], ACT.Sin)
                nc.scalar.activation(ang[c % 2][:], ang[c % 2][:], ACT.Abs).then_inc(abs_ready, 1)
                act.wait_ge(abs_ready, c + 1)
                nc.scalar.activation(sincos[:, :, 0, :], ang[c % 2][:], ACT.Sin, bias=half_pi[:], scale=-1.0) \
                  .then_inc(sin_ready, 1)
                act.wait_ge(sin_ready, c + 1)
                src, t0 = divmod(c * CH, TILES)
                act.dma_start(trig[src, t0:t0 + CH, :, :, :].rearrange("t p c n -> p t (c n)"),
                              sincos[:].rearrange("p t c n -> p t (c n)")).then_inc(st_trig, 16)
            act.wait_ge(ld_const, 16 * N_CONST + 16)
            nc.scalar.activation(gates[:], gates_raw[:], ACT.Tanh).then_inc(gates_ready, 1)
            for raw, hi, lo, loaded in split_pieces():
                act.wait_ge(loaded, 16)
                nc.scalar.activation(hi, raw, ACT.Copy).then_inc(w_hi, 1)
            act.wait_ge(gates_ready, 1)
            nc.scalar.activation(gates_raw[:, 0:1], gates[:, 0:1], ACT.Exp)

            def value_and_key(n, g):
                need(act, kv_done, n + 1)
                kv = b_kv[:].rearrange("p (b w n) -> p b w n", b=NB, w=2)
                nc.scalar.activation(v_s[g % KVH][HI][:], kv[:, :, 1, :], ACT.Copy)
                for b in range(NB):
                    last = nc.scalar.activation(junk[:, REP + b, :], kv[:, b, 0, :], ACT.Square, scale=HD ** -0.5,
                                                accum_out=k_ms[g % 2][:, b:b + 1])
                last.then_inc(k_sq, 1)

            def query_squares(n, g):
                need(act, q_done, n + 1)
                for h in range(REP):
                    last = nc.scalar.activation(junk[:, h, :], b_q[:, h * HD:(h + 1) * HD], ACT.Square, scale=HD ** -0.5,
                                                accum_out=q_ms[g % 2][:, h:h + 1])
                last.then_inc(q_sq, 1)

            def heads_hi(n, g):
                need(act, kT_done, n + 1)
                nc.scalar.activation(kT[HI][:].rearrange("p b n -> p (b n)"), b_kT[:, 0:NB * P], ACT.Copy) \
                  .then_inc(k_hi, 1)
                need(act, qT_done, n + 1)
                nc.scalar.activation(qT[HI][:].rearrange("p b h s -> p h b s"),
                                     b_qT[:].rearrange("p (h b s) -> p h b s", h=REP, b=NB), ACT.Copy).then_inc(q_hi, 1)

            def probs_hi(n, g):
                need(act, pT_done, n + 1)
                nc.scalar.activation(pT[HI][:].rearrange("p b n -> p (b n)"), b_pT[:], ACT.Copy).then_inc(pT_hi, 1)

            def exponentials(n, g):
                need(act, max_ready, n + 1)
                for j in range(REP):
                    last = nc.scalar.activation(probs[:, j, :], b_sc[:, j * P:(j + 1) * P], ACT.Exp,
                                                bias=neg_max[g % 2][:, j:j + 1], scale=SCALE,
                                                accum_out=row_sum[g % 2][:, j:j + 1])
                last.then_inc(exp_done, 1)

            def attended_hi(n, g):
                need(act, aT_done, n + 1)
                nc.scalar.activation(aT[HI][:].rearrange("p h b s -> p b h s"),
                                     b_aT[:].rearrange("p (b h s) -> p b h s", b=NB, h=REP), ACT.Copy) \
                  .then_inc(aT_hi, 1)

            def context_hi(t, i, p):
                act.wait_ge(ld_ctx[p], 16 * (i + 1))
                nc.scalar.activation(kv_in[p][HI][:, :, 0::3, :], ctx_raw[p][:].rearrange("p c (b s) -> p c b s", b=NB),
                                     ACT.Copy).then_inc(ctx_hi, 1)

            def normed_hi(t, p):
                need(act, xT_done, t + 1)
                nc.scalar.activation(kv_in[p][HI][:, :, 1:3, :],
                                     b_kT[:, DC * P:2 * DC * P].rearrange("p (c b s) -> p c b s", c=DC, b=NB), ACT.Copy) \
                  .then_inc(x_hi, 1)

            context_hi(0, 0, 0)
            normed_hi(0, 0)
            query_squares(0, 0)
            value_and_key(0, 0)
            query_squares(1, 1)

            def pair(i, first, last):
                for u in range(2 * KVH):
                    p, g = divmod(u, KVH)
                    t, n = 2 * i + p, 8 * i + u
                    end = last and p == 1
                    if not (end and g == 3):
                        value_and_key(n + 1, g + 1)
                    heads_hi(n, g)
                    if g == 0 and not end:
                        context_hi(t + 1, i + p, 1 - p)
                    if not (end and g >= 2):
                        query_squares(n + 2, g)
                    if not (first and u == 0):
                        probs_hi(n - 1, g - 1)
                    if g == 1 and not end:
                        normed_hi(t + 1, 1 - p)
                    exponentials(n, g)
                    if not (first and u == 0):
                        attended_hi(n - 1, g - 1)

            walk(act, pair)
            probs_hi(4 * TILES - 1, 3)
            attended_hi(4 * TILES - 1, 3)

            act.wait_ge(ld_w2, 48)
            for p in range(2):
                act.wait_ge(st_x1[p], 16 * PAIRS)
            for raw, hi, lo in split2_pieces():
                nc.scalar.activation(hi, raw, ACT.Copy).then_inc(w2_hi, 1)
            nc.scalar.activation(gates_raw[:, 0:1], gates[:, 0:1], ACT.Silu)

            def silu_gate(m, k):
                need(act, gu_done, m + 1)
                nc.scalar.activation(silu[k % 2][:], b_gate[k % 2][:, 0:FB], ACT.Silu).then_inc(silu_done, 1)

            def hidden_hi(m):
                need(act, hT_done, m + 1)
                nc.scalar.activation(hT[HI][:].rearrange("p c n -> p (c n)"), b_hT[:, 0:FW], ACT.Copy) \
                  .then_inc(hT_hi, 1)

            def tokens_hi(t, p):
                need(act, yT_done, t + 1)
                nc.scalar.activation(yT[p][HI][:].rearrange("p c n -> p (c n)"), b_yT[:, 0:D], ACT.Copy) \
                  .then_inc(yT_hi, 1)

            def lead_tanh(t):
                need(act, lead_ready, t + 1)
                nc.scalar.activation(lead_t[:], lead[:], ACT.Tanh, scale=0.5).then_inc(lead_done, 1)

            tokens_hi(0, 0)
            lead_tanh(0)

            def pair2(i, first, last):
                for u in range(2 * BLOCKS):
                    p, k = divmod(u, BLOCKS)
                    t, m = 2 * i + p, 2 * BLOCKS * i + u
                    end = last and p == 1
                    silu_gate(m, u)
                    if k == 2 and not end:
                        tokens_hi(t + 1, 1 - p)
                    if k == 4 and not end:
                        lead_tanh(t + 1)
                    if not (first and u == 0):
                        hidden_hi(m - 1)

            walk(act, pair2)
            hidden_hi(BLOCKS * TILES - 1)

        @block.vector
        def _(dve):
            dve.wait_ge(ld_const, 16 * N_CONST + 16)
            nc.vector.tensor_copy(pos_f[:], pos_i[:]).then_inc(pos_ready, 1)
            nc.vector.tensor_scalar(w_sin[:, :, 0, :], w_sin[:, :, 0, :], -1.0, None, ALU.mult).then_inc(wsin_ready, 1)
            dve.wait_ge(pos_ready, 1)
            steps = [0]

            def link(ins):
                steps[0] += 1
                ins.then_inc(angle_step, 1)
                dve.wait_ge(angle_step, steps[0])

            for c in range(NCH):
                a = ang[c % 2]
                if c >= 2:
                    dve.wait_ge(sin_ready, c - 1)
                shape = [P, CH, HALF]
                link(nc.vector.tensor_tensor(a[:], pos_f[:, c * CH:(c + 1) * CH].unsqueeze(2).to_broadcast(shape),
                                             invf_s[:].unsqueeze(1).to_broadcast(shape), ALU.mult))
                link(nc.vector.tensor_scalar(turn[:], a[:], 1 / (2 * np.pi), ROUND, ALU.mult, ALU.add))
                link(nc.vector.tensor_scalar(turn[:], turn[:], ROUND, None, ALU.subtract))
                for part in TWO_PI:
                    link(nc.vector.scalar_tensor_tensor(out=a[:], in0=turn[:], scalar=-part, in1=a[:],
                                                        op0=ALU.mult, op1=ALU.add))
                nc.vector.tensor_scalar(a[:], a[:], PI_BELOW, -PI_BELOW, ALU.min, ALU.max).then_inc(angle_ready, 1)
            for n, (raw, hi, lo, loaded) in enumerate(split_pieces()):
                dve.wait_ge(w_hi, n + 1)
                nc.vector.tensor_tensor(lo, raw, hi.bitcast(F32), ALU.subtract).then_inc(w_lo, 1)

            def layer_stats(t, i, p):
                dve.wait_ge(ld_x[p], 16 * (i + 1))
                nc.vector.bn_stats(ln_stats[:], x_in[p][:]).then_inc(stats_done, 1)

            def layer_var(p):
                nc.vector.bn_aggr(ln_mv[:, p, :], ln_stats[:]).then_inc(ln_var, 1)

            def normalize_x(t, p):
                need(dve, rstd_ready, t + 1)
                nc.vector.tensor_scalar(x_n[:], x_in[p][:], ln_mv[:, p, 0:1], ln_rstd[:, p:p + 1], ALU.subtract,
                                        ALU.mult).then_inc(x_normed, 1)

            def context_lo(t, p):
                need(dve, ctx_hi, t + 1)
                nc.vector.tensor_tensor(kv_in[p][LO][:, :, 0::3, :], ctx_raw[p][:].rearrange("p c (b s) -> p c b s", b=NB),
                                        kv_in[p][HI][:, :, 0::3, :].bitcast(F32), ALU.subtract).then_inc(ctx_lo, 1)

            def normed_lo(t, p):
                need(dve, x_hi, t + 1)
                nc.vector.tensor_tensor(kv_in[p][LO][:, :, 1:3, :],
                                        b_kT[:, DC * P:2 * DC * P].rearrange("p (c b s) -> p c b s", c=DC, b=NB),
                                        kv_in[p][HI][:, :, 1:3, :].bitcast(F32), ALU.subtract).then_inc(x_lo, 1)

            def value_lo(n, g):
                need(dve, k_sq, n + 1)
                kv = b_kv[:].rearrange("p (b w n) -> p b w n", b=NB, w=2)
                nc.vector.tensor_tensor(v_s[g % KVH][LO][:], kv[:, :, 1, :], v_s[g % KVH][HI][:].bitcast(F32),
                                        ALU.subtract).then_inc(v_lo, 1)

            def turn_keys(n, g, p):
                need(dve, k_r_ready, n + 1)
                kv = b_kv[:].rearrange("p (b w h n) -> p b w h n", b=NB, w=2, h=2)
                for b in range(NB):
                    r = k_r[g % 2][:, b:b + 1]
                    k3 = "p (h n) -> p h n"
                    nc.vector.scalar_tensor_tensor(out=k_rot[g % 2][:, b, :].rearrange(k3, h=2), in0=kv[:, b, 0, :, :],
                                                   scalar=r, in1=cos_w[p][:, 1 + b, :, :], op0=ALU.mult, op1=ALU.mult)
                    last = nc.vector.scalar_tensor_tensor(out=k_sin[g % 2][:, b, :].rearrange(k3, h=2),
                                                          in0=kv[:, b, 0, ::-1, :], scalar=r,
                                                          in1=sin_w[p][:, 1 + b, :, :], op0=ALU.mult, op1=ALU.mult)
                last.then_inc(k_turned, 1)

            def turn_queries(n, g, t, p):
                need(dve, q_sq, n + 1)
                if g % KVH == 0:
                    need(dve, sin_w_ready, t + 1)
                q = b_q[:].rearrange("p (h a n) -> p h a n", h=REP, a=2)
                q4 = "p h (a n) -> p h a n"
                shape = [P, REP, 2, HALF]
                nc.vector.tensor_tensor(q_rot[g % 2][:].rearrange(q4, a=2), q,
                                        cos_w[p][:, 0, :, :].unsqueeze(1).to_broadcast(shape), ALU.mult)
                nc.vector.tensor_tensor(q_sin[g % 2][:].rearrange(q4, a=2), q[:, :, ::-1, :],
                                        sin_w[p][:, 0, :, :].unsqueeze(1).to_broadcast(shape), ALU.mult) \
                  .then_inc(q_turned, 1)

            def heads_lo(n, g):
                need(dve, k_hi, n + 1)
                nc.vector.tensor_tensor(kT[LO][:].rearrange("p b n -> p (b n)"), b_kT[:, 0:NB * P],
                                        kT[HI][:].rearrange("p b n -> p (b n)").bitcast(F32), ALU.subtract) \
                  .then_inc(k_lo, 1)
                need(dve, q_hi, n + 1)
                nc.vector.tensor_tensor(qT[LO][:].rearrange("p b h s -> p h b s"),
                                        b_qT[:].rearrange("p (h b s) -> p h b s", h=REP, b=NB),
                                        qT[HI][:].bitcast(F32).rearrange("p b h s -> p h b s"), ALU.subtract) \
                  .then_inc(q_lo, 1)

            def score_max(n, g):
                need(dve, sc_done, n + 1)
                nc.vector.tensor_reduce(row_max[:], b_sc[:].rearrange("p (j n) -> p j n", j=REP), AX.X, ALU.max) \
                  .then_inc(max_found, 1)
                need(dve, max_found, n + 1)
                nc.vector.tensor_scalar(neg_max[g % 2][:], row_max[:], -SCALE, None, ALU.mult).then_inc(max_ready, 1)

            def probs_lo(n, g):
                need(dve, pT_hi, n + 1)
                nc.vector.tensor_tensor(pT[LO][:].rearrange("p b n -> p (b n)"), b_pT[:],
                                        pT[HI][:].rearrange("p b n -> p (b n)").bitcast(F32), ALU.subtract) \
                  .then_inc(pT_lo, 1)

            def sum_inverse(n, g):
                need(dve, exp_done, n + 1)
                nc.vector.reciprocal(row_inv[g % 2][:], row_sum[g % 2][:]).then_inc(inv_ready, 1)

            def attended_lo(n, g):
                need(dve, aT_hi, n + 1)
                nc.vector.tensor_tensor(aT[LO][:].rearrange("p h b s -> p b h s"),
                                        b_aT[:].rearrange("p (b h s) -> p b h s", b=NB, h=REP),
                                        aT[HI][:].bitcast(F32).rearrange("p h b s -> p b h s"), ALU.subtract) \
                  .then_inc(aT_lo, 1)

            def residual(t, i, p):
                if not isinstance(i, int) or i >= 1:
                    dve.wait_ge(st_x1[p], 16 * i)
                dve.wait_ge(ld_res[p], 16 * (i + 1))
                need(dve, o_done, KVH * (t + 1))
                nc.vector.scalar_tensor_tensor(out=x1_out[p][:], in0=b_o[:, 0:D], scalar=gates[:, 0:1],
                                               in1=x_res[p][:], op0=ALU.mult, op1=ALU.add).then_inc(x1_ready, 1)

            layer_stats(0, 0, 0)
            dve.wait_ge(stats_done, 1)
            layer_var(0)
            normalize_x(0, 0)
            context_lo(0, 0)
            normed_lo(0, 0)
            turn_queries(0, 0, 0, 0)
            value_lo(0, 0)
            turn_keys(0, 0, 0)
            turn_queries(1, 1, 0, 0)

            def pair(i, first, last):
                if first:
                    dve.wait_ge(gates_ready, 1)
                for u in range(2 * KVH):
                    p, g = divmod(u, KVH)
                    t, n = 2 * i + p, 8 * i + u
                    end = last and p == 1
                    p1 = p if g < 3 else 1 - p
                    p2 = p if g < 2 else 1 - p
                    if not (end and g == 3):
                        value_lo(n + 1, g + 1)
                    heads_lo(n, g)
                    if not (end and g == 3):
                        turn_keys(n + 1, g + 1, p1)
                    if g == 0 and not end:
                        layer_stats(t + 1, i + p, 1 - p)
                        need(dve, stats_done, t + 2)
                    if g == 1 and not end:
                        normalize_x(t + 1, 1 - p)
                    score_max(n, g)
                    if g == 0 and not end:
                        layer_var(1 - p)
                    if not (first and u == 0):
                        probs_lo(n - 1, g - 1)
                    if g == 1 and not end:
                        normed_lo(t + 1, 1 - p)
                    if not (end and g >= 2):
                        turn_queries(n + 2, g, t + (g >= 2), p2)
                    sum_inverse(n, g)
                    if g == 0 and not end:
                        context_lo(t + 1, 1 - p)
                    if not (first and u == 0):
                        attended_lo(n - 1, g - 1)
                    if g == 1 and not (first and p == 0):
                        residual(t - 1, i - 1 + p, 1 - p)

            walk(dve, pair)
            probs_lo(4 * TILES - 1, 3)
            attended_lo(4 * TILES - 1, 3)
            residual(TILES - 1, PAIRS - 1, 1)

            for p in range(2):
                dve.wait_ge(st_x1[p], 16 * PAIRS)
            for p in range(2):
                last = nc.vector.memset(hid[p][:, FB:FW], 0.0)
            last.then_inc(pad_done, 1)

            def layer_stats2(t, i, p):
                dve.wait_ge(ld_y[p], 16 * (i + 1))
                nc.vector.bn_stats(ln_stats[:], y_in[p][:]).then_inc(stats2, 1)

            def layer_var2(p):
                nc.vector.bn_aggr(ln_mv[:, p, :], ln_stats[:]).then_inc(var2, 1)

            def normalize_y(t, p):
                need(dve, rstd2_ready, t + 1)
                nc.vector.tensor_scalar(y_n[:], y_in[p][:], ln_mv[:, p, 0:1], ln_rstd[:, p:p + 1], ALU.subtract,
                                        ALU.mult).then_inc(y_normed, 1)

            def tokens_lo(t, p):
                need(dve, yT_hi, t + 1)
                nc.vector.tensor_tensor(yT[p][LO][:].rearrange("p c n -> p (c n)"), b_yT[:, 0:D],
                                        yT[p][HI][:].rearrange("p c n -> p (c n)").bitcast(F32), ALU.subtract) \
                  .then_inc(yT_lo, 1)

            def copy_logits(t):
                need(dve, lg_done, t + 1)
                nc.vector.tensor_copy(logits[:], b_yT[:, D:D + E]).then_inc(lg_copied, 1)

            def top_two(t):
                nc.vector.max(top_v[:], logits[:]).then_inc(top_found, 1)
                need(dve, top_found, t + 1)
                nc.vector.tensor_tensor(lead[:], top_v[:, 0:1], top_v[:, 1:2], ALU.subtract).then_inc(lead_ready, 1)
                nc.vector.max_index(top_i[:], top_v[:], logits[:]).then_inc(idx_found, 1)

            def combine_weights(t, p):
                need(dve, idx_found, t + 1)
                nc.vector.tensor_copy(top_f[:], top_i[:, 0:TOPK])
                need(dve, lead_done, t + 1)
                nc.vector.tensor_scalar(share[:, 0:1], lead_t[:], ROUTED_SCALE / 2, ROUTED_SCALE / 2, ALU.mult, ALU.add)
                nc.vector.tensor_scalar(share[:, 1:2], lead_t[:], -ROUTED_SCALE / 2, ROUTED_SCALE / 2, ALU.mult,
                                        ALU.add).then_inc(share_ready, 1)
                need(dve, share_ready, t + 1)
                for n in range(TOPK):
                    last = nc.vector.tensor_scalar(pick[:, n, :], expert_no[:], top_f[:, n:n + 1], share[:, n:n + 1],
                                                   ALU.is_equal, ALU.mult)
                last.then_inc(pick_ready, 1)
                need(dve, pick_ready, t + 1)
                nc.vector.tensor_tensor(combine[p][:], pick[:, 0, :], pick[:, 1, :], ALU.add).then_inc(combine_ready, 1)

            def hidden(m, u, k, p, t):
                need(dve, silu_done, m + 1)
                up = b_up[u % 2]
                if k == 0:
                    nc.vector.tensor_tensor(hid[u % 2][:, 0:FB], silu[u % 2][:], up[:, 0:FB], ALU.mult) \
                      .then_inc(hid_ready, 1)
                    return
                if k == 1:
                    need(dve, combine_ready, t + 1)
                for j in range(2):
                    cols = slice(j * F, (j + 1) * F)
                    e = 2 * (k - 1) + j
                    last = nc.vector.scalar_tensor_tensor(out=hid[u % 2][:, cols], in0=silu[u % 2][:, cols],
                                                          scalar=combine[p][:, e:e + 1], in1=up[:, cols],
                                                          op0=ALU.mult, op1=ALU.mult)
                last.then_inc(hid_ready, 1)

            def hidden_lo(m):
                need(dve, hT_hi, m + 1)
                nc.vector.tensor_tensor(hT[LO][:].rearrange("p c n -> p (c n)"), b_hT[:, 0:FW],
                                        hT[HI][:].rearrange("p c n -> p (c n)").bitcast(F32), ALU.subtract) \
                  .then_inc(hT_lo, 1)

            def output(t, i, p):
                if not isinstance(i, int) or i >= 1:
                    dve.wait_ge(st_out[p], 16 * i)
                dve.wait_ge(ld_yres[p], 16 * (i + 1))
                need(dve, y_done, BLOCKS * (t + 1))
                nc.vector.scalar_tensor_tensor(out=o_out[p][:], in0=b_y[p][:, 0:D], scalar=gates[:, 1:2],
                                               in1=y_res[p][:], op0=ALU.mult, op1=ALU.add).then_inc(out_ready, 1)

            layer_stats2(0, 0, 0)
            dve.wait_ge(stats2, 1)
            layer_var2(0)
            dve.wait_ge(w2_hi, 1)
            pieces = list(enumerate(split2_pieces()))

            def split2(some):
                for n, (raw, hi, lo) in some:
                    dve.wait_ge(w2_hi, n + 1)
                    nc.vector.tensor_tensor(lo, raw, hi.bitcast(F32), ALU.subtract).then_inc(w2_lo, 1)

            split2(pieces[:1])
            normalize_y(0, 0)
            tokens_lo(0, 0)
            copy_logits(0)
            dve.wait_ge(lg_copied, 1)
            top_two(0)
            split2(pieces[1:])
            combine_weights(0, 0)

            def pair2(i, first, last):
                for u in range(2 * BLOCKS):
                    p, k = divmod(u, BLOCKS)
                    t, m = 2 * i + p, 2 * BLOCKS * i + u
                    end = last and p == 1
                    if k == 0 and not end:
                        layer_stats2(t + 1, i + p, 1 - p)
                    hidden(m, u, k, p, t)
                    if not end:
                        if k == 0:
                            need(dve, stats2, t + 2)
                        if k == 2:
                            tokens_lo(t + 1, 1 - p)
                        if k == 3:
                            copy_logits(t + 1)
                            need(dve, lg_copied, t + 2)
                    if not (first and u == 0):
                        hidden_lo(m - 1)
                    if not end:
                        if k == 0:
                            layer_var2(1 - p)
                        if k == 1:
                            normalize_y(t + 1, 1 - p)
                        if k == 3:
                            top_two(t + 1)
                        if k == 4:
                            combine_weights(t + 1, 1 - p)
                    if k == 1 and not (first and p == 0):
                        output(t - 1, i - 1 + p, 1 - p)

            walk(dve, pair2)
            hidden_lo(BLOCKS * TILES - 1)
            output(TILES - 1, PAIRS - 1, 1)

        @block.tensor
        def _(pe):
            pe.wait_ge(ident_done, 1)

            def normed_x_T(t, p):
                need(pe, x_normed, t + 1)
                for c in range(DC):
                    last = nc.tensor.transpose(b_kT[:, (DC + c) * P:(DC + c + 1) * P], x_n[:, c * P:(c + 1) * P],
                                               ident[:])
                last.then_inc(xT_done, 1)

            def queries(n, g, t, p):
                need(pe, q_turned, n)
                if g % KVH == 0:
                    need(pe, x_lo, t + 1)
                gg = g % KVH
                for c in range(DC):
                    for a, b in PASSES:
                        last = nc.tensor.matmul(b_q[:], kv_in[p][a][:, c, 1:3, :],
                                                wq_s[b][:, c, gg * REP * HD:(gg + 1) * REP * HD],
                                                start=(c == 0 and (a, b) == PASSES[0]),
                                                stop=(c == DC - 1 and (a, b) == PASSES[-1]))
                last.then_inc(q_done, 1)

            def keys_values(n, g, t, p):
                need(pe, k_turned, n)
                if g % KVH == 0:
                    need(pe, ctx_lo, t + 1)
                for s in range(NB):
                    for c in range(DC):
                        for a, b in PASSES:
                            last = nc.tensor.matmul(b_kv[:, s * 2 * HD:(s + 1) * 2 * HD],
                                                    kv_in[p][a][:, c, 2 * s:2 * s + 2, :],
                                                    wkv_s[b][:, c, g % KVH, :],
                                                    start=(c == 0 and (a, b) == PASSES[0]),
                                                    stop=(c == DC - 1 and (a, b) == PASSES[-1]))
                last.then_inc(kv_done, 1)

            def heads_T(n, g):
                need(pe, k_ready, n + 1)
                for s in range(NB):
                    last = nc.tensor.transpose(b_kT[:, s * P:(s + 1) * P], k_rot[g % 2][:, s, :], ident[:])
                last.then_inc(kT_done, 1)
                need(pe, q_ready, n + 1)
                for h in range(REP):
                    last = nc.tensor.transpose(b_qT[:, h * P:(h + 1) * P], q_rot[g % 2][:, h, :], ident[:])
                last.then_inc(qT_done, 1)

            def scores(n, g):
                need(pe, q_lo, n + 1)
                for s in range(NB):
                    for j in range(REP // 2):
                        o = (s * (REP // 2) + j) * P
                        for a, b in PASSES:
                            last = nc.tensor.matmul(b_sc[:, o:o + P], qT[a][:, s, 2 * j:2 * j + 2, :],
                                                    kT[b][:, s, :], start=((a, b) == PASSES[0]),
                                                    stop=((a, b) == PASSES[-1]))
                last.then_inc(sc_done, 1)

            def probs_T(n, g):
                need(pe, p_normed, n + 1)
                for j in range(REP):
                    last = nc.tensor.transpose(b_pT[:, j * P:(j + 1) * P], probs[:, j, :], ident[:])
                last.then_inc(pT_done, 1)

            def attend(n, g):
                need(pe, pT_lo, n + 1)
                for s in range(NB):
                    for a, b in PASSES:
                        last = nc.tensor.matmul(b_aT[:, s * REP * S:(s + 1) * REP * S], v_s[g % KVH][a][:, s, :],
                                                pT[b][:, s, :], start=((a, b) == PASSES[0]),
                                                stop=((a, b) == PASSES[-1]))
                last.then_inc(aT_done, 1)

            def project(n, g, t):
                gg = g % KVH
                need(pe, aT_lo, n + 1)
                if gg == 0:
                    need(pe, x1_ready, t)
                for h in range(REP):
                    for a, b in PASSES:
                        last = nc.tensor.matmul(b_o[:, 0:D], aT[a][:, h, :, :], wo_s[b][:, gg * REP + h, :],
                                                start=(gg == 0 and h == 0 and (a, b) == PASSES[0]),
                                                stop=(gg == KVH - 1 and h == REP - 1 and (a, b) == PASSES[-1]))
                last.then_inc(o_done, 1)

            normed_x_T(0, 0)
            pe.wait_ge(w_lo, SPLITS)
            queries(0, 0, 0, 0)
            keys_values(0, 0, 0, 0)
            queries(1, 1, 0, 0)
            keys_values(1, 1, 0, 0)

            def pair(i, first, last):
                for u in range(2 * KVH):
                    p, g = divmod(u, KVH)
                    t, n = 2 * i + p, 8 * i + u
                    end = last and p == 1
                    t2, p2 = t + (g >= 2), (p if g < 2 else 1 - p)
                    if g == 2 and not end:
                        need(pe, x_lo, t + 2)
                    heads_T(n, g)
                    if not (first and u < 2):
                        project(n - 2, g - 2, t if g >= 2 else t - 1)
                    if not (first and u < 1):
                        probs_T(n - 1, g - 1)
                    if not (end and g >= 2):
                        queries(n + 2, g + 2, t2, p2)
                    scores(n, g)
                    if g == 1 and not end:
                        normed_x_T(t + 1, 1 - p)
                    if not (first and u < 1):
                        attend(n - 1, g - 1)
                    if not (end and g >= 2):
                        keys_values(n + 2, g + 2, t2, p2)

            walk(pe, pair)
            project(4 * TILES - 2, 2, TILES - 1)
            probs_T(4 * TILES - 1, 3)
            attend(4 * TILES - 1, 3)
            project(4 * TILES - 1, 3, TILES - 1)

            def tokens_T(t, p):
                need(pe, y_normed, t + 1)
                need(pe, lg_copied, t)
                for c in range(DC):
                    last = nc.tensor.transpose(b_yT[:, c * P:(c + 1) * P], y_n[:, c * P:(c + 1) * P], ident[:])
                last.then_inc(yT_done, 1)

            def router(t, p):
                need(pe, yT_lo, t + 1)
                for c in range(DC):
                    for a, b in PASSES:
                        last = nc.tensor.matmul(b_yT[:, D:D + E], yT[p][a][:, c, :], wr_s[b][:, c, :],
                                                start=(c == 0 and (a, b) == PASSES[0]),
                                                stop=(c == DC - 1 and (a, b) == PASSES[-1]))
                last.then_inc(lg_done, 1)

            def gate_up(m, u, k, p):
                need(pe, hid_ready, m - 1)
                for j, o in enumerate((b_gate[u % 2], b_up[u % 2])):
                    for c in range(DC):
                        for a, b in PASSES:
                            last = nc.tensor.matmul(o[:, 0:FB], yT[p][a][:, c, :],
                                                    wg_s[b][:, c, k, j * FB:(j + 1) * FB],
                                                    start=(c == 0 and (a, b) == PASSES[0]),
                                                    stop=(c == DC - 1 and (a, b) == PASSES[-1]))
                last.then_inc(gu_done, 1)

            def hidden_T(m, u):
                need(pe, hid_ready, m + 1)
                need(pe, hT_lo, m)
                for c in range(FC):
                    last = nc.tensor.transpose(b_hT[:, c * P:(c + 1) * P], hid[u % 2][:, c * P:(c + 1) * P], ident[:])
                last.then_inc(hT_done, 1)

            def down(m, k, t, p):
                need(pe, hT_lo, m + 1)
                if k == 0:
                    need(pe, out_ready, t - 1)
                for c in range(FC):
                    rows = min(P, FB - c * P)
                    for a, b in PASSES:
                        last = nc.tensor.matmul(b_y[p][:, 0:D], hT[a][0:rows, c, :], wd_s[b][0:rows, k, c, :],
                                                start=(k == 0 and c == 0 and (a, b) == PASSES[0]),
                                                stop=(k == BLOCKS - 1 and c == FC - 1 and (a, b) == PASSES[-1]))
                last.then_inc(y_done, 1)

            pe.wait_ge(x1_ready, TILES)
            pe.wait_ge(pad_done, 1)
            tokens_T(0, 0)
            pe.wait_ge(w2_lo, 1)
            router(0, 0)

            def pair2(i, first, last):
                for u in range(2 * BLOCKS):
                    p, k = divmod(u, BLOCKS)
                    t, m = 2 * i + p, 2 * BLOCKS * i + u
                    end = last and p == 1
                    if first and p == 0:
                        pe.wait_ge(w2_lo, W2_READY[k])
                    gate_up(m, u, k, p)
                    if k == 2 and not end:
                        tokens_T(t + 1, 1 - p)
                    if k == 3 and not end:
                        router(t + 1, 1 - p)
                    if not (first and u < 2):
                        k2 = (u - 2) % BLOCKS
                        down(m - 2, k2, t if k >= 2 else t - 1, p if k >= 2 else 1 - p)
                    if not (first and u < 1):
                        hidden_T(m - 1, u - 1)

            walk(pe, pair2)
            M = BLOCKS * TILES
            down(M - 2, BLOCKS - 2, TILES - 1, 1)
            hidden_T(M - 1, 2 * BLOCKS - 1)
            down(M - 1, BLOCKS - 1, TILES - 1, 1)


def kernel(x, ctx_2048, pos_BxS2, itok_BxS_4096_4607, g_xattn, g_ffn, L0_xattn_Wq, L0_xattn_Wk, L0_xattn_Wv,
           L0_xattn_Wo, L0_xattn_q_norm_w, L0_xattn_k_norm_w, L0_ffn_w_router, L0_ffn_w_gate, L0_ffn_w_up,
           L0_ffn_w_down, L0_ffn_ws_gate, L0_ffn_ws_up, L0_ffn_ws_down):
    import numpy as np
    import concourse.bacc as bacc
    from concourse.bass_utils import run_bass_kernel_spmd as run

    def arr(a):
        return np.asarray(a)

    def chunked(w):
        return w.reshape(DC, P, -1).transpose(1, 0, 2)

    wk, wv = arr(L0_xattn_Wk).T, arr(L0_xattn_Wv).T
    wkv = np.stack([wk.reshape(D, KVH, HD), wv.reshape(D, KVH, HD)], 2)
    gate, up, down = arr(L0_ffn_w_gate), arr(L0_ffn_w_up), arr(L0_ffn_w_down)
    gu = [np.concatenate([arr(L0_ffn_ws_gate), arr(L0_ffn_ws_up)], 1)]
    gu += [np.concatenate([gate[e], gate[e + 1], up[e], up[e + 1]], 1) for e in range(0, E, 2)]
    dn = [arr(L0_ffn_ws_down)] + [np.concatenate([down[e], down[e + 1]], 0) for e in range(0, E, 2)]
    dn = [np.concatenate([w, np.zeros((FW - FB, D), w.dtype)], 0).reshape(FC, P, D) for w in dn]
    inv_freq = (np.float32(1.0) / np.float32(10000.0) ** (np.arange(0, HD, 2, dtype=np.float32) / np.float32(HD)))
    ins = {
        "x": arr(x).reshape(TILES, P, D),
        "ctxT": arr(ctx_2048).reshape(TILES, P, DC, P).transpose(0, 3, 2, 1),
        "posx": arr(itok_BxS_4096_4607).reshape(TILES, P).T,
        "posc": arr(pos_BxS2).reshape(TILES, P).T,
        "invf": np.broadcast_to(inv_freq.astype(np.float32), (P, HALF)),
        "g_xattn": arr(g_xattn), "g_ffn": arr(g_ffn),
        "q_w": arr(L0_xattn_q_norm_w), "k_w": arr(L0_xattn_k_norm_w),
        "wq": chunked(arr(L0_xattn_Wq).T),
        "wkv": chunked(wkv.reshape(D, KVH * 2 * HD)).reshape(P, DC, KVH, 2 * HD),
        "wo": arr(L0_xattn_Wo).T.reshape(H, P, D).transpose(1, 0, 2),
        "wr": chunked(arr(L0_ffn_w_router)),
        "wg": chunked(np.concatenate(gu, 1)).reshape(P, DC, BLOCKS, 2 * FB),
        "wd": np.stack(dn).transpose(2, 0, 1, 3),
    }
    nc = bacc.Bacc("TRN2", target_bir_lowering=False, num_devices=1)
    arrays, aps = {}, []
    for name, a in ins.items():
        arrays[f"in_{name}"] = np.ascontiguousarray(a)
        aps.append(nc.dram_tensor(f"in_{name}", a.shape, mybir.dt.from_np(a.dtype), kind="ExternalInput").ap())
    out = nc.dram_tensor("out", (TILES, P, D), F32, kind="ExternalOutput").ap()
    flamingo(nc, *aps, out)
    got = run(nc, [arrays], core_ids=[0]).results[0]["out"]
    return got.reshape(B, S, D)
```

```python
import concourse.bass as bass
from concourse import mybir
from contextlib import ExitStack
import numpy as np

F32 = mybir.dt.float32
F32R = mybir.dt.float32r
I32 = mybir.dt.int32
U32 = mybir.dt.uint32
BF16 = mybir.dt.bfloat16
ALU = mybir.AluOpType
ACT = mybir.ActivationFunctionType
AX = mybir.AxisListType

P = 128
B, S, D = 64, 64, 256
H, KVH, HD = 16, 4, 128
REP = H // KVH
NB = P // S
TILES = B * S // P
PAIRS = TILES // 2
DC = D // P
HALF = HD // 2
E, TOPK, F, FS = 8, 2, 176, 352
BLOCKS = 1 + E // 2
FB = FS
FC = -(-FB // P)
FW = FC * P
ROUTED_SCALE = 2.5
SCALE = float(np.float32(1.0) / np.sqrt(np.float32(HD)))
RMS_EPS, LN_EPS = 1e-6, 1e-5
TWO_PI = (6.28125, 0.0019350051879882812, 2 * np.pi - 6.28125 - 0.0019350051879882812)
ROUND = 1.5 * 2.0 ** 23
PI_BELOW = 3.1415925
PASSES = ((0, 0), (0, 1), (1, 0))
HI, LO = 0, 1


def need(eng, sem, count):
    if not isinstance(count, int) or count > 0:
        eng.wait_ge(sem, count)


def walk(eng, body):
    body(0, True, False)
    with eng.Fori(1, PAIRS - 1) as i:
        body(i, False, False)
    body(PAIRS - 1, False, True)


def flamingo(nc, x, ctxT, posx, posc, invf, g_xattn, g_ffn, q_w, k_w, wq, wkv, wo, wr, wg, wd, out):
    ctx = ExitStack()
    with ctx:
        cursor = [-(-nc.sbuf_base // 64) * 64]

        def sb(name, shape, dt, at=None):
            size = int(np.prod(shape[1:])) * mybir.dt.size(dt)
            where = cursor if at is None else at
            t = nc.alloc_sbuf_tensor_at(name, shape, dt, offset=where[0])
            where[0] += -(-size // 64) * 64
            return t

        def parts(name, shape, at=None):
            return [sb(f"{name}_{p}", shape, F32R, at) for p in ("hi", "lo")]

        ident = sb("ident", [P, P], F32)
        gates = sb("gates", [P, 2], F32)
        gates_raw = sb("gates_raw", [P, 2], F32)
        minus_half = sb("minus_half", [P, 8], F32)
        eps_rms = sb("eps_rms", [P, 8], F32)
        eps_ln = sb("eps_ln", [P, 1], F32)
        half_pi = sb("half_pi", [P, 1], F32)
        expert_no = sb("expert_no", [P, E], F32)
        ln_stats = sb("ln_stats", [P, 6], F32)
        ln_mv = sb("ln_mv", [P, 2, 2], F32)
        ln_ve = sb("ln_ve", [P, 2], F32)
        ln_rstd = sb("ln_rstd", [P, 2], F32)
        wr_raw = sb("wr_raw", [P, DC, E], F32)
        wr_s = parts("wr", [P, DC, E])
        stage_at = list(cursor)
        wg_at = list(cursor)
        wg_raw = sb("wg_raw", [P, DC, BLOCKS, 2 * FB], F32)
        wd_at = list(cursor)
        wd_raw = sb("wd_raw", [P, BLOCKS, FC, D], F32)
        wg_lo = sb("wg_lo", [P, DC, BLOCKS, 2 * FB], F32R, wg_at)
        wd_lo = sb("wd_lo", [P, BLOCKS, FC, D], F32R, wd_at)
        wq_raw = sb("wq_raw", [P, DC, H * HD], F32, stage_at)
        wkv_raw = sb("wkv_raw", [P, DC, KVH, 2 * HD], F32, stage_at)
        wo_raw = sb("wo_raw", [P, H, D], F32, stage_at)
        assert stage_at[0] <= cursor[0]
        stage_end = cursor[0]
        phase_at = list(cursor)
        wq_s = parts("wq", [P, DC, H * HD])
        wkv_s = parts("wkv", [P, DC, KVH, 2 * HD])
        phase_end = cursor[0]
        wo_s = parts("wo", [P, H, D])
        w_cos = sb("w_cos", [P, 3, 2, HALF], F32)
        w_sin = sb("w_sin", [P, 3, 2, HALF], F32)
        trig_raw = [sb(f"trig_raw{p}", [P, 3, 2, HALF], F32) for p in range(2)]
        cos_w = [sb(f"cos_w{p}", [P, 3, 2, HALF], F32) for p in range(2)]
        sin_w = [sb(f"sin_w{p}", [P, 3, 2, HALF], F32) for p in range(2)]
        x_in = [sb(f"x_in{p}", [P, D], F32) for p in range(2)]
        x_res = [sb(f"x_res{p}", [P, D], F32) for p in range(2)]
        x1_out = [sb(f"x1_out{p}", [P, D], F32) for p in range(2)]
        ctx_raw = [sb(f"ctx_raw{p}", [P, DC, P], F32) for p in range(2)]
        x_n = sb("x_n", [P, D], F32)
        kv_in = [parts(f"kv_in{p}", [P, DC, 4, S]) for p in range(2)]
        junk = sb("junk", [P, REP + NB, HD], BF16)
        qk_ms = [sb(f"qk_ms{p}", [P, REP + NB], F32) for p in range(2)]
        qk_me = sb("qk_me", [P, REP + NB], F32)
        qk_r = [sb(f"qk_r{p}", [P, REP + NB], F32) for p in range(2)]
        q_rot = [sb(f"q_rot{p}", [P, REP, HD], F32) for p in range(2)]
        q_sin = [sb(f"q_sin{p}", [P, REP, HD], F32) for p in range(2)]
        k_rot = [sb(f"k_rot{p}", [P, NB, HD], F32) for p in range(2)]
        k_sin = [sb(f"k_sin{p}", [P, NB, HD], F32) for p in range(2)]
        v_s = [sb(f"v{g}", [P, NB, HD], F32) for g in range(KVH)]
        early_at = list(cursor)
        qT = sb("qT", [P, NB, REP, S], F32)
        kT = sb("kT", [P, NB, P], F32)
        probs = sb("probs", [P, REP, P], F32)
        pT = sb("pT", [P, NB, REP * S], F32)
        aT = parts("aT", [P, REP, NB, S])
        early_end = cursor[0]
        row_max = sb("row_max", [P, REP], F32)
        neg_max = [sb(f"neg_max{p}", [P, REP], F32) for p in range(2)]
        row_sum = [sb(f"row_sum{p}", [P, REP], F32) for p in range(2)]
        row_inv = [sb(f"row_inv{p}", [P, REP], F32) for p in range(2)]
        late_at = list(cursor)
        CH = 8
        NCH = 2 * TILES // CH
        X0 = NCH // 2
        sincos = [sb(f"sincos{c}", [P, CH, 2, HALF], F32, early_at if c in (0, X0) else None) for c in range(NCH)]
        turn_v = sb("turn_v", [P, CH, HALF], F32, early_at)
        turn_p = sb("turn_p", [P, CH, HALF], F32, stage_at)
        invf_s = sb("invf_s", [P, HALF], F32, early_at)
        pos_i = sb("pos_i", [P, 2 * TILES], I32, early_at)
        pos_f = sb("pos_f", [P, 2 * TILES], F32, stage_at)
        assert early_at[0] <= early_end and cursor[0] <= nc.sbuf_usable_end, (early_at, early_end, cursor)
        wg_s = [sb("wg_hi", [P, DC, BLOCKS, 2 * FB], F32R, phase_at), wg_lo]
        wd_s = [sb("wd_hi", [P, BLOCKS, FC, D], F32R, phase_at), wd_lo]
        assert phase_at[0] <= phase_end and stage_at[0] <= stage_end
        phase_at = late_at
        y_in = [sb(f"y_in{p}", [P, D], F32, phase_at) for p in range(2)]
        y_res = [sb(f"y_res{p}", [P, D], F32, phase_at) for p in range(2)]
        y_n = sb("y_n", [P, D], F32, phase_at)
        yT = [parts(f"yT{p}", [P, DC, P], phase_at) for p in range(2)]
        logits = sb("logits", [P, E], F32, phase_at)
        top_v = sb("top_v", [P, 8], F32, phase_at)
        top_i = sb("top_i", [P, 8], U32, phase_at)
        top_f = sb("top_f", [P, TOPK], F32, phase_at)
        lead = sb("lead", [P, 1], F32, phase_at)
        lead_t = sb("lead_t", [P, 1], F32, phase_at)
        share = sb("share", [P, TOPK], F32, phase_at)
        pick = sb("pick", [P, TOPK, E], F32, phase_at)
        combine = [sb(f"combine{p}", [P, E], F32, phase_at) for p in range(2)]
        silu = [sb(f"silu{p}", [P, FB], F32, phase_at) for p in range(2)]
        hid = [sb(f"hid{p}", [P, FW], F32, phase_at) for p in range(2)]
        hT = parts("hT", [P, FC, P], phase_at)
        o_out = [sb(f"o_out{p}", [P, D], F32, phase_at) for p in range(2)]
        assert late_at[0] <= nc.sbuf_usable_end

        trig = nc.dram_tensor("trig_scratch", (2, TILES, P, 2, HALF), F32, kind="Internal").ap()
        x1_dram = nc.dram_tensor("x1_scratch", (TILES, P, D), F32, kind="Internal").ap()

        def bank(name):
            return ctx.enter_context(nc.psum_tensor(name, [P, 512], F32))

        b_q, b_kv, b_qT, b_kT, b_sc, b_pT, b_aT, b_o = [
            bank(n) for n in ("b_q", "b_kv", "b_qT", "b_kT", "b_sc", "b_pT", "b_aT", "b_o")]
        b_gate, b_up, b_hT, b_yT, b_y = [b_q, b_kv], [b_qT, b_kT], b_sc, b_pT, [b_aT, b_o]

        def sem(name):
            return ctx.enter_context(nc.semaphore(name))

        ld_pos, ld_const, ld_wq, ld_wkv, ld_wo, ld_w2 = map(sem, (
            "ld_pos", "ld_const", "ld_wq", "ld_wkv", "ld_wo", "ld_w2"))
        ld_x, ld_ctx, ld_trig, ld_res, ld_y, ld_yres = [[sem(f"{n}{p}") for p in range(2)] for n in
                                               ("ld_x", "ld_ctx", "ld_trig", "ld_res", "ld_y", "ld_yres")]
        st_trig_first, st_trig = map(sem, ("st_trig_first", "st_trig"))
        st_x1, st_out = [[sem(f"{n}{p}") for p in range(2)] for n in ("st_x1", "st_out")]
        consts_set, ident_done, pos_ready, wsin_ready, sin_ready, gates_ready = map(sem, (
            "consts_set", "ident_done", "pos_ready", "wsin_ready", "sin_ready", "gates_ready"))
        step_v, angle_v, step_p, angle_p = map(sem, ("step_v", "angle_v", "step_p", "angle_p"))
        abs_ready = sem("abs_ready")
        w_hi, w_lo = sem("w_hi"), sem("w_lo")
        q_done, kv_done, qT_done, kT_done, sc_done, pT_done, aT_done, o_done, xT_done = map(sem, (
            "q_done", "kv_done", "qT_done", "kT_done", "sc_done", "pT_done", "aT_done", "o_done", "xT_done"))
        q_sq, k_sq, q_out, exp_done, pT_out, aT_hi, x_hi, ctx_hi = map(sem, (
            "q_sq", "k_sq", "q_out", "exp_done", "pT_out", "aT_hi", "x_hi", "ctx_hi"))
        (v_out, k_out, k_turned, q_turned, max_found, max_ready, inv_ready, aT_lo, stats_done, ln_var,
         x_normed, x_lo, ctx_lo, x1_ready) = map(sem, (
             "v_out", "k_out", "k_turned", "q_turned", "max_found", "max_ready", "inv_ready", "aT_lo",
             "stats_done", "ln_var", "x_normed", "x_lo", "ctx_lo", "x1_ready"))
        p_normed, p_normed2, me_done, r_ready, q_summed, q_ready, k_ready, ve_done, rstd_ready, \
            cos_ready, sin_w_ready = map(sem, (
                "p_normed", "p_normed2", "me_done", "r_ready", "q_summed", "q_ready", "k_ready",
                "ve_done", "rstd_ready", "cos_ready", "sin_w_ready"))
        w2_hi, wg_lo_done, wd_lo_done, pad_done = map(sem, ("w2_hi", "wg_lo_done", "wd_lo_done", "pad_done"))
        gu_done, hT_done, y_done, yT_done, lg_done = map(sem, ("gu_done", "hT_done", "y_done", "yT_done", "lg_done"))
        silu_done, hT_hi, yT_hi, lead_done = map(sem, ("silu_done", "hT_hi", "yT_hi", "lead_done"))
        (stats2, var2, y_normed, yT_lo, lg_copied, top_found, idx_found, lead_ready, share_ready, pick_ready,
         combine_ready, hid_ready, hT_lo, out_ready) = map(sem, (
             "stats2", "var2", "y_normed", "yT_lo", "lg_copied", "top_found", "idx_found", "lead_ready",
             "share_ready", "pick_ready", "combine_ready", "hid_ready", "hT_lo", "out_ready"))
        ve2_done, rstd2_ready = sem("ve2_done"), sem("rstd2_ready")

        SPLITS = 4 + 2 + 4
        N_CONST = 11

        block = ctx.enter_context(nc.Block())

        def split_pieces():
            for c in range(4):
                yield tuple(w[:, :, 512 * c:512 * c + 512] for w in (wq_raw, *wq_s)) + (ld_wq,)
                if c == 0:
                    for d in range(DC):
                        yield tuple(w[:, d, :, :] for w in (wkv_raw, *wkv_s)) + (ld_wkv,)
            for c in range(4):
                yield tuple(w[:, 4 * c:4 * c + 4, :] for w in (wo_raw, *wo_s)) + (ld_wo,)

        QUERY_SPLITS = (1, 4, 5, 6)
        KV_SPLITS = 3

        def wg_piece(k, c):
            return tuple(w[:, c, k, :] for w in (wg_raw, *wg_s))

        def wd_piece(k):
            return tuple(w[:, k, :, :] for w in (wd_raw, *wd_s))

        W2_ORDER = ["r", "g00", "g01", "g10", "g11", "g20", "g21", "d0", "d1", "g30", "g31", "d2", "g40", "g41",
                    "d3", "d4"]

        def w2_piece(name):
            if name == "r":
                return wr_raw[:], wr_s[HI][:], wr_s[LO][:]
            return wg_piece(int(name[1]), int(name[2])) if name[0] == "g" else wd_piece(int(name[1]))

        def angle_steps(nce, c, a, turn, spare, link, done):
            shape = [P, CH, HALF]
            link(nce.tensor_tensor(a, pos_f[:, c * CH:(c + 1) * CH].unsqueeze(2).to_broadcast(shape),
                                   invf_s[:].unsqueeze(1).to_broadcast(shape), ALU.mult))
            link(nce.tensor_scalar(turn, a, 1 / (2 * np.pi), ROUND, ALU.mult, ALU.add))
            link(nce.tensor_scalar(turn, turn, ROUND, 1.0, ALU.subtract, ALU.mult))
            for part in TWO_PI:
                if spare is None:
                    link(nce.scalar_tensor_tensor(out=a, in0=turn, scalar=-part, in1=a, op0=ALU.mult, op1=ALU.add))
                else:
                    link(nce.tensor_scalar(spare, turn, -part, 0.0, ALU.mult, ALU.add))
                    link(nce.tensor_tensor(a, a, spare, ALU.add))
            nce.tensor_scalar(a, a, PI_BELOW, -PI_BELOW, ALU.min, ALU.max).then_inc(done, 1)

        CHUNKS_V = (0, X0, 1, X0 + 1, X0 + 3)
        CHUNKS_P = (2, X0 + 2, 3)

        @block.sync
        def _(sp):
            sp.dma_start(pos_i[:, 0:TILES], posc).then_inc(ld_pos, 16)
            sp.dma_start(pos_i[:, TILES:2 * TILES], posx).then_inc(ld_pos, 16)
            sp.dma_start(invf_s[:], invf).then_inc(ld_pos, 16)

            def load_inputs(t, p):
                need(sp, x_normed, t - 1)
                sp.dma_start(x_in[p][:], x[bass.ds(t, 1), :, :].rearrange("a p n -> p (a n)")).then_inc(ld_x[p], 16)
                need(sp, ctx_lo, t - 1)
                sp.dma_start(ctx_raw[p][:], ctxT[bass.ds(t, 1), :, :, :].rearrange("a p c n -> p (a c) n")) \
                  .then_inc(ld_ctx[p], 16)

            def load_trig(t, p):
                need(sp, sin_w_ready, t - 1)
                t_x = trig[1, bass.ds(t, 1), :, :, :].rearrange("a p c n -> p (a c n)")
                t_c = trig[0, bass.ds(t, 1), :, :, :].rearrange("a p c n -> p (a c n)")
                sp.dma_start(trig_raw[p][:, 0, :, :].rearrange("p c n -> p (c n)"), t_x).then_inc(ld_trig[p], 16)
                for b in range(NB):
                    first, second = (t_c, t_x) if b == 0 else (t_x, t_c)
                    sp.dma_start(trig_raw[p][0:S, 1 + b, :, :].rearrange("p c n -> p (c n)"),
                                 first[b * S:(b + 1) * S, :]).then_inc(ld_trig[p], 16)
                    sp.dma_start(trig_raw[p][S:P, 1 + b, :, :].rearrange("p c n -> p (c n)"),
                                 second[b * S:(b + 1) * S, :]).then_inc(ld_trig[p], 16)

            load_inputs(0, 0)
            sp.dma_start(wq_raw[:], wq).then_inc(ld_wq, 16)
            sp.dma_start(wkv_raw[:], wkv).then_inc(ld_wkv, 16)
            for n, w in ((0, q_w), (1, k_w), (2, k_w)):
                row = w.rearrange("(a n) -> a n", a=1)
                sp.dma_start(w_cos[:, n, :, :].rearrange("p a b -> p (a b)"),
                             row.to_broadcast([P, HD])).then_inc(ld_const, 16)
                sp.dma_start(w_sin[:, n, 0, :], row[:, HALF:HD].to_broadcast([P, HALF])).then_inc(ld_const, 16)
                sp.dma_start(w_sin[:, n, 1, :], row[:, 0:HALF].to_broadcast([P, HALF])).then_inc(ld_const, 16)
            for n, gate in enumerate((g_xattn, g_ffn)):
                sp.dma_start(gates_raw[:, n:n + 1], gate.rearrange("(a n) -> a n", a=1).to_broadcast([P, 1])) \
                  .then_inc(ld_const, 16)
            sp.dma_start(wo_raw[:], wo).then_inc(ld_wo, 16)

            def load_residual(t, p):
                need(sp, x1_ready, t - 1)
                sp.dma_start(x_res[p][:], x[bass.ds(t, 1), :, :].rearrange("a p n -> p (a n)")).then_inc(ld_res[p], 16)

            def store_x1(t, p):
                need(sp, x1_ready, t + 1)
                sp.dma_start(x1_dram[bass.ds(t, 1), :, :].rearrange("a p n -> p (a n)"), x1_out[p][:]) \
                  .then_inc(st_x1[p], 16)

            def load_y(t, p):
                need(sp, y_normed, t - 1)
                sp.dma_start(y_in[p][:], x1_dram[bass.ds(t, 1), :, :].rearrange("a p n -> p (a n)")) \
                  .then_inc(ld_y[p], 16)

            sp.wait_ge(st_trig_first, 16 * 2)
            load_trig(0, 0)

            def pair(i, first, last):
                for p in range(2):
                    t = 2 * i + p
                    if not (last and p == 1):
                        load_inputs(t + 1, 1 - p)
                        load_trig(t + 1, 1 - p)
                    load_residual(t, p)
                    if last and p == 1:
                        sp.wait_ge(st_x1[0], 16)
                        load_y(0, 0)
                    if not (first and p == 0):
                        store_x1(t - 1, 1 - p)
                if first:
                    sp.wait_ge(st_trig, 16 * (NCH - 2))
                    sp.wait_ge(w_lo, SPLITS)
                    sp.dma_start(wg_raw[:], wg).then_inc(ld_w2, 16)
                    sp.dma_start(wd_raw[:], wd).then_inc(ld_w2, 16)
                    sp.dma_start(wr_raw[:], wr).then_inc(ld_w2, 16)

            walk(sp, pair)

            def load_y_residual(t, p):
                need(sp, out_ready, t - 1)
                sp.dma_start(y_res[p][:], x1_dram[bass.ds(t, 1), :, :].rearrange("a p n -> p (a n)")) \
                  .then_inc(ld_yres[p], 16)

            def store_out(t, p):
                need(sp, out_ready, t + 1)
                sp.dma_start(out[bass.ds(t, 1), :, :].rearrange("a p n -> p (a n)"), o_out[p][:]) \
                  .then_inc(st_out[p], 16)

            def pair2(i, first, last):
                for p in range(2):
                    t = 2 * i + p
                    if first and p == 0:
                        sp.wait_ge(st_x1[1], 16 * (PAIRS - 1))
                    if not (last and p == 1):
                        load_y(t + 1, 1 - p)
                    load_y_residual(t, p)
                    if not (first and p == 0):
                        store_out(t - 1, 1 - p)
                    if first and p == 0:
                        store_x1(TILES - 1, 1)
                        for b in range(2):
                            sp.wait_ge(st_x1[b], 16 * PAIRS)

            walk(sp, pair2)
            store_out(TILES - 1, 1)
            for p in range(2):
                sp.wait_ge(st_out[p], 16 * PAIRS)

        @block.gpsimd
        def _(pool):
            nc.gpsimd.memset(ident[:], 0.0).then_inc(consts_set, 1)
            nc.gpsimd.memset(minus_half[:], -0.5).then_inc(consts_set, 1)
            nc.gpsimd.memset(eps_rms[:], RMS_EPS).then_inc(consts_set, 1)
            nc.gpsimd.memset(eps_ln[:], LN_EPS).then_inc(consts_set, 1)
            nc.gpsimd.memset(half_pi[:], np.pi / 2).then_inc(consts_set, 1)
            nc.gpsimd.iota(expert_no[:], pattern=[[1, E]], base=0, channel_multiplier=0,
                           allow_small_or_imprecise_dtypes=True).then_inc(consts_set, 1)
            pool.wait_ge(consts_set, 6)
            nc.gpsimd.affine_select(out=ident[:], in_=ident[:], compare_op=ALU.not_equal, fill=1.0, base=0,
                                    pattern=[[-1, P]], channel_multiplier=1).then_inc(ident_done, 1)
            steps = [0]

            def link(ins):
                steps[0] += 1
                ins.then_inc(step_p, 1)
                pool.wait_ge(step_p, steps[0])

            def angles(c):
                angle_steps(nc.gpsimd, c, sincos[c][:, :, 1, :], turn_p[:], sincos[c][:, :, 0, :], link, angle_p)

            def cos_table(i, p):
                pool.wait_ge(ld_trig[p], 80 * (i + 1))
                nc.gpsimd.tensor_tensor(cos_w[p][:], trig_raw[p][:, :, 0:1, :].to_broadcast([P, 3, 2, HALF]), w_cos[:],
                                        ALU.mult).then_inc(cos_ready, 1)

            def sin_table(p):
                nc.gpsimd.tensor_tensor(sin_w[p][:], trig_raw[p][:, :, 1:2, :].to_broadcast([P, 3, 2, HALF]), w_sin[:],
                                        ALU.mult).then_inc(sin_w_ready, 1)

            def layer_rstd(t, p):
                need(pool, ln_var, t + 1)
                nc.gpsimd.tensor_tensor(ln_ve[:, p:p + 1], ln_mv[:, p, 1:2], eps_ln[:], ALU.add).then_inc(ve_done, 1)
                need(pool, ve_done, t + 1)
                nc.gpsimd.tensor_tensor(ln_rstd[:, p:p + 1], ln_ve[:, p:p + 1], minus_half[:, 0:1], ALU.pow) \
                  .then_inc(rstd_ready, 1)

            def normalize_probs(n, g):
                need(pool, inv_ready, n + 1)
                nc.gpsimd.tensor_tensor(probs[:, 0:REP // 2, :], probs[:, 0:REP // 2, :],
                                        row_inv[g % 2][:, 0:REP // 2].unsqueeze(2).to_broadcast([P, REP // 2, P]),
                                        ALU.mult).then_inc(p_normed, 1)

            def scales(n, g):
                need(pool, q_sq, n + 1)
                need(pool, k_sq, n + 1)
                nc.gpsimd.tensor_tensor(qk_me[:], qk_ms[g % 2][:], eps_rms[:, 0:REP + NB], ALU.add).then_inc(me_done, 1)
                need(pool, me_done, n + 1)
                nc.gpsimd.tensor_tensor(qk_r[g % 2][:], qk_me[:], minus_half[:, 0:REP + NB], ALU.pow).then_inc(r_ready, 1)

            def query_sum(n, g):
                need(pool, q_turned, n + 1)
                nc.gpsimd.tensor_tensor(q_rot[g % 2][:], q_rot[g % 2][:], q_sin[g % 2][:], ALU.add) \
                  .then_inc(q_summed, 1)
                need(pool, q_summed, n + 1)
                nc.gpsimd.tensor_tensor(q_rot[g % 2][:], q_rot[g % 2][:],
                                        qk_r[g % 2][:, 0:REP].unsqueeze(2).to_broadcast([P, REP, HD]), ALU.mult) \
                  .then_inc(q_ready, 1)

            def key_sum(n, g):
                need(pool, k_turned, n + 1)
                nc.gpsimd.tensor_tensor(k_rot[g % 2][:], k_rot[g % 2][:], k_sin[g % 2][:], ALU.add) \
                  .then_inc(k_ready, 1)

            def layer_rstd2(t, p):
                need(pool, var2, t + 1)
                nc.gpsimd.tensor_tensor(ln_ve[:, p:p + 1], ln_mv[:, p, 1:2], eps_ln[:], ALU.add).then_inc(ve2_done, 1)
                need(pool, ve2_done, t + 1)
                nc.gpsimd.tensor_tensor(ln_rstd[:, p:p + 1], ln_ve[:, p:p + 1], minus_half[:, 0:1], ALU.pow) \
                  .then_inc(rstd2_ready, 1)

            layer_rstd(0, 0)
            pool.wait_ge(pos_ready, 1)
            for c in CHUNKS_P[:2]:
                angles(c)
            pool.wait_ge(wsin_ready, 1)
            cos_table(0, 0)
            sin_table(0)
            angles(CHUNKS_P[2])
            scales(0, 0)
            query_sum(0, 0)
            key_sum(0, 0)

            def pair(i, first, last):
                for u in range(2 * KVH):
                    p, g = divmod(u, KVH)
                    t, n = 2 * i + p, 8 * i + u
                    end = last and p == 1
                    if not (end and g == 3):
                        scales(n + 1, g + 1)
                        query_sum(n + 1, g + 1)
                        key_sum(n + 1, g + 1)
                    normalize_probs(n, g)
                    if g == 0 and not end:
                        cos_table(i + p, 1 - p)
                        layer_rstd(t + 1, 1 - p)
                    if g == 1 and not end:
                        sin_table(1 - p)
                    if g == 1 and end:
                        layer_rstd2(0, 0)

            walk(pool, pair)

            def pair2(i, first, last):
                for p in range(2):
                    if not (last and p == 1):
                        layer_rstd2(2 * i + p + 1, 1 - p)
                    if first and p == 0:
                        for k in range(1, BLOCKS):
                            down_lo(k)

            def down_lo(k):
                pool.wait_ge(w2_hi, W2_ORDER.index(f"d{k}") + 1)
                raw, hi, lo = wd_piece(k)
                nc.gpsimd.tensor_tensor(lo, raw, hi.bitcast(F32), ALU.subtract).then_inc(wd_lo_done, 1)

            down_lo(0)
            walk(pool, pair2)

        @block.scalar
        def _(act):
            act.wait_ge(consts_set, 6)
            nc.scalar.activation(gates[:, 0:1], half_pi[:], ACT.Sin)
            turns = [0]

            def tables(c):
                if c in CHUNKS_V:
                    act.wait_ge(angle_v, CHUNKS_V.index(c) + 1)
                else:
                    act.wait_ge(angle_p, CHUNKS_P.index(c) + 1)
                turns[0] += 1
                cos, sin = sincos[c][:, :, 0, :], sincos[c][:, :, 1, :]
                nc.scalar.activation(cos, sin, ACT.Abs).then_inc(abs_ready, 1)
                nc.scalar.activation(sin, sin, ACT.Sin)
                act.wait_ge(abs_ready, turns[0])
                nc.scalar.activation(cos, cos, ACT.Sin, bias=half_pi[:], scale=-1.0).then_inc(sin_ready, 1)
                act.wait_ge(sin_ready, turns[0])
                src, t0 = divmod(c * CH, TILES)
                act.dma_start(trig[src, t0:t0 + CH, :, :, :].rearrange("t p c n -> p t (c n)"),
                              sincos[c][:].rearrange("p t c n -> p t (c n)")) \
                   .then_inc(st_trig_first if c in (0, X0) else st_trig, 16)

            pieces = list(split_pieces())

            def split_hi(some):
                for raw, hi, lo, loaded in some:
                    act.wait_ge(loaded, 16)
                    nc.scalar.activation(hi, raw, ACT.Copy).then_inc(w_hi, 1)

            def key_squares(n, g):
                need(act, kv_done, n + 1)
                kv = b_kv[:].rearrange("p (b w n) -> p b w n", b=NB, w=2)
                for b in range(NB):
                    last = nc.scalar.activation(junk[:, REP + b, :], kv[:, b, 0, :], ACT.Square, scale=HD ** -0.5,
                                                accum_out=qk_ms[g % 2][:, REP + b:REP + b + 1])
                last.then_inc(k_sq, 1)

            def query_squares(n, g):
                need(act, q_done, n + 1)
                for h in range(REP):
                    last = nc.scalar.activation(junk[:, h, :], b_q[:, h * HD:(h + 1) * HD], ACT.Square, scale=HD ** -0.5,
                                                accum_out=qk_ms[g % 2][:, h:h + 1])
                last.then_inc(q_sq, 1)

            def queries_out(n, g):
                need(act, qT_done, n + 1)
                nc.scalar.activation(qT[:].rearrange("p b h s -> p h b s"),
                                     b_qT[:].rearrange("p (h b s) -> p h b s", h=REP, b=NB), ACT.Copy).then_inc(q_out, 1)

            def probs_out(n, g):
                need(act, pT_done, n + 1)
                nc.scalar.activation(pT[:].rearrange("p b n -> p (b n)"), b_pT[:], ACT.Copy).then_inc(pT_out, 1)

            def exponentials(n, g):
                need(act, pT_done, n)
                need(act, max_ready, n + 1)
                for j in range(REP):
                    last = nc.scalar.activation(probs[:, j, :], b_sc[:, j * P:(j + 1) * P], ACT.Exp,
                                                bias=neg_max[g % 2][:, j:j + 1], scale=SCALE,
                                                accum_out=row_sum[g % 2][:, j:j + 1])
                last.then_inc(exp_done, 1)

            def attended_hi(n, g):
                need(act, aT_done, n + 1)
                nc.scalar.activation(aT[HI][:].rearrange("p h b s -> p b h s"),
                                     b_aT[:].rearrange("p (b h s) -> p b h s", b=NB, h=REP), ACT.Copy) \
                  .then_inc(aT_hi, 1)

            def context_hi(t, i, p):
                act.wait_ge(ld_ctx[p], 16 * (i + 1))
                nc.scalar.activation(kv_in[p][HI][:, :, 0::3, :], ctx_raw[p][:].rearrange("p c (b s) -> p c b s", b=NB),
                                     ACT.Copy).then_inc(ctx_hi, 1)

            def normed_hi(t, p):
                need(act, xT_done, t + 1)
                nc.scalar.activation(kv_in[p][HI][:, :, 1:3, :],
                                     b_kT[:, DC * P:2 * DC * P].rearrange("p (c b s) -> p c b s", c=DC, b=NB), ACT.Copy) \
                  .then_inc(x_hi, 1)

            def split2_hi(*names):
                for name in names:
                    raw, hi, lo = w2_piece(name)
                    nc.scalar.activation(hi, raw, ACT.Copy).then_inc(w2_hi, 1)

            def tokens_hi(t, p, bank=b_yT):
                need(act, yT_done, t + 1)
                nc.scalar.activation(yT[p][HI][:].rearrange("p c n -> p (c n)"), bank[:, 0:D], ACT.Copy) \
                  .then_inc(yT_hi, 1)

            def lead_tanh(t):
                need(act, lead_ready, t + 1)
                nc.scalar.activation(lead_t[:], lead[:], ACT.Tanh, scale=0.5).then_inc(lead_done, 1)

            split_hi(pieces[0:1])
            tables(0)
            context_hi(0, 0, 0)
            tables(X0)
            split_hi(pieces[1:3])
            normed_hi(0, 0)
            split_hi(pieces[3:6])
            tables(1)
            query_squares(0, 0)
            key_squares(0, 0)
            tables(2)
            tables(X0 + 1)
            split_hi(pieces[6:10])
            tables(X0 + 2)
            tables(X0 + 3)
            query_squares(1, 1)
            tables(3)
            act.wait_ge(ld_const, 16 * N_CONST)
            nc.scalar.activation(gates[:], gates_raw[:], ACT.Tanh).then_inc(gates_ready, 1)
            act.wait_ge(gates_ready, 1)
            nc.scalar.activation(gates_raw[:, 0:1], gates[:, 0:1], ACT.Exp)

            def pair(i, first, last):
                for u in range(2 * KVH):
                    p, g = divmod(u, KVH)
                    t, n = 2 * i + p, 8 * i + u
                    end = last and p == 1
                    queries_out(n, g)
                    if not (end and g == 3):
                        key_squares(n + 1, g + 1)
                    if end and g == 3:
                        split2_hi("g10", "g11")
                        lead_tanh(0)
                    if g == 0 and not end:
                        context_hi(t + 1, i + p, 1 - p)
                    if g == 1 and not end:
                        normed_hi(t + 1, 1 - p)
                    if not (first and u == 0):
                        probs_out(n - 1, g - 1)
                    exponentials(n, g)
                    if not (first and u == 0):
                        attended_hi(n - 1, g - 1)
                    if not (end and g >= 2):
                        query_squares(n + 2, g)
                    if end and g == 2:
                        act.wait_ge(ld_w2, 48)
                        split2_hi("r", "g00", "g01")
                        tokens_hi(0, 0, b_q)

            walk(act, pair)
            nc.scalar.activation(gates_raw[:, 0:1], gates[:, 0:1], ACT.Silu)

            def silu_gate(m, k):
                need(act, gu_done, m + 1)
                nc.scalar.activation(silu[k % 2][:], b_gate[k % 2][:, 0:FB], ACT.Silu).then_inc(silu_done, 1)

            def hidden_hi(m):
                need(act, hT_done, m + 1)
                nc.scalar.activation(hT[HI][:].rearrange("p c n -> p (c n)"), b_hT[:, 0:FW], ACT.Copy) \
                  .then_inc(hT_hi, 1)

            def pair2(i, first, last):
                for u in range(2 * BLOCKS):
                    p, k = divmod(u, BLOCKS)
                    t, m = 2 * i + p, 2 * BLOCKS * i + u
                    end = last and p == 1
                    silu_gate(m, u)
                    if k == 2 and not end:
                        tokens_hi(t + 1, 1 - p)
                    if k == 4 and not end:
                        lead_tanh(t + 1)
                    if first and u == 0:
                        probs_out(4 * TILES - 1, 3)
                    if first and u == 1:
                        attended_hi(4 * TILES - 1, 3)
                    if not (first and u == 0):
                        hidden_hi(m - 1)
                    if first and p == 0:
                        split2_hi(*(("g20", "g21", "d0"), ("d1", "g30", "g31"), ("d2", "g40", "g41"), ("d3",), ("d4",))[k])

            walk(act, pair2)
            hidden_hi(BLOCKS * TILES - 1)

        @block.vector
        def _(dve):
            dve.wait_ge(ld_pos, 48)
            nc.vector.tensor_copy(pos_f[:], pos_i[:]).then_inc(pos_ready, 1)
            dve.wait_ge(pos_ready, 1)
            steps = [0]

            def link(ins):
                steps[0] += 1
                ins.then_inc(step_v, 1)
                dve.wait_ge(step_v, steps[0])

            def angles(c):
                angle_steps(nc.vector, c, sincos[c][:, :, 1, :], turn_v[:], None, link, angle_v)

            pieces = list(enumerate(split_pieces()))

            def split_lo(some):
                for n, (raw, hi, lo, loaded) in some:
                    dve.wait_ge(w_hi, n + 1)
                    nc.vector.tensor_tensor(lo, raw, hi.bitcast(F32), ALU.subtract).then_inc(w_lo, 1)

            def layer_stats(t, i, p):
                dve.wait_ge(ld_x[p], 16 * (i + 1))
                nc.vector.bn_stats(ln_stats[:], x_in[p][:]).then_inc(stats_done, 1)

            def layer_var(p):
                nc.vector.bn_aggr(ln_mv[:, p, :], ln_stats[:]).then_inc(ln_var, 1)

            def normalize_x(t, p):
                need(dve, rstd_ready, t + 1)
                nc.vector.tensor_scalar(x_n[:], x_in[p][:], ln_mv[:, p, 0:1], ln_rstd[:, p:p + 1], ALU.subtract,
                                        ALU.mult).then_inc(x_normed, 1)

            def context_lo(t, p):
                need(dve, ctx_hi, t + 1)
                nc.vector.tensor_tensor(kv_in[p][LO][:, :, 0::3, :], ctx_raw[p][:].rearrange("p c (b s) -> p c b s", b=NB),
                                        kv_in[p][HI][:, :, 0::3, :].bitcast(F32), ALU.subtract).then_inc(ctx_lo, 1)

            def normed_lo(t, p):
                need(dve, x_hi, t + 1)
                nc.vector.tensor_tensor(kv_in[p][LO][:, :, 1:3, :],
                                        b_kT[:, DC * P:2 * DC * P].rearrange("p (c b s) -> p c b s", c=DC, b=NB),
                                        kv_in[p][HI][:, :, 1:3, :].bitcast(F32), ALU.subtract).then_inc(x_lo, 1)

            def values_out(n, g):
                need(dve, k_sq, n + 1)
                kv = b_kv[:].rearrange("p (b w n) -> p b w n", b=NB, w=2)
                nc.vector.tensor_copy(v_s[g % KVH][:], kv[:, :, 1, :]).then_inc(v_out, 1)

            def turn_keys(n, g, p):
                need(dve, r_ready, n + 1)
                kv = b_kv[:].rearrange("p (b w h n) -> p b w h n", b=NB, w=2, h=2)
                for b in range(NB):
                    r = qk_r[g % 2][:, REP + b:REP + b + 1]
                    k3 = "p (h n) -> p h n"
                    nc.vector.scalar_tensor_tensor(out=k_rot[g % 2][:, b, :].rearrange(k3, h=2), in0=kv[:, b, 0, :, :],
                                                   scalar=r, in1=cos_w[p][:, 1 + b, :, :], op0=ALU.mult, op1=ALU.mult)
                    last = nc.vector.scalar_tensor_tensor(out=k_sin[g % 2][:, b, :].rearrange(k3, h=2),
                                                          in0=kv[:, b, 0, ::-1, :], scalar=r,
                                                          in1=sin_w[p][:, 1 + b, :, :], op0=ALU.mult, op1=ALU.mult)
                last.then_inc(k_turned, 1)

            def turn_queries(n, g, t, p):
                need(dve, q_sq, n + 1)
                if g % KVH == 0:
                    need(dve, sin_w_ready, t + 1)
                q = b_q[:].rearrange("p (h a n) -> p h a n", h=REP, a=2)
                q4 = "p h (a n) -> p h a n"
                shape = [P, REP, 2, HALF]
                nc.vector.tensor_tensor(q_rot[g % 2][:].rearrange(q4, a=2), q,
                                        cos_w[p][:, 0, :, :].unsqueeze(1).to_broadcast(shape), ALU.mult)
                nc.vector.tensor_tensor(q_sin[g % 2][:].rearrange(q4, a=2), q[:, :, ::-1, :],
                                        sin_w[p][:, 0, :, :].unsqueeze(1).to_broadcast(shape), ALU.mult) \
                  .then_inc(q_turned, 1)

            def keys_out(n, g):
                need(dve, kT_done, n + 1)
                nc.vector.tensor_copy(kT[:].rearrange("p b n -> p (b n)"), b_kT[:, 0:NB * P]).then_inc(k_out, 1)

            def score_max(n, g):
                need(dve, sc_done, n + 1)
                nc.vector.tensor_reduce(row_max[:], b_sc[:].rearrange("p (j n) -> p j n", j=REP), AX.X, ALU.max) \
                  .then_inc(max_found, 1)
                need(dve, max_found, n + 1)
                nc.vector.tensor_scalar(neg_max[g % 2][:], row_max[:], -SCALE, None, ALU.mult).then_inc(max_ready, 1)

            def sum_inverse(n, g):
                need(dve, exp_done, n + 1)
                nc.vector.reciprocal(row_inv[g % 2][:], row_sum[g % 2][:]).then_inc(inv_ready, 1)
                need(dve, inv_ready, n + 1)
                nc.vector.tensor_tensor(probs[:, REP // 2:REP, :], probs[:, REP // 2:REP, :],
                                        row_inv[g % 2][:, REP // 2:REP].unsqueeze(2).to_broadcast([P, REP // 2, P]),
                                        ALU.mult).then_inc(p_normed2, 1)

            def attended_lo(n, g):
                need(dve, aT_hi, n + 1)
                nc.vector.tensor_tensor(aT[LO][:].rearrange("p h b s -> p b h s"),
                                        b_aT[:].rearrange("p (b h s) -> p b h s", b=NB, h=REP),
                                        aT[HI][:].bitcast(F32).rearrange("p h b s -> p b h s"), ALU.subtract) \
                  .then_inc(aT_lo, 1)

            def residual(t, i, p):
                if not isinstance(i, int) or i >= 1:
                    dve.wait_ge(st_x1[p], 16 * i)
                dve.wait_ge(ld_res[p], 16 * (i + 1))
                need(dve, o_done, KVH * (t + 1))
                nc.vector.scalar_tensor_tensor(out=x1_out[p][:], in0=b_o[:, 0:D], scalar=gates[:, 0:1],
                                               in1=x_res[p][:], op0=ALU.mult, op1=ALU.add).then_inc(x1_ready, 1)

            def layer_stats2(t, i, p):
                dve.wait_ge(ld_y[p], 16 * (i + 1))
                nc.vector.bn_stats(ln_stats[:], y_in[p][:]).then_inc(stats2, 1)

            def layer_var2(p):
                nc.vector.bn_aggr(ln_mv[:, p, :], ln_stats[:]).then_inc(var2, 1)

            def normalize_y(t, p):
                need(dve, rstd2_ready, t + 1)
                nc.vector.tensor_scalar(y_n[:], y_in[p][:], ln_mv[:, p, 0:1], ln_rstd[:, p:p + 1], ALU.subtract,
                                        ALU.mult).then_inc(y_normed, 1)

            def tokens_lo(t, p, bank=b_yT):
                need(dve, yT_hi, t + 1)
                nc.vector.tensor_tensor(yT[p][LO][:].rearrange("p c n -> p (c n)"), bank[:, 0:D],
                                        yT[p][HI][:].rearrange("p c n -> p (c n)").bitcast(F32), ALU.subtract) \
                  .then_inc(yT_lo, 1)

            def copy_logits(t, bank=b_yT):
                need(dve, lg_done, t + 1)
                nc.vector.tensor_copy(logits[:], bank[:, D:D + E]).then_inc(lg_copied, 1)

            def top_two(t):
                nc.vector.max(top_v[:], logits[:]).then_inc(top_found, 1)
                need(dve, top_found, t + 1)
                nc.vector.tensor_tensor(lead[:], top_v[:, 0:1], top_v[:, 1:2], ALU.subtract).then_inc(lead_ready, 1)
                nc.vector.max_index(top_i[:], top_v[:], logits[:]).then_inc(idx_found, 1)

            def combine_weights(t, p):
                need(dve, idx_found, t + 1)
                nc.vector.tensor_copy(top_f[:], top_i[:, 0:TOPK])
                need(dve, lead_done, t + 1)
                nc.vector.tensor_scalar(share[:, 0:1], lead_t[:], ROUTED_SCALE / 2, ROUTED_SCALE / 2, ALU.mult, ALU.add)
                nc.vector.tensor_scalar(share[:, 1:2], lead_t[:], -ROUTED_SCALE / 2, ROUTED_SCALE / 2, ALU.mult,
                                        ALU.add).then_inc(share_ready, 1)
                need(dve, share_ready, t + 1)
                for n in range(TOPK):
                    last = nc.vector.tensor_scalar(pick[:, n, :], expert_no[:], top_f[:, n:n + 1], share[:, n:n + 1],
                                                   ALU.is_equal, ALU.mult)
                last.then_inc(pick_ready, 1)
                need(dve, pick_ready, t + 1)
                nc.vector.tensor_tensor(combine[p][:], pick[:, 0, :], pick[:, 1, :], ALU.add).then_inc(combine_ready, 1)

            def split2_lo(*names):
                for name in names:
                    raw, hi, lo = w2_piece(name)
                    dve.wait_ge(w2_hi, W2_ORDER.index(name) + 1)
                    nc.vector.tensor_tensor(lo, raw, hi.bitcast(F32), ALU.subtract).then_inc(wg_lo_done, 1)

            layer_stats(0, 0, 0)
            dve.wait_ge(stats_done, 1)
            layer_var(0)
            angles(0)
            normalize_x(0, 0)
            angles(X0)
            split_lo(pieces[0:1])
            context_lo(0, 0)
            split_lo(pieces[1:3])
            normed_lo(0, 0)
            split_lo(pieces[3:4])
            angles(1)
            dve.wait_ge(ld_const, 16 * N_CONST)
            nc.vector.tensor_scalar(w_sin[:, :, 0, :], w_sin[:, :, 0, :], -1.0, None, ALU.mult).then_inc(wsin_ready, 1)
            angles(X0 + 1)
            split_lo(pieces[4:6])
            angles(X0 + 3)
            turn_queries(0, 0, 0, 0)
            split_lo(pieces[6:10])
            values_out(0, 0)
            turn_keys(0, 0, 0)

            def pair(i, first, last):
                for u in range(2 * KVH):
                    p, g = divmod(u, KVH)
                    t, n = 2 * i + p, 8 * i + u
                    end = last and p == 1
                    p1 = p if g < 3 else 1 - p
                    keys_out(n, g)
                    if not (end and g == 3):
                        turn_queries(n + 1, g + 1, t + (g == 3), p1)
                        values_out(n + 1, g + 1)
                    if g == 1 and not end:
                        normalize_x(t + 1, 1 - p)
                    if g == 1 and not (first and p == 0):
                        if first:
                            dve.wait_ge(gates_ready, 1)
                        residual(t - 1, i - 1 + p, 1 - p)
                    if end and g == 2:
                        normalize_y(0, 0)
                    if end and g == 3:
                        copy_logits(0, b_q)
                        dve.wait_ge(lg_copied, 1)
                        top_two(0)
                    score_max(n, g)
                    if not (end and g == 3):
                        turn_keys(n + 1, g + 1, p1)
                    if g == 1 and not end:
                        normed_lo(t + 1, 1 - p)
                    if g == 0 and not end:
                        layer_stats(t + 1, i + p, 1 - p)
                        context_lo(t + 1, 1 - p)
                        need(dve, stats_done, t + 2)
                    if end and g == 3:
                        split2_lo("g10", "g11")
                    sum_inverse(n, g)
                    if g == 0 and not end:
                        layer_var(1 - p)
                    if not (first and u == 0):
                        attended_lo(n - 1, g - 1)
                    if end and g == 1:
                        layer_stats2(0, 0, 0)
                        dve.wait_ge(stats2, 1)
                        layer_var2(0)
                    if end and g == 2:
                        split2_lo("r", "g00", "g01")
                        tokens_lo(0, 0, b_q)
                    if end and g == 3:
                        combine_weights(0, 0)
            walk(dve, pair)
            for p in range(2):
                last = nc.vector.memset(hid[p][:, FB:FW], 0.0)
            last.then_inc(pad_done, 1)

            def hidden(m, u, k, p, t):
                need(dve, silu_done, m + 1)
                up = b_up[u % 2]
                if k == 0:
                    nc.vector.tensor_tensor(hid[u % 2][:, 0:FB], silu[u % 2][:], up[:, 0:FB], ALU.mult) \
                      .then_inc(hid_ready, 1)
                    return
                if k == 1:
                    need(dve, combine_ready, t + 1)
                for j in range(2):
                    cols = slice(j * F, (j + 1) * F)
                    e = 2 * (k - 1) + j
                    last = nc.vector.scalar_tensor_tensor(out=hid[u % 2][:, cols], in0=silu[u % 2][:, cols],
                                                          scalar=combine[p][:, e:e + 1], in1=up[:, cols],
                                                          op0=ALU.mult, op1=ALU.mult)
                last.then_inc(hid_ready, 1)

            def hidden_lo(m):
                need(dve, hT_hi, m + 1)
                nc.vector.tensor_tensor(hT[LO][:].rearrange("p c n -> p (c n)"), b_hT[:, 0:FW],
                                        hT[HI][:].rearrange("p c n -> p (c n)").bitcast(F32), ALU.subtract) \
                  .then_inc(hT_lo, 1)

            def output(t, i, p):
                if not isinstance(i, int) or i >= 1:
                    dve.wait_ge(st_out[p], 16 * i)
                dve.wait_ge(ld_yres[p], 16 * (i + 1))
                need(dve, y_done, BLOCKS * (t + 1))
                nc.vector.scalar_tensor_tensor(out=o_out[p][:], in0=b_y[p][:, 0:D], scalar=gates[:, 1:2],
                                               in1=y_res[p][:], op0=ALU.mult, op1=ALU.add).then_inc(out_ready, 1)

            def pair2(i, first, last):
                for u in range(2 * BLOCKS):
                    p, k = divmod(u, BLOCKS)
                    t, m = 2 * i + p, 2 * BLOCKS * i + u
                    end = last and p == 1
                    if k == 0 and not end:
                        layer_stats2(t + 1, i + p, 1 - p)
                    hidden(m, u, k, p, t)
                    if not end:
                        if k == 0:
                            need(dve, stats2, t + 2)
                        if k == 2:
                            tokens_lo(t + 1, 1 - p)
                        if k == 3:
                            copy_logits(t + 1)
                            need(dve, lg_copied, t + 2)
                    if first and u == 1:
                        attended_lo(4 * TILES - 1, 3)
                    if not (first and u == 0):
                        hidden_lo(m - 1)
                    if first and u == 2:
                        residual(TILES - 1, PAIRS - 1, 1)
                    if first and u < 3:
                        split2_lo(f"g{u + 2}0", f"g{u + 2}1")
                    if not end:
                        if k == 0:
                            layer_var2(1 - p)
                        if k == 1:
                            normalize_y(t + 1, 1 - p)
                        if k == 3:
                            top_two(t + 1)
                        if k == 4:
                            combine_weights(t + 1, 1 - p)
                    if k == 1 and not (first and p == 0):
                        output(t - 1, i - 1 + p, 1 - p)

            walk(dve, pair2)
            hidden_lo(BLOCKS * TILES - 1)
            output(TILES - 1, PAIRS - 1, 1)

        @block.tensor
        def _(pe):
            pe.wait_ge(ident_done, 1)

            def normed_x_T(t, p):
                need(pe, x_normed, t + 1)
                for c in range(DC):
                    last = nc.tensor.transpose(b_kT[:, (DC + c) * P:(DC + c + 1) * P], x_n[:, c * P:(c + 1) * P],
                                               ident[:])
                last.then_inc(xT_done, 1)

            def queries(n, g, t, p):
                need(pe, q_turned, n)
                if g % KVH == 0:
                    need(pe, x_lo, t + 1)
                gg = g % KVH
                for c in range(DC):
                    for a, b in PASSES:
                        last = nc.tensor.matmul(b_q[:], kv_in[p][a][:, c, 1:3, :],
                                                wq_s[b][:, c, gg * REP * HD:(gg + 1) * REP * HD],
                                                start=(c == 0 and (a, b) == PASSES[0]),
                                                stop=(c == DC - 1 and (a, b) == PASSES[-1]))
                last.then_inc(q_done, 1)

            def keys_values(n, g, t, p):
                need(pe, k_turned, n)
                if g % KVH == 0:
                    need(pe, ctx_lo, t + 1)
                for s in range(NB):
                    for c in range(DC):
                        for a, b in PASSES:
                            last = nc.tensor.matmul(b_kv[:, s * 2 * HD:(s + 1) * 2 * HD],
                                                    kv_in[p][a][:, c, 2 * s:2 * s + 2, :],
                                                    wkv_s[b][:, c, g % KVH, :],
                                                    start=(c == 0 and (a, b) == PASSES[0]),
                                                    stop=(c == DC - 1 and (a, b) == PASSES[-1]))
                last.then_inc(kv_done, 1)

            def heads_T(n, g):
                need(pe, k_ready, n + 1)
                for s in range(NB):
                    last = nc.tensor.transpose(b_kT[:, s * P:(s + 1) * P], k_rot[g % 2][:, s, :], ident[:])
                last.then_inc(kT_done, 1)
                need(pe, q_ready, n + 1)
                for h in range(REP):
                    last = nc.tensor.transpose(b_qT[:, h * P:(h + 1) * P], q_rot[g % 2][:, h, :], ident[:])
                last.then_inc(qT_done, 1)

            def scores(n, g):
                need(pe, exp_done, n)
                need(pe, k_out, n + 1)
                need(pe, q_out, n + 1)
                for s in range(NB):
                    for j in range(REP // 2):
                        o = (s * (REP // 2) + j) * P
                        last = nc.tensor.matmul(b_sc[:, o:o + P], qT[:, s, 2 * j:2 * j + 2, :], kT[:, s, :],
                                                start=True, stop=True)
                last.then_inc(sc_done, 1)

            def probs_T(n, g):
                need(pe, p_normed, n + 1)
                need(pe, p_normed2, n + 1)
                for j in range(REP):
                    last = nc.tensor.transpose(b_pT[:, j * P:(j + 1) * P], probs[:, j, :], ident[:])
                last.then_inc(pT_done, 1)

            def attend(n, g):
                need(pe, pT_out, n + 1)
                for s in range(NB):
                    last = nc.tensor.matmul(b_aT[:, s * REP * S:(s + 1) * REP * S], v_s[g % KVH][:, s, :],
                                            pT[:, s, :], start=True, stop=True)
                last.then_inc(aT_done, 1)

            def project(n, g, t):
                gg = g % KVH
                need(pe, aT_lo, n + 1)
                if gg == 0:
                    need(pe, x1_ready, t)
                for h in range(REP):
                    for a, b in PASSES:
                        last = nc.tensor.matmul(b_o[:, 0:D], aT[a][:, h, :, :], wo_s[b][:, gg * REP + h, :],
                                                start=(gg == 0 and h == 0 and (a, b) == PASSES[0]),
                                                stop=(gg == KVH - 1 and h == REP - 1 and (a, b) == PASSES[-1]))
                last.then_inc(o_done, 1)

            normed_x_T(0, 0)
            pe.wait_ge(w_lo, QUERY_SPLITS[0])
            queries(0, 0, 0, 0)
            pe.wait_ge(w_lo, KV_SPLITS)
            keys_values(0, 0, 0, 0)
            pe.wait_ge(w_lo, QUERY_SPLITS[1])
            queries(1, 1, 0, 0)
            keys_values(1, 1, 0, 0)

            def pair(i, first, last):
                for u in range(2 * KVH):
                    p, g = divmod(u, KVH)
                    t, n = 2 * i + p, 8 * i + u
                    end = last and p == 1
                    t2, p2 = t + (g >= 2), (p if g < 2 else 1 - p)
                    if g == 2 and not end:
                        need(pe, x_lo, t + 2)
                    heads_T(n, g)
                    if first and u == 2:
                        pe.wait_ge(w_lo, SPLITS)
                    if not (first and u < 2):
                        project(n - 2, g - 2, t if g >= 2 else t - 1)
                    scores(n, g)
                    if g == 1 and not end:
                        normed_x_T(t + 1, 1 - p)
                    if not (first and u < 1):
                        probs_T(n - 1, g - 1)
                    if end and g == 2:
                        pe.wait_ge(q_turned, n + 2)
                        tokens_T(0, 0, b_q)
                    if end and g == 3:
                        gate_up(0, 0, 0, 0)
                    if first and u < 2:
                        pe.wait_ge(w_lo, QUERY_SPLITS[u + 2])
                    if not (end and g >= 2):
                        queries(n + 2, g + 2, t2, p2)
                    if not (first and u < 1):
                        attend(n - 1, g - 1)
                    if not (end and g >= 2):
                        keys_values(n + 2, g + 2, t2, p2)
                    if end and g == 2:
                        router(0, 0, b_q)

            def tokens_T(t, p, bank=b_yT):
                need(pe, y_normed, t + 1)
                need(pe, lg_copied, t)
                for c in range(DC):
                    last = nc.tensor.transpose(bank[:, c * P:(c + 1) * P], y_n[:, c * P:(c + 1) * P], ident[:])
                last.then_inc(yT_done, 1)

            def router(t, p, bank=b_yT):
                if isinstance(t, int) and t == 0:
                    pe.wait_ge(wg_lo_done, 1)
                need(pe, yT_lo, t + 1)
                for c in range(DC):
                    for a, b in PASSES:
                        last = nc.tensor.matmul(bank[:, D:D + E], yT[p][a][:, c, :], wr_s[b][:, c, :],
                                                start=(c == 0 and (a, b) == PASSES[0]),
                                                stop=(c == DC - 1 and (a, b) == PASSES[-1]))
                last.then_inc(lg_done, 1)

            def gate_up(m, u, k, p):
                need(pe, hid_ready, m - 1)
                if isinstance(m, int) and m < BLOCKS:
                    pe.wait_ge(wg_lo_done, 1 + DC * (m + 1))
                    if m == 0:
                        pe.wait_ge(lg_copied, 1)
                for j, o in enumerate((b_gate[u % 2], b_up[u % 2])):
                    for c in range(DC):
                        for a, b in PASSES:
                            last = nc.tensor.matmul(o[:, 0:FB], yT[p][a][:, c, :],
                                                    wg_s[b][:, c, k, j * FB:(j + 1) * FB],
                                                    start=(c == 0 and (a, b) == PASSES[0]),
                                                    stop=(c == DC - 1 and (a, b) == PASSES[-1]))
                last.then_inc(gu_done, 1)

            walk(pe, pair)
            project(4 * TILES - 2, 2, TILES - 1)
            gate_up(1, 1, 1, 0)
            probs_T(4 * TILES - 1, 3)
            attend(4 * TILES - 1, 3)

            pe.wait_ge(pad_done, 1)

            def hidden_T(m, u):
                need(pe, hid_ready, m + 1)
                need(pe, hT_lo, m)
                for c in range(FC):
                    last = nc.tensor.transpose(b_hT[:, c * P:(c + 1) * P], hid[u % 2][:, c * P:(c + 1) * P], ident[:])
                last.then_inc(hT_done, 1)

            def down(m, k, t, p):
                need(pe, hT_lo, m + 1)
                if k == 0:
                    need(pe, out_ready, t - 1)
                for c in range(FC):
                    rows = min(P, FB - c * P)
                    for a, b in PASSES:
                        last = nc.tensor.matmul(b_y[p][:, 0:D], hT[a][0:rows, c, :], wd_s[b][0:rows, k, c, :],
                                                start=(k == 0 and c == 0 and (a, b) == PASSES[0]),
                                                stop=(k == BLOCKS - 1 and c == FC - 1 and (a, b) == PASSES[-1]))
                last.then_inc(y_done, 1)

            def pair2(i, first, last):
                for u in range(2 * BLOCKS):
                    p, k = divmod(u, BLOCKS)
                    t, m = 2 * i + p, 2 * BLOCKS * i + u
                    end = last and p == 1
                    if not (first and u < 2):
                        gate_up(m, u, k, p)
                    if first and u == 2:
                        project(4 * TILES - 1, 3, TILES - 1)
                    if k == 2 and not end:
                        tokens_T(t + 1, 1 - p)
                    if k == 3 and not end:
                        router(t + 1, 1 - p)
                    if not (first and u < 2):
                        k2 = (u - 2) % BLOCKS
                        if first and u < 2 + BLOCKS:
                            pe.wait_ge(wd_lo_done, u - 1)
                        if first and u == 2 + BLOCKS:
                            pe.wait_ge(x1_ready, TILES)
                        down(m - 2, k2, t if k >= 2 else t - 1, p if k >= 2 else 1 - p)
                    if not (first and u < 1):
                        hidden_T(m - 1, u - 1)

            walk(pe, pair2)
            M = BLOCKS * TILES
            down(M - 2, BLOCKS - 2, TILES - 1, 1)
            hidden_T(M - 1, 2 * BLOCKS - 1)
            down(M - 1, BLOCKS - 1, TILES - 1, 1)


def kernel(x, ctx_2048, pos_BxS2, itok_BxS_4096_4607, g_xattn, g_ffn, L0_xattn_Wq, L0_xattn_Wk, L0_xattn_Wv,
           L0_xattn_Wo, L0_xattn_q_norm_w, L0_xattn_k_norm_w, L0_ffn_w_router, L0_ffn_w_gate, L0_ffn_w_up,
           L0_ffn_w_down, L0_ffn_ws_gate, L0_ffn_ws_up, L0_ffn_ws_down):
    import numpy as np
    import concourse.bacc as bacc
    from concourse.bass_utils import run_bass_kernel_spmd as run

    def arr(a):
        return np.asarray(a)

    def chunked(w):
        return w.reshape(DC, P, -1).transpose(1, 0, 2)

    wk, wv = arr(L0_xattn_Wk).T, arr(L0_xattn_Wv).T
    wkv = np.stack([wk.reshape(D, KVH, HD), wv.reshape(D, KVH, HD)], 2)
    gate, up, down = arr(L0_ffn_w_gate), arr(L0_ffn_w_up), arr(L0_ffn_w_down)
    gu = [np.concatenate([arr(L0_ffn_ws_gate), arr(L0_ffn_ws_up)], 1)]
    gu += [np.concatenate([gate[e], gate[e + 1], up[e], up[e + 1]], 1) for e in range(0, E, 2)]
    dn = [arr(L0_ffn_ws_down)] + [np.concatenate([down[e], down[e + 1]], 0) for e in range(0, E, 2)]
    dn = [np.concatenate([w, np.zeros((FW - FB, D), w.dtype)], 0).reshape(FC, P, D) for w in dn]
    inv_freq = (np.float32(1.0) / np.float32(10000.0) ** (np.arange(0, HD, 2, dtype=np.float32) / np.float32(HD)))
    ins = {
        "x": arr(x).reshape(TILES, P, D),
        "ctxT": arr(ctx_2048).reshape(TILES, P, DC, P).transpose(0, 3, 2, 1),
        "posx": arr(itok_BxS_4096_4607).reshape(TILES, P).T,
        "posc": arr(pos_BxS2).reshape(TILES, P).T,
        "invf": np.broadcast_to(inv_freq.astype(np.float32), (P, HALF)),
        "g_xattn": arr(g_xattn), "g_ffn": arr(g_ffn),
        "q_w": arr(L0_xattn_q_norm_w), "k_w": arr(L0_xattn_k_norm_w),
        "wq": chunked(arr(L0_xattn_Wq).T),
        "wkv": chunked(wkv.reshape(D, KVH * 2 * HD)).reshape(P, DC, KVH, 2 * HD),
        "wo": arr(L0_xattn_Wo).T.reshape(H, P, D).transpose(1, 0, 2),
        "wr": chunked(arr(L0_ffn_w_router)),
        "wg": chunked(np.concatenate(gu, 1)).reshape(P, DC, BLOCKS, 2 * FB),
        "wd": np.stack(dn).transpose(2, 0, 1, 3),
    }
    nc = bacc.Bacc("TRN2", target_bir_lowering=False, num_devices=1)
    arrays, aps = {}, []
    for name, a in ins.items():
        arrays[f"in_{name}"] = np.ascontiguousarray(a)
        aps.append(nc.dram_tensor(f"in_{name}", a.shape, mybir.dt.from_np(a.dtype), kind="ExternalInput").ap())
    out = nc.dram_tensor("out", (TILES, P, D), F32, kind="ExternalOutput").ap()
    flamingo(nc, *aps, out)
    got = run(nc, [arrays], core_ids=[0]).results[0]["out"]
    return got.reshape(B, S, D)
```

```python
import concourse.bass as bass
from concourse import mybir
from contextlib import ExitStack
import numpy as np

F32 = mybir.dt.float32
F32R = mybir.dt.float32r
I32 = mybir.dt.int32
U32 = mybir.dt.uint32
BF16 = mybir.dt.bfloat16
ALU = mybir.AluOpType
ACT = mybir.ActivationFunctionType
AX = mybir.AxisListType

P = 128
B, S, D = 64, 64, 256
H, KVH, HD = 16, 4, 128
REP = H // KVH
NB = P // S
TILES = B * S // P
PAIRS = TILES // 2
DC = D // P
HALF = HD // 2
E, TOPK, F, FS = 8, 2, 176, 352
FC = -(-FS // P)
FW = FC * P
EFC = -(-F // P)
EFW = EFC * P
REST, AGAIN = F - P, P // 2
STRIDE = B * S + P
PAD_TILES = 2
PAD = (PAD_TILES + 1) * P
QUAD = 4
SLOTS = -(-(TOPK * TILES + E - 1) // QUAD) * QUAD
TURNS = SLOTS // 2
ROUTED_SCALE = 2.5
SCALE = float(np.float32(1.0) / np.sqrt(np.float32(HD)))
RMS_EPS, LN_EPS = 1e-6, 1e-5
TWO_PI = (6.28125, 0.0019350051879882812, 2 * np.pi - 6.28125 - 0.0019350051879882812)
ROUND = 1.5 * 2.0 ** 23
PI_BELOW = 3.1415925
PASSES = ((0, 0), (0, 1), (1, 0))
HI, LO = 0, 1


def need(eng, sem, count):
    if not isinstance(count, int) or count > 0:
        eng.wait_ge(sem, count)


def walk(eng, body, pairs=PAIRS, start=1):
    for i in range(start):
        body(i, i == 0, False)
    with eng.Fori(start, pairs - 1) as i:
        body(i, False, False)
    body(pairs - 1, False, True)


def flamingo(nc, x, ctxT, posx, posc, invf, g_xattn, g_ffn, q_w, k_w, wq, wkv, wo, wr, wg, wd, out):
    ctx = ExitStack()
    with ctx:
        cursor = [-(-nc.sbuf_base // 64) * 64]

        def sb(name, shape, dt, at=None):
            size = int(np.prod(shape[1:])) * mybir.dt.size(dt)
            where = cursor if at is None else at
            t = nc.alloc_sbuf_tensor_at(name, shape, dt, offset=where[0])
            where[0] += -(-size // 64) * 64
            return t

        def parts(name, shape, at=None):
            return [sb(f"{name}_{p}", shape, F32R, at) for p in ("hi", "lo")]

        ident = sb("ident", [P, P], F32)
        gates = sb("gates", [P, 2], F32)
        gates_raw = sb("gates_raw", [P, 2], F32)
        minus_half = sb("minus_half", [P, 8], F32)
        eps_rms = sb("eps_rms", [P, 8], F32)
        eps_ln = sb("eps_ln", [P, 1], F32)
        half_pi = sb("half_pi", [P, 1], F32)
        expert_no = sb("expert_no", [P, E], F32)
        ln_stats = sb("ln_stats", [P, 6], F32)
        ln_mv = sb("ln_mv", [P, 2, 2], F32)
        ln_ve = sb("ln_ve", [P, 2], F32)
        ln_rstd = sb("ln_rstd", [P, 2], F32)
        ln2_stats = sb("ln2_stats", [P, 6], F32)
        ln2_mv = sb("ln2_mv", [P, 2], F32)
        ln2_ve = sb("ln2_ve", [P, 1], F32)
        ln2_rstd = sb("ln2_rstd", [P, 1], F32)
        wr_raw = sb("wr_raw", [P, DC, E], F32)
        wr_both = sb("wr", [P, DC, 2, E], F32R)
        wr_s = [wr_both[:, :, a, :] for a in (HI, LO)]
        stage_at = list(cursor)
        GU, DN = 2 * FS + 2 * E * F, FC + E * EFC
        wg_at = list(cursor)
        wg_raw = sb("wg_raw", [P, DC, GU], F32)
        wd_at = list(cursor)
        wd_raw = sb("wd_raw", [P, DN, D], F32)
        wg_lo = sb("wg_lo", [P, DC, GU], F32R, wg_at)
        wd_lo = sb("wd_lo", [P, DN, D], F32R, wd_at)
        wq_raw = sb("wq_raw", [P, DC, H * HD], F32, stage_at)
        wkv_raw = sb("wkv_raw", [P, DC, KVH, 2 * HD], F32, stage_at)
        wo_raw = sb("wo_raw", [P, H, D], F32, stage_at)
        assert stage_at[0] <= cursor[0] and EFC == 2 and REST <= AGAIN
        assert (TILES - PAD_TILES) * P + PAD <= STRIDE
        stage_end = cursor[0]
        phase_at = list(cursor)
        wq_s = parts("wq", [P, DC, H * HD])
        wkv_s = parts("wkv", [P, DC, KVH, 2 * HD])
        phase_end = cursor[0]
        wo_s = parts("wo", [P, H, D])
        w_cos = sb("w_cos", [P, 3, 2, HALF], F32)
        w_sin = sb("w_sin", [P, 3, 2, HALF], F32)
        trig_raw = [sb(f"trig_raw{p}", [P, 3, 2, HALF], F32) for p in range(2)]
        cos_w = [sb(f"cos_w{p}", [P, 3, 2, HALF], F32) for p in range(2)]
        sin_w = [sb(f"sin_w{p}", [P, 3, 2, HALF], F32) for p in range(2)]
        free_end = cursor[0]
        x_in = [sb(f"x_in{p}", [P, D], F32) for p in range(2)]
        x_res = [sb(f"x_res{p}", [P, D], F32) for p in range(2)]
        x1_out = [sb(f"x1_out{p}", [P, D], F32) for p in range(2)]
        ctx_raw = [sb(f"ctx_raw{p}", [P, DC, P], F32) for p in range(2)]
        x_n = sb("x_n", [P, D], F32)
        kv_in = [parts(f"kv_in{p}", [P, DC, 4, S]) for p in range(2)]
        junk = sb("junk", [P, REP + NB, HD], BF16)
        qk_ms = [sb(f"qk_ms{p}", [P, REP + NB], F32) for p in range(2)]
        qk_me = sb("qk_me", [P, REP + NB], F32)
        qk_r = [sb(f"qk_r{p}", [P, REP + NB], F32) for p in range(2)]
        q_rot = [sb(f"q_rot{p}", [P, REP, HD], F32) for p in range(2)]
        q_sin = [sb(f"q_sin{p}", [P, REP, HD], F32) for p in range(2)]
        k_rot = [sb(f"k_rot{p}", [P, NB, HD], F32) for p in range(2)]
        k_sin = [sb(f"k_sin{p}", [P, NB, HD], F32) for p in range(2)]
        v_s = [sb(f"v{g}", [P, NB, HD], F32) for g in range(KVH)]
        early_at = list(cursor)
        qT = sb("qT", [P, NB, REP, S], F32)
        kT = sb("kT", [P, NB, P], F32)
        probs = sb("probs", [P, REP, P], F32)
        pT = sb("pT", [P, NB, REP * S], F32)
        aT = parts("aT", [P, REP, NB, S])
        early_end = cursor[0]
        row_max = sb("row_max", [P, REP], F32)
        neg_max = [sb(f"neg_max{p}", [P, REP], F32) for p in range(2)]
        row_sum = [sb(f"row_sum{p}", [P, REP], F32) for p in range(2)]
        row_inv = [sb(f"row_inv{p}", [P, REP], F32) for p in range(2)]
        late_at = list(cursor)
        CH = 8
        NCH = 2 * TILES // CH
        X0 = NCH // 2
        turn_p = sb("turn_p", [P, CH, HALF], F32, stage_at)
        pos_f = sb("pos_f", [P, 2 * TILES], F32, stage_at)
        sincos = [sb(f"sincos{c}", [P, CH, 2, HALF], F32,
                     early_at if c in (0, X0) else stage_at if c == 2 else None) for c in range(NCH)]
        invf_s = sb("invf_s", [P, HALF], F32, early_at)
        pos_i = sb("pos_i", [P, 2 * TILES], I32, early_at)
        assert early_at[0] <= early_end and cursor[0] <= nc.sbuf_usable_end, (early_at, early_end, cursor)
        wg_s = [sb("wg_hi", [P, DC, GU], F32R, phase_at), wg_lo]
        wd_s = [sb("wd_hi", [P, DN, D], F32R, phase_at), wd_lo]
        assert phase_at[0] <= phase_end and stage_at[0] <= stage_end, (phase_at, phase_end, stage_at, stage_end)
        y_n = [sb(f"y_n{p}", [P, D], F32, late_at) for p in range(2)]
        yT_both = [sb(f"yT{p}", [P, 2, DC, P], F32R, late_at) for p in range(2)]
        yT = [[yT_both[p][:, a, :, :] for a in (HI, LO)] for p in range(2)]
        below = sb("below", [P, P], F32R, late_at)
        ones = sb("ones", [P, P], F32R, late_at)
        below_f = sb("below_f", [P, P], F32, late_at)
        zeros = sb("zeros", [P, D], F32, late_at)
        logits = sb("logits", [P, E], F32, late_at)
        top_v = sb("top_v", [P, 8], F32, late_at)
        top_i = sb("top_i", [P, 8], U32, late_at)
        top_f = sb("top_f", [P, TOPK], F32, late_at)
        lead = sb("lead", [P, 1], F32, late_at)
        lead_t = sb("lead_t", [P, 1], F32, late_at)
        share = sb("share", [P, TOPK], F32, late_at)
        pick = sb("pick", [P, TOPK, E], F32, late_at)
        mask = sb("mask", [P, E], F32R, late_at)
        seen = sb("seen", [P, E], F32R, late_at)
        ranked = sb("ranked", [P, TOPK, E], F32, late_at)
        rank = sb("rank", [P, TOPK], F32, late_at)
        row_f = sb("row_f", [P, TOPK], F32, late_at)
        row_i = [sb(f"row_i{p}", [P, TOPK], I32, late_at) for p in range(2)]
        w_all = sb("w_all", [P, TILES, TOPK], F32, late_at)
        e_all = sb("e_all", [P, TILES, TOPK], F32, late_at)
        rank_all = sb("rank_all", [P, TILES, TOPK], F32, late_at)
        count = sb("count", [P, E], F32, late_at)
        first_pad = sb("first_pad", [P, E], I32, late_at)
        full = sb("full", [P, E], F32, late_at)
        upto = [sb(f"upto{n}", [P, E], F32, late_at) for n in range(4)]
        slot_no = sb("slot_no", [P, SLOTS], F32, late_at)
        s_expert, s_first, s_valid, s_row, s_a, s_b = [sb(n, [P, SLOTS], F32, late_at) for n in (
            "s_expert", "s_first", "s_valid", "s_row", "s_a", "s_b")]
        slot_expert = sb("slot_expert", [P, SLOTS], I32, late_at)
        slot_row = sb("slot_row", [P, SLOTS], I32, late_at)
        assert late_at[0] <= nc.sbuf_usable_end, late_at
        free_at = [phase_end]
        past = sb("past", [P, SLOTS, E], F32, free_at)
        past_w = sb("past_w", [P, SLOTS, E], F32, free_at)
        at_e = sb("at_e", [P, TILES * TOPK, E], F32, free_at)
        at_w = sb("at_w", [P, TILES * TOPK, E], F32, free_at)
        at_s = sb("at_s", [P, TILES * TOPK], F32, free_at)
        at_f = sb("at_f", [P, TILES * TOPK], F32, free_at)
        at_all = sb("at_all", [P, TILES, TOPK], I32, free_at)
        none_i = sb("none_i", [P, TOPK], I32, free_at)
        tick = sb("tick", [P, TOPK], I32, free_at)
        at_t = [sb(f"at_t{p}", [P, TOPK], I32, free_at) for p in range(2)]
        s_in = [sb(f"s_in{p}", [P, D], F32, free_at) for p in range(2)]
        sT = [parts(f"sT{p}", [P, DC, P], free_at) for p in range(2)]
        s_silu = [sb(f"s_silu{p}", [P, F], F32, free_at) for p in range(2)]
        s_hid = [sb(f"s_hid{p}", [P, EFW], F32, free_at) for p in range(2)]
        s_hT = [parts(f"s_hT{p}", [P, EFC, P], free_at) for p in range(2)]
        s_out = [sb(f"s_out{p}", [P, D], F32, free_at) for p in range(2)]
        silu = [sb(f"silu{p}", [P, FS], F32, free_at) for p in range(2)]
        hid = [sb(f"hid{p}", [P, FW], F32, free_at) for p in range(2)]
        hT = parts("hT", [P, FC, P], free_at)
        x1_in = [sb(f"x1_in{p}", [P, D], F32, free_at) for p in range(2)]
        routed = [[sb(f"routed{p}{j}", [P, D], F32, free_at) for j in range(TOPK)] for p in range(2)]
        mix = [sb(f"mix{j}", [P, D], F32, free_at) for j in range(TOPK)]
        o_out = [sb(f"o_out{p}", [P, D], F32, free_at) for p in range(2)]
        assert free_at[0] <= free_end, (free_at, free_end)

        trig = nc.dram_tensor("trig_scratch", (2, TILES, P, 2, HALF), F32, kind="Internal").ap()
        x1_dram = nc.dram_tensor("x1_scratch", (TILES, P, D), F32, kind="Internal").ap()
        yT_dram = nc.dram_tensor("yT_scratch", (TILES, P, 2 * D), F32, kind="Internal").ap()
        xs_dram = nc.dram_tensor("xs_scratch", (E * STRIDE, D), F32, kind="Internal").ap()
        ys_dram = nc.dram_tensor("ys_scratch", (SLOTS * P, D), F32, kind="Internal").ap()

        def bank(name):
            return ctx.enter_context(nc.psum_tensor(name, [P, 512], F32))

        b_q, b_kv, b_qT, b_kT, b_sc, b_pT, b_aT, b_o = [
            bank(n) for n in ("b_q", "b_kv", "b_qT", "b_kT", "b_sc", "b_pT", "b_aT", "b_o")]
        b_count = b_pT
        b_sg, b_shT, b_sT, b_sy = [b_q, b_kv], [b_qT, b_kT], [b_sc, b_pT], [b_aT, b_o]
        b_gate, b_up, b_hT, b_y = [b_q, b_kv], [b_qT, b_kT], b_sc, [b_aT, b_o]

        def sem(name):
            return ctx.enter_context(nc.semaphore(name))

        ld_pos, ld_const, ld_wq, ld_wkv, ld_w2 = map(sem, ("ld_pos", "ld_const", "ld_wq", "ld_wkv", "ld_w2"))
        ld_wo = [sem(f"ld_wo{n}") for n in range(2)]
        ld_x, ld_ctx, ld_trig, ld_res, ld_slot, ld_yT, ld_x1, ld_routed = [[sem(f"{n}{p}") for p in range(2)] for n in (
            "ld_x", "ld_ctx", "ld_trig", "ld_res", "ld_slot", "ld_yT", "ld_x1", "ld_routed")]
        ld_wr, st_yT, st_xs, st_pad = map(sem, ("ld_wr", "st_yT", "st_xs", "st_pad"))
        st_trig_first, st_trig = map(sem, ("st_trig_first", "st_trig"))
        st_x1, st_ys, st_out = [[sem(f"{n}{p}") for p in range(2)] for n in ("st_x1", "st_ys", "st_out")]
        consts_set, ident_done, pos_ready, wsin_ready, sin_ready, gates_ready = map(sem, (
            "consts_set", "ident_done", "pos_ready", "wsin_ready", "sin_ready", "gates_ready"))
        step_v, angle_v, step_p, angle_p = map(sem, ("step_v", "angle_v", "step_p", "angle_p"))
        abs_ready = sem("abs_ready")
        w_hi, w_lo, wo_lo = map(sem, ("w_hi", "w_lo", "wo_lo"))
        q_done, kv_done, qT_done, kT_done, sc_done, pT_done, aT_done, o_done, xT_done = map(sem, (
            "q_done", "kv_done", "qT_done", "kT_done", "sc_done", "pT_done", "aT_done", "o_done", "xT_done"))
        q_sq, k_sq, q_out, exp_done, pT_out, aT_hi, x_hi, ctx_hi = map(sem, (
            "q_sq", "k_sq", "q_out", "exp_done", "pT_out", "aT_hi", "x_hi", "ctx_hi"))
        (v_out, k_out, k_turned, q_turned, max_found, max_ready, inv_ready, aT_lo, stats_done, ln_var,
         x_normed, x_lo, ctx_lo, x1_ready) = map(sem, (
             "v_out", "k_out", "k_turned", "q_turned", "max_found", "max_ready", "inv_ready", "aT_lo",
             "stats_done", "ln_var", "x_normed", "x_lo", "ctx_lo", "x1_ready"))
        p_normed, p_normed2, me_done, r_ready, q_summed, q_ready, k_ready, ve_done, rstd_ready, \
            sin_w_ready = map(sem, (
                "p_normed", "p_normed2", "me_done", "r_ready", "q_summed", "q_ready", "k_ready",
                "ve_done", "rstd_ready", "sin_w_ready"))
        (wr_hi, wr_lo, below_set, below_cut, below_ready, stats2, var2, ve2_done, rstd2_ready, y_normed, yT_done, yT_hi,
         yT_lo, lg_done, lg_copied, top_found, lead_ready, idx_found, lead_done, top_copied, share_ready, pick_ready,
         w_ready, mask_ready, rk_done, rk_read, seen_ready, rank_ready, row_f_ready, row_ready) = map(sem, (
             "wr_hi", "wr_lo", "below_set", "below_cut", "below_ready", "stats2", "var2", "ve2_done", "rstd2_ready",
             "y_normed", "yT_done", "yT_hi", "yT_lo", "lg_done", "lg_copied", "top_found", "lead_ready", "idx_found",
             "lead_done", "top_copied", "share_ready", "pick_ready", "w_ready", "mask_ready", "rk_done", "rk_read",
             "seen_ready", "rank_ready", "row_f_ready", "row_ready"))
        (w2_hi, wg_lo_done, wd_lo_done, count_done, early_done, early_read, early_ready, table_step,
         table_ready, at_ready, s_pad_done) = map(
            sem, ("w2_hi", "wg_lo_done", "wd_lo_done", "count_done", "early_done", "early_read", "early_ready",
                  "table_step", "table_ready", "at_ready", "s_pad_done"))
        sT_done, sT_hi, sT_lo, sg_done, s_silu_done, s_hid_ready, shT_done, shT_hi, shT_lo, sy_done, s_out_ready = map(
            sem, ("sT_done", "sT_hi", "sT_lo", "sg_done", "s_silu_done", "s_hid_ready", "shT_done", "shT_hi", "shT_lo",
                  "sy_done", "s_out_ready"))
        (gu_done, silu_done, pad_done, hid_ready, hT_done, hT_hi, hT_lo, y_done, tick_done, at_t_ready, mix_step,
         out_ready) = map(sem, (
             "gu_done", "silu_done", "pad_done", "hid_ready", "hT_done", "hT_hi", "hT_lo", "y_done", "tick_done",
             "at_t_ready", "mix_step", "out_ready"))

        SPLITS, WO_SPLITS = 4 + 2, 4
        N_CONST = 11

        block = ctx.enter_context(nc.Block())

        def split_pieces():
            for c in range(4):
                yield tuple(w[:, :, 512 * c:512 * c + 512] for w in (wq_raw, *wq_s)) + (ld_wq,)
                if c == 0:
                    for d in range(DC):
                        yield tuple(w[:, d, :, :] for w in (wkv_raw, *wkv_s)) + (ld_wkv,)
            for c in range(4):
                yield tuple(w[:, 4 * c:4 * c + 4, :] for w in (wo_raw, *wo_s)) + (ld_wo[c // 2],)

        QUERY_SPLITS = (1, 4, 5, 6)
        KV_SPLITS = 3

        WG_PIECES = [(c, o) for o in range(2 * FS, GU, 2 * FS) for c in range(DC)] + [(c, 0) for c in range(DC)]
        WD_PIECES = [(o, o + 2 * EFC) for o in range(FC, DN, 2 * EFC)] + [(0, FC)]
        W2_ORDER = [("g", n) for n in range(4)]
        for n in range(len(WD_PIECES)):
            W2_ORDER += [("d", n)] + [("g", m) for m in range(4 + 2 * n, min(6 + 2 * n, len(WG_PIECES)))]

        def w2_piece(kind, n):
            if kind == "g":
                c, o = WG_PIECES[n]
                return tuple(w[:, c, o:o + 2 * FS] for w in (wg_raw, *wg_s))
            a, b = WD_PIECES[n]
            return tuple(w[:, a:b, :] for w in (wd_raw, *wd_s))

        def angle_steps(nce, chunks, spare, link, settle, done):
            shape = [P, CH, HALF]

            def each(step):
                for c in chunks:
                    link(step(c, sincos[c][:, :, 1, :], sincos[c][:, :, 0, :]), len(chunks))

            each(lambda c, a, turn: nce.tensor_tensor(
                a, pos_f[:, c * CH:(c + 1) * CH].unsqueeze(2).to_broadcast(shape),
                invf_s[:].unsqueeze(1).to_broadcast(shape), ALU.mult))
            each(lambda c, a, turn: nce.tensor_scalar(turn, a, 1 / (2 * np.pi), ROUND, ALU.mult, ALU.add))
            each(lambda c, a, turn: nce.tensor_scalar(turn, turn, 1.0, -ROUND, ALU.mult, ALU.add))
            for part in TWO_PI:
                if spare is None:
                    each(lambda c, a, turn: nce.scalar_tensor_tensor(out=a, in0=turn, scalar=-part, in1=a, op0=ALU.mult,
                                                                     op1=ALU.add))
                else:
                    each(lambda c, a, turn: nce.tensor_scalar(spare, turn, -part, 0.0, ALU.mult, ALU.add))
                    each(lambda c, a, turn: nce.tensor_tensor(a, a, spare, ALU.add))
            for n, c in enumerate(chunks):
                if n == 1:
                    settle()
                a = sincos[c][:, :, 1, :]
                nce.tensor_scalar(a, a, PI_BELOW, -PI_BELOW, ALU.min, ALU.max).then_inc(done, 1)

        CHUNKS_V = (0, X0, 1, X0 + 1, 3, X0 + 3)
        CHUNKS_P = (2, X0 + 2)

        @block.sync
        def _(sp):
            sp.dma_start(pos_i[:, 0:TILES], posc).then_inc(ld_pos, 16)
            sp.dma_start(pos_i[:, TILES:2 * TILES], posx).then_inc(ld_pos, 16)
            sp.dma_start(invf_s[:], invf).then_inc(ld_pos, 16)

            def load_inputs(t, p):
                need(sp, x_normed, t - 1)
                sp.dma_start(x_in[p][:], x[bass.ds(t, 1), :, :].rearrange("a p n -> p (a n)")).then_inc(ld_x[p], 16)
                need(sp, ctx_lo, t - 1)
                sp.dma_start(ctx_raw[p][:], ctxT[bass.ds(t, 1), :, :, :].rearrange("a p c n -> p (a c) n")) \
                  .then_inc(ld_ctx[p], 16)

            def load_trig(t, p):
                need(sp, sin_w_ready, t - 1)
                t_x = trig[1, bass.ds(t, 1), :, :, :].rearrange("a p c n -> p (a c n)")
                t_c = trig[0, bass.ds(t, 1), :, :, :].rearrange("a p c n -> p (a c n)")
                sp.dma_start(trig_raw[p][:, 0, :, :].rearrange("p c n -> p (c n)"), t_x).then_inc(ld_trig[p], 16)
                for b in range(NB):
                    first, second = (t_c, t_x) if b == 0 else (t_x, t_c)
                    sp.dma_start(trig_raw[p][0:S, 1 + b, :, :].rearrange("p c n -> p (c n)"),
                                 first[b * S:(b + 1) * S, :]).then_inc(ld_trig[p], 16)
                    sp.dma_start(trig_raw[p][S:P, 1 + b, :, :].rearrange("p c n -> p (c n)"),
                                 second[b * S:(b + 1) * S, :]).then_inc(ld_trig[p], 16)

            load_inputs(0, 0)
            sp.dma_start(wq_raw[:], wq).then_inc(ld_wq, 16)
            sp.dma_start(wkv_raw[:], wkv).then_inc(ld_wkv, 16)
            for n, w in ((0, q_w), (1, k_w), (2, k_w)):
                row = w.rearrange("(a n) -> a n", a=1)
                sp.dma_start(w_cos[:, n, :, :].rearrange("p a b -> p (a b)"),
                             row.to_broadcast([P, HD])).then_inc(ld_const, 16)
                sp.dma_start(w_sin[:, n, 0, :], row[:, HALF:HD].to_broadcast([P, HALF])).then_inc(ld_const, 16)
                sp.dma_start(w_sin[:, n, 1, :], row[:, 0:HALF].to_broadcast([P, HALF])).then_inc(ld_const, 16)
            for n, gate in enumerate((g_xattn, g_ffn)):
                sp.dma_start(gates_raw[:, n:n + 1], gate.rearrange("(a n) -> a n", a=1).to_broadcast([P, 1])) \
                  .then_inc(ld_const, 16)
            sp.dma_start(wr_raw[:], wr).then_inc(ld_wr, 16)
            sp.dma_start(wo_raw[:, 0:H // 2, :], wo[:, 0:H // 2, :]).then_inc(ld_wo[0], 16)

            def load_residual(t, p):
                need(sp, x1_ready, t - 1)
                sp.dma_start(x_res[p][:], x[bass.ds(t, 1), :, :].rearrange("a p n -> p (a n)")).then_inc(ld_res[p], 16)

            def store_x1(t, p):
                need(sp, x1_ready, t + 1)
                sp.dma_start(x1_dram[bass.ds(t, 1), :, :].rearrange("a p n -> p (a n)"), x1_out[p][:]) \
                  .then_inc(st_x1[p], 16)

            def store_yT(t, p):
                need(sp, yT_lo, t + 1)
                sp.dma_start(yT_dram[bass.ds(t, 1), :, :].rearrange("a p n -> p (a n)"),
                             yT_both[p][:].rearrange("p a c n -> p (a c n)").bitcast(F32)).then_inc(st_yT, 16)

            sp.wait_ge(st_trig_first, 16 * 2)
            load_trig(0, 0)
            load_inputs(1, 1)
            sp.dma_start(wo_raw[:, H // 2:H, :], wo[:, H // 2:H, :]).then_inc(ld_wo[1], 16)

            def pair(i, first, last):
                for p in range(2):
                    t = 2 * i + p
                    if not (last and p == 1):
                        if not (first and p == 0):
                            load_inputs(t + 1, 1 - p)
                        load_trig(t + 1, 1 - p)
                    load_residual(t, p)
                    if isinstance(i, int) and i == 1:
                        w, raw = ((wg, wg_raw), (wd, wd_raw))[p]
                        sp.dma_start(raw[:], w).then_inc(ld_w2, 16)
                    if not (first and p == 0):
                        store_x1(t - 1, 1 - p)
                        store_yT(t - 1, 1 - p)
                if first:
                    sp.wait_ge(w_lo, SPLITS)
                    sp.wait_ge(wo_lo, WO_SPLITS)
                    sp.wait_ge(st_trig, 16 * (NCH - 2))

            walk(sp, pair, start=2)

            sp.wait_ge(early_ready, 1)
            sp.wait_ge(st_xs, 16 * TOPK * (TILES - PAD_TILES))
            for e in range(E):
                n_e = sp.value_load(first_pad[0:1, e:e + 1], min_val=0, max_val=(TILES - PAD_TILES) * P)
                sp.dma_start(xs_dram[bass.ds(n_e + e * STRIDE, PAD), :].rearrange("(a p) n -> p a n", p=P),
                             zeros[:].unsqueeze(1).to_broadcast([P, PAD // P, D])).then_inc(st_pad, 16)

            store_x1(TILES - 1, 1)
            store_yT(TILES - 1, 1)

            sp.wait_ge(table_ready, 1)
            sp.wait_ge(st_xs, 16 * TOPK * TILES)

            def load_slot(m, p):
                row = sp.value_load(slot_row[0:1, bass.ds(m, 1)], min_val=0, max_val=E * STRIDE - P)
                need(sp, sT_done, m - 1)
                sp.dma_start(s_in[p][:], xs_dram[bass.ds(row, P), :]).then_inc(ld_slot[p], 16)

            load_slot(0, 0)
            load_slot(1, 1)

            def slots(i, first, last):
                for p in range(2):
                    m = 2 * i + p
                    if not last:
                        load_slot(m + 2, p)

            walk(sp, slots, TURNS, start=2)
            for p in range(2):
                sp.wait_ge(st_x1[p], 16 * PAIRS)
            
            def load_x1(t, p):
                need(sp, out_ready, t - 1)
                sp.dma_start(x1_in[p][:], x1_dram[bass.ds(t, 1), :, :].rearrange("a p n -> p (a n)")) \
                  .then_inc(ld_x1[p], 16)

            def store_out(t, p):
                need(sp, out_ready, t + 1)
                sp.dma_start(out[bass.ds(t, 1), :, :].rearrange("a p n -> p (a n)"), o_out[p][:]) \
                  .then_inc(st_out[p], 16)

            def pair3(i, first, last):
                for p in range(2):
                    t = 2 * i + p
                    load_x1(t, p)
                    if not first:
                        store_out(t - 2, p)

            walk(sp, pair3, start=2)
            for p in range(2):
                store_out(TILES - 2 + p, p)
            for p in range(2):
                sp.wait_ge(st_out[p], 16 * PAIRS)

        @block.gpsimd
        def _(pool):
            nc.gpsimd.memset(ident[:], 0.0).then_inc(consts_set, 1)
            nc.gpsimd.memset(minus_half[:], -0.5).then_inc(consts_set, 1)
            nc.gpsimd.memset(eps_rms[:], RMS_EPS).then_inc(consts_set, 1)
            nc.gpsimd.memset(eps_ln[:], LN_EPS).then_inc(consts_set, 1)
            nc.gpsimd.memset(half_pi[:], np.pi / 2).then_inc(consts_set, 1)
            nc.gpsimd.iota(expert_no[:], pattern=[[1, E]], base=0, channel_multiplier=0,
                           allow_small_or_imprecise_dtypes=True).then_inc(consts_set, 1)
            pool.wait_ge(consts_set, 6)
            nc.gpsimd.affine_select(out=ident[:], in_=ident[:], compare_op=ALU.not_equal, fill=1.0, base=0,
                                    pattern=[[-1, P]], channel_multiplier=1).then_inc(ident_done, 1)
            steps = [0]

            def link(ins, chunks):
                steps[0] += 1
                ins.then_inc(step_p, 1)
                pool.wait_ge(step_p, steps[0])

            def angles(c):
                angle_steps(nc.gpsimd, (c,), turn_p[:], link, None, angle_p)

            def cos_table(i, p):
                pool.wait_ge(ld_trig[p], 80 * (i + 1))
                nc.gpsimd.tensor_tensor(cos_w[p][:], trig_raw[p][:, :, 0:1, :].to_broadcast([P, 3, 2, HALF]), w_cos[:],
                                        ALU.mult)

            def sin_table(p):
                nc.gpsimd.tensor_tensor(sin_w[p][:], trig_raw[p][:, :, 1:2, :].to_broadcast([P, 3, 2, HALF]), w_sin[:],
                                        ALU.mult).then_inc(sin_w_ready, 1)

            def layer_rstd(t, p):
                need(pool, ln_var, t + 1)
                nc.gpsimd.tensor_tensor(ln_ve[:, p:p + 1], ln_mv[:, p, 1:2], eps_ln[:], ALU.add).then_inc(ve_done, 1)
                need(pool, ve_done, t + 1)
                nc.gpsimd.tensor_tensor(ln_rstd[:, p:p + 1], ln_ve[:, p:p + 1], minus_half[:, 0:1], ALU.pow) \
                  .then_inc(rstd_ready, 1)

            def scales(n, g):
                need(pool, q_sq, n + 1)
                need(pool, k_sq, n + 1)
                nc.gpsimd.tensor_tensor(qk_me[:], qk_ms[g % 2][:], eps_rms[:, 0:REP + NB], ALU.add).then_inc(me_done, 1)
                need(pool, me_done, n + 1)
                nc.gpsimd.tensor_tensor(qk_r[g % 2][:], qk_me[:], minus_half[:, 0:REP + NB], ALU.pow).then_inc(r_ready, 1)

            def query_sum(n, g):
                need(pool, q_turned, n + 1)
                nc.gpsimd.tensor_tensor(q_rot[g % 2][:], q_rot[g % 2][:], q_sin[g % 2][:], ALU.add) \
                  .then_inc(q_summed, 1)
                need(pool, q_summed, n + 1)
                nc.gpsimd.tensor_tensor(q_rot[g % 2][:], q_rot[g % 2][:],
                                        qk_r[g % 2][:, 0:REP].unsqueeze(2).to_broadcast([P, REP, HD]), ALU.mult) \
                  .then_inc(q_ready, 1)

            def key_sum(n, g):
                need(pool, k_turned, n + 1)
                nc.gpsimd.tensor_tensor(k_rot[g % 2][:], k_rot[g % 2][:], k_sin[g % 2][:], ALU.add) \
                  .then_inc(k_ready, 1)

            def layer_rstd2(t):
                need(pool, var2, t + 1)
                nc.gpsimd.tensor_tensor(ln2_ve[:], ln2_mv[:, 1:2], eps_ln[:], ALU.add).then_inc(ve2_done, 1)
                need(pool, ve2_done, t + 1)
                nc.gpsimd.tensor_tensor(ln2_rstd[:], ln2_ve[:], minus_half[:, 0:1], ALU.pow).then_inc(rstd2_ready, 1)


            def scatter(t, p, j):
                nc.gpsimd.indirect_dma_start(out=xs_dram[:, :],
                                             out_offset=bass.IndirectOffsetOnAxis(ap=row_i[p][:, j:j + 1], axis=0),
                                             in_=y_n[p][:], in_offset=None).then_inc(st_xs, 16)

            layer_rstd(0, 0)
            pool.wait_ge(pos_ready, 1)
            for c in CHUNKS_P[:2]:
                angles(c)
            pool.wait_ge(wsin_ready, 1)
            cos_table(0, 0)
            sin_table(0)
            def wo_lo_part(n):
                raw, hi, lo, loaded = list(split_pieces())[n]
                pool.wait_ge(w_hi, n + 1)
                nc.gpsimd.tensor_tensor(lo, raw, hi.bitcast(F32), ALU.subtract).then_inc(wo_lo, 1)

            wo_lo_part(SPLITS)
            scales(0, 0)
            query_sum(0, 0)
            wo_lo_part(SPLITS + 1)
            key_sum(0, 0)

            def pair(i, first, last):
                for u in range(2 * KVH):
                    p, g = divmod(u, KVH)
                    t, n = 2 * i + p, 8 * i + u
                    end = last and p == 1
                    if not (end and g == 3):
                        scales(n + 1, g + 1)
                        query_sum(n + 1, g + 1)
                        if g == 1 and not first:
                            need(pool, row_ready, t - 1)
                        if g == 2 and not first:
                            need(pool, st_xs, 32 * (t - 2) + 16)
                        if g == 3 and not first:
                            need(pool, st_xs, 32 * (t - 1))
                        key_sum(n + 1, g + 1)
                    if g in (1, 2) and not first:
                        scatter(t - 2, p, g - 1)
                    if g == 0 and not end:
                        cos_table(i + p, 1 - p)
                        layer_rstd(t + 1, 1 - p)
                    if g == 2 and not end:
                        sin_table(1 - p)
                    if g == 1 and not (first and p == 0):
                        layer_rstd2(t - 1)
                    if first and u == KVH:
                        pool.wait_ge(below_set, 1)
                        nc.gpsimd.affine_select(out=below_f[:], in_=below_f[:], compare_op=ALU.is_gt, fill=0.0, base=0,
                                                pattern=[[1, P]], channel_multiplier=-1).then_inc(below_cut, 1)
                        nc.gpsimd.iota(slot_no[:], pattern=[[1, SLOTS]], base=0, channel_multiplier=0,
                                       allow_small_or_imprecise_dtypes=True).then_inc(below_cut, 1)

            walk(pool, pair)

            def down_lo(n):
                pool.wait_ge(w2_hi, W2_ORDER.index(("d", n)) + 1)
                raw, hi, lo = w2_piece("d", n)
                nc.gpsimd.tensor_tensor(lo, raw, hi.bitcast(F32), ALU.subtract).then_inc(wd_lo_done, 1)

            pool.wait_ge(st_xs, 16 * TOPK * (TILES - 2))
            pool.wait_ge(st_pad, 16 * E)
            pool.wait_ge(row_ready, TILES - 1)
            scatter(TILES - 2, 0, 0)
            layer_rstd2(TILES - 1)
            pool.wait_ge(st_xs, 16 * (TOPK * (TILES - 2) + 1))
            scatter(TILES - 2, 0, 1)
            for n in range(2):
                down_lo(n)
            pool.wait_ge(st_xs, 16 * TOPK * (TILES - 1))
            pool.wait_ge(row_ready, TILES)
            scatter(TILES - 1, 1, 0)
            down_lo(2)
            pool.wait_ge(st_xs, 16 * (TOPK * (TILES - 1) + 1))
            scatter(TILES - 1, 1, 1)
            for n in range(3, len(WD_PIECES)):
                down_lo(n)

            nc.gpsimd.iota(none_i[:], pattern=[[0, TOPK]], base=0, channel_multiplier=0).then_inc(tick_done, 1)
            pool.wait_ge(at_ready, 1)
            for p in range(2):
                pool.wait_ge(st_ys[p], 16 * TURNS)

            def gather(t, p):
                need(pool, tick_done, 2 * t + 1)
                need(pool, mix_step, 2 * (t - 1))
                nc.gpsimd.tensor_tensor(tick[:], none_i[:], none_i[:], ALU.add).then_inc(tick_done, 1)
                nc.gpsimd.tensor_tensor(at_t[p][:], at_all[:, bass.ds(t, 1), :].rearrange("p a j -> p (a j)"), none_i[:],
                                        ALU.add).then_inc(at_t_ready, 1)
                need(pool, tick_done, 2 * t + 2)
                need(pool, at_t_ready, t + 1)
                nc.gpsimd.tensor_tensor(tick[:], none_i[:], none_i[:], ALU.add).then_inc(tick_done, 1)
                for j in range(TOPK):
                    nc.gpsimd.indirect_dma_start(out=routed[p][j][:], out_offset=None, in_=ys_dram[:, :],
                                                 in_offset=bass.IndirectOffsetOnAxis(ap=at_t[p][:, j:j + 1], axis=0)) \
                      .then_inc(ld_routed[p], 16)

            def pair3(i, first, last):
                for p in range(2):
                    gather(2 * i + p, p)

            walk(pool, pair3, start=2)

        @block.scalar
        def _(act):
            act.wait_ge(consts_set, 6)
            nc.scalar.activation(gates[:, 0:1], half_pi[:], ACT.Sin)
            turns = [0]

            def tables(c):
                if c in CHUNKS_V:
                    act.wait_ge(angle_v, CHUNKS_V.index(c) + 1)
                else:
                    act.wait_ge(angle_p, CHUNKS_P.index(c) + 1)
                turns[0] += 1
                cos, sin = sincos[c][:, :, 0, :], sincos[c][:, :, 1, :]
                nc.scalar.activation(cos, sin, ACT.Abs).then_inc(abs_ready, 1)
                nc.scalar.activation(sin, sin, ACT.Sin)
                act.wait_ge(abs_ready, turns[0])
                nc.scalar.activation(cos, cos, ACT.Sin, bias=half_pi[:], scale=-1.0).then_inc(sin_ready, 1)
                act.wait_ge(sin_ready, turns[0])
                src, t0 = divmod(c * CH, TILES)
                act.dma_start(trig[src, t0:t0 + CH, :, :, :].rearrange("t p c n -> p t (c n)"),
                              sincos[c][:].rearrange("p t c n -> p t (c n)")) \
                   .then_inc(st_trig_first if c in (0, X0) else st_trig, 16)

            pieces = list(split_pieces())

            def split_hi(some):
                for raw, hi, lo, loaded in some:
                    act.wait_ge(loaded, 16)
                    nc.scalar.activation(hi, raw, ACT.Copy).then_inc(w_hi, 1)

            def key_squares(n, g):
                need(act, kv_done, n + 1)
                kv = b_kv[:].rearrange("p (b w n) -> p b w n", b=NB, w=2)
                nc.scalar.activation(v_s[g % KVH][:], kv[:, :, 1, :], ACT.Copy).then_inc(v_out, 1)
                for b in range(NB):
                    last = nc.scalar.activation(junk[:, REP + b, :], kv[:, b, 0, :], ACT.Square, scale=HD ** -0.5,
                                                accum_out=qk_ms[g % 2][:, REP + b:REP + b + 1])
                last.then_inc(k_sq, 1)

            def query_squares(n, g):
                need(act, q_done, n + 1)
                for h in range(REP):
                    last = nc.scalar.activation(junk[:, h, :], b_q[:, h * HD:(h + 1) * HD], ACT.Square, scale=HD ** -0.5,
                                                accum_out=qk_ms[g % 2][:, h:h + 1])
                last.then_inc(q_sq, 1)

            def queries_out(n, g):
                need(act, qT_done, n + 1)
                nc.scalar.activation(qT[:].rearrange("p b h s -> p h b s"),
                                     b_qT[:].rearrange("p (h b s) -> p h b s", h=REP, b=NB), ACT.Copy).then_inc(q_out, 1)

            def probs_out(n, g):
                need(act, pT_done, n + 1)
                nc.scalar.activation(pT[:].rearrange("p b n -> p (b n)"), b_pT[:], ACT.Copy).then_inc(pT_out, 1)

            def exponentials(n, g):
                need(act, pT_done, n)
                need(act, max_ready, n + 1)
                for j in range(REP):
                    last = nc.scalar.activation(probs[:, j, :], b_sc[:, j * P:(j + 1) * P], ACT.Exp,
                                                bias=neg_max[g % 2][:, j:j + 1], scale=SCALE,
                                                accum_out=row_sum[g % 2][:, j:j + 1])
                last.then_inc(exp_done, 1)

            def normalize_first(n, g):
                need(act, inv_ready, n + 1)
                nc.scalar.activation(probs[:, 0, :], probs[:, 0, :], ACT.Copy, scale=row_inv[g % 2][:, 0:1]) \
                  .then_inc(p_normed, 1)

            def attended_hi(n, g):
                need(act, aT_done, n + 1)
                nc.scalar.activation(aT[HI][:].rearrange("p h b s -> p b h s"),
                                     b_aT[:].rearrange("p (b h s) -> p b h s", b=NB, h=REP), ACT.Copy) \
                  .then_inc(aT_hi, 1)

            def context_hi(t, i, p):
                act.wait_ge(ld_ctx[p], 16 * (i + 1))
                nc.scalar.activation(kv_in[p][HI][:, :, 0::3, :], ctx_raw[p][:].rearrange("p c (b s) -> p c b s", b=NB),
                                     ACT.Copy).then_inc(ctx_hi, 1)

            def normed_hi(t, p):
                need(act, xT_done, t + 1)
                nc.scalar.activation(kv_in[p][HI][:, :, 1:3, :],
                                     b_kT[:, DC * P:2 * DC * P].rearrange("p (c b s) -> p c b s", c=DC, b=NB), ACT.Copy) \
                  .then_inc(x_hi, 1)

            def split2_hi(count):
                for name in [next(pieces2) for _ in range(count)]:
                    raw, hi, lo = w2_piece(*name)
                    nc.scalar.activation(hi, raw, ACT.Copy).then_inc(w2_hi, 1)

            pieces2 = iter(W2_ORDER)

            def tokens_hi(t, p):
                need(act, yT_done, t + 1)
                need(act, st_yT, 16 * t)
                nc.scalar.activation(yT[p][HI][:].rearrange("p c n -> p (c n)"), b_kT[:, D:2 * D], ACT.Copy) \
                  .then_inc(yT_hi, 1)

            def lead_tanh(t):
                need(act, lead_ready, t + 1)
                nc.scalar.activation(lead_t[:], lead[:], ACT.Tanh, scale=0.5).then_inc(lead_done, 1)

            split_hi(pieces[0:1])
            tables(0)
            context_hi(0, 0, 0)
            tables(X0)
            split_hi(pieces[1:3])
            normed_hi(0, 0)
            split_hi(pieces[3:6])
            tables(2)
            tables(1)
            split_hi(pieces[6:7])
            query_squares(0, 0)
            split_hi(pieces[7:8])
            key_squares(0, 0)
            tables(X0 + 1)
            tables(X0 + 2)
            split_hi(pieces[8:9])
            query_squares(1, 1)
            tables(3)
            tables(X0 + 3)
            act.wait_ge(ld_wr, 16)
            nc.scalar.activation(wr_s[HI][:], wr_raw[:], ACT.Copy).then_inc(wr_hi, 1)
            act.wait_ge(ld_const, 16 * N_CONST)
            nc.scalar.activation(gates[:], gates_raw[:], ACT.Tanh).then_inc(gates_ready, 1)
            act.wait_ge(gates_ready, 1)
            nc.scalar.activation(gates_raw[:, 0:1], gates[:, 0:1], ACT.Exp)

            def pair(i, first, last):
                for u in range(2 * KVH):
                    p, g = divmod(u, KVH)
                    t, n = 2 * i + p, 8 * i + u
                    end = last and p == 1
                    queries_out(n, g)
                    if not (end and g == 3):
                        key_squares(n + 1, g + 1)
                    if end and g == 3:
                        split2_hi(2)
                    if g == 0 and not end:
                        context_hi(t + 1, i + p, 1 - p)
                    if g == 1 and not end:
                        normed_hi(t + 1, 1 - p)
                    if g == 2 and not (first and p == 0):
                        tokens_hi(t - 1, 1 - p)
                    if not (first and u == 0):
                        probs_out(n - 1, g - 1)
                    exponentials(n, g)
                    if not (first and u == 0):
                        attended_hi(n - 1, g - 1)
                    normalize_first(n, g)
                    if first and u == 0:
                        split_hi(pieces[9:10])
                    if not (end and g >= 2):
                        query_squares(n + 2, g)
                    if g == 3 and not (first and p == 0):
                        lead_tanh(t - 1)
                    if end and g == 2:
                        act.wait_ge(ld_w2, 32)
                        split2_hi(2)

            walk(act, pair)
            probs_out(4 * TILES - 1, 3)
            split2_hi(1)
            attended_hi(4 * TILES - 1, 3)
            split2_hi(3)
            tokens_hi(TILES - 1, 1)
            split2_hi(2)
            lead_tanh(TILES - 1)
            split2_hi(len(W2_ORDER) - 10)
            nc.scalar.activation(gates_raw[:, 0:1], gates[:, 0:1], ACT.Silu)

            def load_yT(t, p):
                act.dma_start(yT_both[p][:].rearrange("p a c n -> p (a c n)").bitcast(F32),
                              yT_dram[bass.ds(t, 1), :, :].rearrange("a p n -> p (a n)")).then_inc(ld_yT[p], 16)

            def slot_hi(m, p):
                need(act, sT_done, m + 1)
                nc.scalar.activation(sT[p][HI][:].rearrange("p c n -> p (c n)"), b_sT[p][:, 0:D], ACT.Copy) \
                  .then_inc(sT_hi, 1)

            def slot_silu(m, p):
                need(act, sg_done, m + 1)
                nc.scalar.activation(s_silu[p][:], b_sg[p][:, 0:F], ACT.Silu).then_inc(s_silu_done, 1)

            def slot_hidden_hi(m, p):
                need(act, shT_done, m + 1)
                nc.scalar.activation(s_hT[p][HI][:].rearrange("p c n -> p (c n)"), b_shT[p][:, 0:EFW], ACT.Copy) \
                  .then_inc(shT_hi, 1)

            def slot_out(m, i, p):
                if not isinstance(i, int) or i >= 1:
                    act.wait_ge(st_ys[p], 16 * i)
                need(act, sy_done, m + 1)
                nc.scalar.activation(s_out[p][:], b_sy[p][:, 0:D], ACT.Copy).then_inc(s_out_ready, 1)
                need(act, s_out_ready, m + 1)
                act.dma_start(ys_dram[bass.ds(m * P, P), :], s_out[p][:]).then_inc(st_ys[p], 16)

            slot_hi(0, 0)
            slot_hi(1, 1)
            act.wait_ge(st_yT, 16 * TILES)
            for p in range(2):
                load_yT(p, p)

            def slots(i, first, last):
                for p in range(2):
                    m = 2 * i + p
                    slot_silu(m, p)
                    if not (first and p == 0):
                        slot_hidden_hi(m - 1, 1 - p)
                    if not last:
                        slot_hi(m + 2, p)
                    if not first:
                        slot_out(m - 2, i - 1, p)

            walk(act, slots, TURNS, start=2)
            slot_hidden_hi(SLOTS - 1, 1)
            slot_out(SLOTS - 2, TURNS - 1, 0)

            def silu_gate(t, p):
                need(act, gu_done, t + 1)
                nc.scalar.activation(silu[p][:], b_gate[p][:, 0:FS], ACT.Silu).then_inc(silu_done, 1)

            def hidden_hi(t):
                need(act, hT_done, t + 1)
                nc.scalar.activation(hT[HI][:].rearrange("p c n -> p (c n)"), b_hT[:, 0:FW], ACT.Copy) \
                  .then_inc(hT_hi, 1)

            def pair3(i, first, last):
                for p in range(2):
                    t = 2 * i + p
                    silu_gate(t, p)
                    if not last:
                        load_yT(t + 2, p)
                    if first and p == 0:
                        slot_out(SLOTS - 1, TURNS - 1, 1)
                    if not (first and p == 0):
                        hidden_hi(t - 1)

            walk(act, pair3, start=2)
            hidden_hi(TILES - 1)

        @block.vector
        def _(dve):
            dve.wait_ge(ld_pos, 48)
            nc.vector.tensor_copy(pos_f[:], pos_i[:]).then_inc(pos_ready, 1)
            dve.wait_ge(pos_ready, 1)
            steps = [0]

            def link(ins, chunks):
                steps[0] += 1
                ins.then_inc(step_v, 1)
                dve.wait_ge(step_v, steps[0] - chunks + 1)

            def settle():
                dve.wait_ge(step_v, steps[0])

            def angles(*chunks):
                angle_steps(nc.vector, chunks, None, link, settle, angle_v)

            pieces = list(enumerate(split_pieces()))

            def split_lo(some):
                for n, (raw, hi, lo, loaded) in some:
                    dve.wait_ge(w_hi, n + 1)
                    nc.vector.tensor_tensor(lo, raw, hi.bitcast(F32), ALU.subtract) \
                      .then_inc(w_lo if n < SPLITS else wo_lo, 1)

            def layer_stats(t, i, p):
                dve.wait_ge(ld_x[p], 16 * (i + 1))
                nc.vector.bn_stats(ln_stats[:], x_in[p][:]).then_inc(stats_done, 1)

            def layer_var(p):
                nc.vector.bn_aggr(ln_mv[:, p, :], ln_stats[:]).then_inc(ln_var, 1)

            def normalize_x(t, p):
                need(dve, rstd_ready, t + 1)
                nc.vector.tensor_scalar(x_n[:], x_in[p][:], ln_mv[:, p, 0:1], ln_rstd[:, p:p + 1], ALU.subtract,
                                        ALU.mult).then_inc(x_normed, 1)

            def context_lo(t, p):
                need(dve, ctx_hi, t + 1)
                nc.vector.tensor_tensor(kv_in[p][LO][:, :, 0::3, :], ctx_raw[p][:].rearrange("p c (b s) -> p c b s", b=NB),
                                        kv_in[p][HI][:, :, 0::3, :].bitcast(F32), ALU.subtract).then_inc(ctx_lo, 1)

            def normed_lo(t, p):
                need(dve, x_hi, t + 1)
                nc.vector.tensor_tensor(kv_in[p][LO][:, :, 1:3, :],
                                        b_kT[:, DC * P:2 * DC * P].rearrange("p (c b s) -> p c b s", c=DC, b=NB),
                                        kv_in[p][HI][:, :, 1:3, :].bitcast(F32), ALU.subtract).then_inc(x_lo, 1)

            def turn_keys(n, g, p):
                need(dve, r_ready, n + 1)
                kv = b_kv[:].rearrange("p (b w h n) -> p b w h n", b=NB, w=2, h=2)
                for b in range(NB):
                    r = qk_r[g % 2][:, REP + b:REP + b + 1]
                    k3 = "p (h n) -> p h n"
                    nc.vector.scalar_tensor_tensor(out=k_rot[g % 2][:, b, :].rearrange(k3, h=2), in0=kv[:, b, 0, :, :],
                                                   scalar=r, in1=cos_w[p][:, 1 + b, :, :], op0=ALU.mult, op1=ALU.mult)
                    last = nc.vector.scalar_tensor_tensor(out=k_sin[g % 2][:, b, :].rearrange(k3, h=2),
                                                          in0=kv[:, b, 0, ::-1, :], scalar=r,
                                                          in1=sin_w[p][:, 1 + b, :, :], op0=ALU.mult, op1=ALU.mult)
                last.then_inc(k_turned, 1)

            def turn_queries(n, g, t, p):
                need(dve, q_sq, n + 1)
                if g % KVH == 0:
                    need(dve, sin_w_ready, t + 1)
                q = b_q[:].rearrange("p (h a n) -> p h a n", h=REP, a=2)
                q4 = "p h (a n) -> p h a n"
                shape = [P, REP, 2, HALF]
                nc.vector.tensor_tensor(q_rot[g % 2][:].rearrange(q4, a=2), q,
                                        cos_w[p][:, 0, :, :].unsqueeze(1).to_broadcast(shape), ALU.mult)
                nc.vector.tensor_tensor(q_sin[g % 2][:].rearrange(q4, a=2), q[:, :, ::-1, :],
                                        sin_w[p][:, 0, :, :].unsqueeze(1).to_broadcast(shape), ALU.mult) \
                  .then_inc(q_turned, 1)

            def keys_out(n, g):
                need(dve, kT_done, n + 1)
                nc.vector.tensor_copy(kT[:].rearrange("p b n -> p (b n)"), b_kT[:, 0:NB * P]).then_inc(k_out, 1)

            def score_max(n, g):
                need(dve, sc_done, n + 1)
                nc.vector.tensor_reduce(row_max[:], b_sc[:].rearrange("p (j n) -> p j n", j=REP), AX.X, ALU.max) \
                  .then_inc(max_found, 1)
                need(dve, max_found, n + 1)
                nc.vector.tensor_scalar(neg_max[g % 2][:], row_max[:], -SCALE, None, ALU.mult).then_inc(max_ready, 1)

            def sum_inverse(n, g):
                need(dve, exp_done, n + 1)
                nc.vector.reciprocal(row_inv[g % 2][:], row_sum[g % 2][:]).then_inc(inv_ready, 1)
                need(dve, inv_ready, n + 1)
                nc.vector.tensor_tensor(probs[:, 1:REP, :], probs[:, 1:REP, :],
                                        row_inv[g % 2][:, 1:REP].unsqueeze(2).to_broadcast([P, REP - 1, P]),
                                        ALU.mult).then_inc(p_normed2, 1)

            def attended_lo(n, g):
                need(dve, aT_hi, n + 1)
                nc.vector.tensor_tensor(aT[LO][:].rearrange("p h b s -> p b h s"),
                                        b_aT[:].rearrange("p (b h s) -> p b h s", b=NB, h=REP),
                                        aT[HI][:].bitcast(F32).rearrange("p h b s -> p b h s"), ALU.subtract) \
                  .then_inc(aT_lo, 1)

            def residual(t, i, p):
                if not isinstance(i, int) or i >= 1:
                    dve.wait_ge(st_x1[p], 16 * i)
                dve.wait_ge(ld_res[p], 16 * (i + 1))
                need(dve, o_done, KVH * (t + 1))
                nc.vector.scalar_tensor_tensor(out=x1_out[p][:], in0=b_o[:, 0:D], scalar=gates[:, 0:1],
                                               in1=x_res[p][:], op0=ALU.mult, op1=ALU.add).then_inc(x1_ready, 1)

            def layer_stats2(t, p):
                need(dve, x1_ready, t + 1)
                nc.vector.bn_stats(ln2_stats[:], x1_out[p][:]).then_inc(stats2, 1)

            def layer_var2():
                nc.vector.bn_aggr(ln2_mv[:], ln2_stats[:]).then_inc(var2, 1)

            def normalize_y(t, p):
                need(dve, rstd2_ready, t + 1)
                nc.vector.tensor_scalar(y_n[p][:], x1_out[p][:], ln2_mv[:, 0:1], ln2_rstd[:], ALU.subtract,
                                        ALU.mult).then_inc(y_normed, 1)

            def tokens_lo(t, p):
                need(dve, yT_hi, t + 1)
                nc.vector.tensor_tensor(yT[p][LO][:].rearrange("p c n -> p (c n)"), b_kT[:, D:2 * D],
                                        yT[p][HI][:].rearrange("p c n -> p (c n)").bitcast(F32), ALU.subtract) \
                  .then_inc(yT_lo, 1)

            def copy_logits(t):
                need(dve, lg_done, t + 1)
                nc.vector.tensor_reduce(logits[:], b_kT[:, D:D + 2 * E].rearrange("p (a e) -> p e a", a=2), AX.X,
                                        ALU.add).then_inc(lg_copied, 1)

            def top_two(t):
                nc.vector.max(top_v[:], logits[:]).then_inc(top_found, 1)
                need(dve, top_found, t + 1)
                nc.vector.tensor_tensor(lead[:], top_v[:, 0:1], top_v[:, 1:2], ALU.subtract).then_inc(lead_ready, 1)
                nc.vector.max_index(top_i[:], top_v[:], logits[:]).then_inc(idx_found, 1)

            def of_tile(a, t):
                return a[:, bass.ds(t, 1), :].rearrange("p a j -> p (a j)")

            def weights_and_mask(t):
                need(dve, idx_found, t + 1)
                nc.vector.tensor_copy(top_f[:], top_i[:, 0:TOPK]).then_inc(top_copied, 1)
                nc.vector.tensor_copy(of_tile(e_all, t), top_i[:, 0:TOPK])
                need(dve, lead_done, t + 1)
                nc.vector.tensor_scalar(share[:, 0:1], lead_t[:], ROUTED_SCALE / 2, ROUTED_SCALE / 2, ALU.mult, ALU.add)
                nc.vector.tensor_scalar(share[:, 1:2], lead_t[:], -ROUTED_SCALE / 2, ROUTED_SCALE / 2, ALU.mult,
                                        ALU.add).then_inc(share_ready, 1)
                need(dve, top_copied, t + 1)
                for n in range(TOPK):
                    last = nc.vector.tensor_scalar(pick[:, n, :], expert_no[:], top_f[:, n:n + 1], None, ALU.is_equal)
                last.then_inc(pick_ready, 1)
                need(dve, share_ready, t + 1)
                nc.vector.tensor_scalar(of_tile(w_all, t), share[:], gates[:, 1:2], None, ALU.mult).then_inc(w_ready, 1)
                need(dve, pick_ready, t + 1)
                nc.vector.tensor_tensor(mask[:], pick[:, 0, :], pick[:, 1, :], ALU.add).then_inc(mask_ready, 1)

            def rows_of_tokens(t, p):
                need(dve, rk_read, t + 1)
                nc.vector.tensor_reduce(rank[:], ranked[:], AX.X, ALU.add).then_inc(rank_ready, 1)
                need(dve, rank_ready, t + 1)
                nc.vector.scalar_tensor_tensor(out=row_f[:], in0=top_f[:], scalar=float(STRIDE), in1=rank[:], op0=ALU.mult,
                                               op1=ALU.add).then_inc(row_f_ready, 1)
                nc.vector.tensor_copy(of_tile(rank_all, t), rank[:])
                need(dve, row_f_ready, t + 1)
                nc.vector.tensor_copy(row_i[p][:], row_f[:]).then_inc(row_ready, 1)

            def read_ranks(t):
                need(dve, rk_done, t + 1)
                nc.vector.tensor_tensor(ranked[:], pick[:], b_kT[:, D:D + E].unsqueeze(1).to_broadcast([P, TOPK, E]),
                                        ALU.mult).then_inc(rk_read, 1)
                nc.vector.tensor_tensor(seen[:], seen[:].bitcast(F32), mask[:].bitcast(F32), ALU.add) \
                  .then_inc(seen_ready, 1)

            pieces2 = iter([name for name in W2_ORDER if name[0] == "g"])

            def split2_lo(count):
                for name in [next(pieces2) for _ in range(count)]:
                    raw, hi, lo = w2_piece(*name)
                    dve.wait_ge(w2_hi, W2_ORDER.index(name) + 1)
                    nc.vector.tensor_tensor(lo, raw, hi.bitcast(F32), ALU.subtract).then_inc(wg_lo_done, 1)

            layer_stats(0, 0, 0)
            dve.wait_ge(stats_done, 1)
            layer_var(0)
            normalize_x(0, 0)
            angles(0, X0)
            split_lo(pieces[0:1])
            context_lo(0, 0)
            angles(1, X0 + 1)
            split_lo(pieces[1:3])
            normed_lo(0, 0)
            split_lo(pieces[3:4])
            dve.wait_ge(ld_const, 16 * N_CONST)
            nc.vector.tensor_scalar(w_sin[:, :, 0, :], w_sin[:, :, 0, :], -1.0, None, ALU.mult).then_inc(wsin_ready, 1)
            split_lo(pieces[4:6])
            layer_stats(1, 0, 1)
            dve.wait_ge(stats_done, 2)
            layer_var(1)
            turn_queries(0, 0, 0, 0)
            angles(3, X0 + 3)
            turn_keys(0, 0, 0)
            split_lo(pieces[8:9])

            def pair(i, first, last):
                for u in range(2 * KVH):
                    p, g = divmod(u, KVH)
                    t, n = 2 * i + p, 8 * i + u
                    end = last and p == 1
                    p1 = p if g < 3 else 1 - p
                    keys_out(n, g)
                    if first and u == KVH:
                        dve.wait_ge(st_trig, 16 * (NCH - 2))
                        nc.vector.memset(below_f[:], 1.0).then_inc(below_ready, 1)
                        nc.vector.memset(zeros[:], 0.0)
                        nc.vector.memset(seen[:].bitcast(F32), 0.0).then_inc(seen_ready, 1)
                        dve.wait_ge(below_ready, 1)
                        nc.vector.tensor_copy(ones[:], below_f[:]).then_inc(below_set, 1)
                        dve.wait_ge(wr_hi, 1)
                        nc.vector.tensor_tensor(wr_s[LO][:], wr_raw[:], wr_s[HI][:].bitcast(F32), ALU.subtract) \
                          .then_inc(wr_lo, 1)
                    if first and u == KVH + 2:
                        dve.wait_ge(below_cut, 2)
                        nc.vector.tensor_copy(below[:], below_f[:]).then_inc(below_ready, 1)
                    if g == 0 and not first:
                        weights_and_mask(t - 2)
                    if not (end and g == 3):
                        turn_queries(n + 1, g + 1, t + (g == 3), p1)
                    if g == 1 and not end:
                        normalize_x(t + 1, 1 - p)
                    if g == 1 and not (first and p == 0):
                        if first:
                            dve.wait_ge(gates_ready, 1)
                        residual(t - 1, i - 1 + p, 1 - p)
                    if g == 2 and not (first and p == 0):
                        normalize_y(t - 1, 1 - p)
                    score_max(n, g)
                    if g == 1 and not (first and p == 0):
                        layer_stats2(t - 1, 1 - p)
                        need(dve, stats2, t)
                    if g == 3 and not last:
                        layer_stats(t + 2, i + 1, p)
                        need(dve, stats_done, t + 3)
                    if not (end and g == 3):
                        turn_keys(n + 1, g + 1, p1)
                    if g == 0 and not first:
                        read_ranks(t - 2)
                    if g == 3 and not (first and p == 0):
                        copy_logits(t - 1)
                    if g == 1 and not end:
                        normed_lo(t + 1, 1 - p)
                    if g == 1 and end:
                        dve.wait_ge(early_done, 1)
                        nc.vector.tensor_copy(count[:], b_kT[:, D:D + E]).then_inc(early_read, 1)
                    if g == 2 and not (first and p == 0):
                        tokens_lo(t - 1, 1 - p)
                    if end and g == 3:
                        split2_lo(2)
                    if g == 3 and not (first and p == 0):
                        need(dve, lg_copied, t)
                    sum_inverse(n, g)
                    if first and u == 0:
                        split_lo(pieces[9:10])
                    if not (first and u == 0):
                        attended_lo(n - 1, g - 1)
                    if g == 0 and not first:
                        rows_of_tokens(t - 2, p)
                    if g == 0 and not end:
                        context_lo(t + 1, 1 - p)
                    if g == 1 and end:
                        dve.wait_ge(early_read, 1)
                        nc.vector.tensor_copy(first_pad[:], count[:]).then_inc(early_ready, 1)
                    if g == 1 and not (first and p == 0):
                        layer_var2()
                    if g == 3 and not (first and p == 0):
                        top_two(t - 1)
                    if g == 3 and not last:
                        layer_var(p)
                    if end and g == 2:
                        split2_lo(2)

            walk(dve, pair)
            T2, T1 = TILES - 2, TILES - 1
            weights_and_mask(T2)
            read_ranks(T2)
            rows_of_tokens(T2, 0)
            attended_lo(4 * TILES - 1, 3)
            split2_lo(1)
            residual(T1, PAIRS - 1, 1)
            layer_stats2(T1, 1)
            dve.wait_ge(stats2, TILES)
            layer_var2()
            split2_lo(1)
            normalize_y(T1, 1)
            tokens_lo(T1, 1)
            split2_lo(1)
            copy_logits(T1)
            dve.wait_ge(lg_copied, TILES)
            top_two(T1)
            weights_and_mask(T1)
            read_ranks(T1)
            rows_of_tokens(T1, 1)

            steps2 = [0]

            def then(ins):
                steps2[0] += 1
                ins.then_inc(table_step, 1)
                dve.wait_ge(table_step, steps2[0])

            V = nc.vector
            dve.wait_ge(count_done, 1)
            then(V.tensor_copy(count[:], b_count[:, 0:E]))
            then(V.tensor_scalar(full[:], count[:], 1 / P, (P - 1) / (2 * P), ALU.mult, ALU.add))
            then(V.tensor_scalar(full[:], full[:], ROUND, None, ALU.add))
            then(V.tensor_scalar(full[:], full[:], ROUND, None, ALU.subtract))
            then(V.tensor_copy(upto[0][:], full[:]))
            for n, d in enumerate((1, 2, 4)):
                V.tensor_copy(upto[n + 1][:, 0:d], upto[n][:, 0:d])
                then(V.tensor_tensor(upto[n + 1][:, d:E], upto[n][:, d:E], upto[n][:, 0:E - d], ALU.add))
            by_slot = [P, SLOTS, E]
            then(V.tensor_tensor(past[:], slot_no[:].unsqueeze(2).to_broadcast(by_slot),
                                 upto[3][:].unsqueeze(1).to_broadcast(by_slot), ALU.is_ge))
            V.tensor_tensor(past_w[:], past[:], full[:].unsqueeze(1).to_broadcast(by_slot), ALU.mult)
            then(V.tensor_reduce(s_expert[:], past[:], AX.X, ALU.add))
            then(V.tensor_reduce(s_first[:], past_w[:], AX.X, ALU.add))
            V.tensor_scalar(s_valid[:], s_expert[:], float(E), None, ALU.is_lt)
            then(V.tensor_tensor(s_a[:], slot_no[:], s_first[:], ALU.subtract))
            then(V.tensor_scalar(s_b[:], s_expert[:], float(STRIDE), None, ALU.mult))
            then(V.scalar_tensor_tensor(out=s_row[:], in0=s_a[:], scalar=float(P), in1=s_b[:], op0=ALU.mult, op1=ALU.add))
            V.tensor_tensor(slot_expert[:], s_expert[:], s_valid[:], ALU.mult)
            V.tensor_tensor(slot_row[:], s_row[:], s_valid[:], ALU.mult).then_inc(table_ready, 1)
            split2_lo(len(WG_PIECES) - 7)
            for p in range(2):
                for o in (P, P + AGAIN):
                    last = V.memset(s_hid[p][:, o + REST:o + AGAIN], 0.0)
            last.then_inc(s_pad_done, 1)

            def slot_lo(m, p):
                need(dve, sT_hi, m + 1)
                nc.vector.tensor_tensor(sT[p][LO][:].rearrange("p c n -> p (c n)"), b_sT[p][:, 0:D],
                                        sT[p][HI][:].rearrange("p c n -> p (c n)").bitcast(F32), ALU.subtract) \
                  .then_inc(sT_lo, 1)

            def slot_hidden(m, p):
                need(dve, s_silu_done, m + 1)
                nc.vector.tensor_tensor(s_hid[p][:, 0:P], s_silu[p][:, 0:P], b_sg[p][:, F:F + P], ALU.mult)
                twice = [P, 2, REST]
                nc.vector.tensor_tensor(s_hid[p][:, P:EFW].rearrange("p (a n) -> p a n", a=2)[:, :, 0:REST],
                                        s_silu[p][:, P:F].unsqueeze(1).to_broadcast(twice),
                                        b_sg[p][:, F + P:2 * F].unsqueeze(1).to_broadcast(twice), ALU.mult) \
                  .then_inc(s_hid_ready, 1)

            def slot_hidden_lo(m, p):
                need(dve, shT_hi, m + 1)
                hi, lo = s_hT[p]
                nc.vector.tensor_copy(lo[0:AGAIN, 1, :], hi[0:AGAIN, 1, :].bitcast(F32))
                nc.vector.tensor_tensor(lo[:, 0, :], b_shT[p][:, 0:P], hi[:, 0, :].bitcast(F32), ALU.subtract)
                nc.vector.tensor_tensor(lo[AGAIN:P, 1, :], b_shT[p][AGAIN:P, P:EFW], hi[AGAIN:P, 1, :].bitcast(F32),
                                        ALU.subtract).then_inc(shT_lo, 1)

            slot_lo(0, 0)
            slot_lo(1, 1)

            def slots(i, first, last):
                for p in range(2):
                    m = 2 * i + p
                    slot_hidden(m, p)
                    if not (first and p == 0):
                        slot_hidden_lo(m - 1, 1 - p)
                    if not last:
                        slot_lo(m + 2, p)
                    if first and p == 0:
                        by_token = [P, TILES * TOPK, E]
                        then(V.tensor_tensor(at_e[:], e_all[:].rearrange("p t j -> p (t j)").unsqueeze(2).to_broadcast(by_token),
                                             expert_no[:].unsqueeze(1).to_broadcast(by_token), ALU.is_equal))
                        then(V.tensor_tensor(upto[0][:], upto[3][:], full[:], ALU.subtract))
                        then(V.tensor_tensor(at_w[:], at_e[:], upto[0][:].unsqueeze(1).to_broadcast(by_token), ALU.mult))
                        then(V.tensor_reduce(at_s[:], at_w[:], AX.X, ALU.add))
                        then(V.scalar_tensor_tensor(out=at_f[:], in0=at_s[:], scalar=float(P),
                                                    in1=rank_all[:].rearrange("p t j -> p (t j)"), op0=ALU.mult,
                                                    op1=ALU.add))
                        V.tensor_copy(at_all[:].rearrange("p t j -> p (t j)"), at_f[:]).then_inc(at_ready, 1)

            walk(dve, slots, TURNS, start=2)
            slot_hidden_lo(SLOTS - 1, 1)

            for p in range(2):
                last = nc.vector.memset(hid[p][:, FS:FW], 0.0)
            last.then_inc(pad_done, 1)
            dve.wait_ge(w_ready, TILES)

            def hidden(t, p):
                need(dve, silu_done, t + 1)
                nc.vector.tensor_tensor(hid[p][:, 0:FS], silu[p][:], b_up[p][:, 0:FS], ALU.mult).then_inc(hid_ready, 1)

            def hidden_lo(t):
                need(dve, hT_hi, t + 1)
                nc.vector.tensor_tensor(hT[LO][:].rearrange("p c n -> p (c n)"), b_hT[:, 0:FW],
                                        hT[HI][:].rearrange("p c n -> p (c n)").bitcast(F32), ALU.subtract) \
                  .then_inc(hT_lo, 1)

            def weight(t, j):
                return w_all[:, bass.ds(t, 1), j:j + 1].rearrange("p a j -> p (a j)")

            def first_sum(t, i, p):
                dve.wait_ge(ld_x1[p], 16 * (i + 1))
                dve.wait_ge(ld_routed[p], 16 * TOPK * (i + 1))
                nc.vector.scalar_tensor_tensor(out=mix[0][:], in0=routed[p][0][:], scalar=weight(t, 0), in1=x1_in[p][:],
                                               op0=ALU.mult, op1=ALU.add).then_inc(mix_step, 1)

            def second_sum(t, p):
                need(dve, mix_step, 2 * t + 1)
                nc.vector.scalar_tensor_tensor(out=mix[1][:], in0=routed[p][1][:], scalar=weight(t, 1), in1=mix[0][:],
                                               op0=ALU.mult, op1=ALU.add).then_inc(mix_step, 1)

            def output(t, i, p):
                need(dve, mix_step, 2 * t + 2)
                need(dve, y_done, t + 1)
                if not isinstance(i, int) or i >= 1:
                    dve.wait_ge(st_out[p], 16 * i)
                nc.vector.scalar_tensor_tensor(out=o_out[p][:], in0=b_y[p][:, 0:D], scalar=gates[:, 1:2], in1=mix[1][:],
                                               op0=ALU.mult, op1=ALU.add).then_inc(out_ready, 1)

            def pair3(i, first, last):
                for p in range(2):
                    t = 2 * i + p
                    hidden(t, p)
                    if not (first and p == 0):
                        hidden_lo(t - 1)
                    if not first:
                        first_sum(t - 2, i - 1, p)
                        second_sum(t - 2, p)
                        output(t - 2, i - 1, p)

            walk(dve, pair3, start=2)
            hidden_lo(TILES - 1)
            for p in range(2):
                first_sum(TILES - 2 + p, PAIRS - 1, p)
                second_sum(TILES - 2 + p, p)
                output(TILES - 2 + p, PAIRS - 1, p)

        @block.tensor
        def _(pe):
            pe.wait_ge(ident_done, 1)

            def normed_x_T(t, p):
                need(pe, x_normed, t + 1)
                for c in range(DC):
                    last = nc.tensor.transpose(b_kT[:, (DC + c) * P:(DC + c + 1) * P], x_n[:, c * P:(c + 1) * P],
                                               ident[:])
                last.then_inc(xT_done, 1)

            def queries(n, g, t, p):
                need(pe, q_turned, n)
                if g % KVH == 0:
                    need(pe, x_lo, t + 1)
                gg = g % KVH
                for c in range(DC):
                    for a, b in PASSES:
                        last = nc.tensor.matmul(b_q[:], kv_in[p][a][:, c, 1:3, :],
                                                wq_s[b][:, c, gg * REP * HD:(gg + 1) * REP * HD],
                                                start=(c == 0 and (a, b) == PASSES[0]),
                                                stop=(c == DC - 1 and (a, b) == PASSES[-1]))
                last.then_inc(q_done, 1)

            def keys_values(n, g, t, p):
                need(pe, k_turned, n)
                if g % KVH == 0:
                    need(pe, ctx_lo, t + 1)
                for s in range(NB):
                    for c in range(DC):
                        for a, b in PASSES:
                            last = nc.tensor.matmul(b_kv[:, s * 2 * HD:(s + 1) * 2 * HD],
                                                    kv_in[p][a][:, c, 2 * s:2 * s + 2, :],
                                                    wkv_s[b][:, c, g % KVH, :],
                                                    start=(c == 0 and (a, b) == PASSES[0]),
                                                    stop=(c == DC - 1 and (a, b) == PASSES[-1]))
                last.then_inc(kv_done, 1)

            def heads_T(n, g):
                need(pe, k_ready, n + 1)
                for s in range(NB):
                    last = nc.tensor.transpose(b_kT[:, s * P:(s + 1) * P], k_rot[g % 2][:, s, :], ident[:])
                last.then_inc(kT_done, 1)
                need(pe, q_ready, n + 1)
                for h in range(REP):
                    last = nc.tensor.transpose(b_qT[:, h * P:(h + 1) * P], q_rot[g % 2][:, h, :], ident[:])
                last.then_inc(qT_done, 1)

            def scores(n, g):
                need(pe, exp_done, n)
                need(pe, k_out, n + 1)
                need(pe, q_out, n + 1)
                for s in range(NB):
                    for j in range(REP // 2):
                        o = (s * (REP // 2) + j) * P
                        last = nc.tensor.matmul(b_sc[:, o:o + P], qT[:, s, 2 * j:2 * j + 2, :], kT[:, s, :],
                                                start=True, stop=True)
                last.then_inc(sc_done, 1)

            def probs_T(n, g):
                need(pe, p_normed, n + 1)
                need(pe, p_normed2, n + 1)
                for j in range(REP):
                    last = nc.tensor.transpose(b_pT[:, j * P:(j + 1) * P], probs[:, j, :], ident[:])
                last.then_inc(pT_done, 1)

            def attend(n, g):
                need(pe, v_out, n + 1)
                need(pe, pT_out, n + 1)
                for s in range(NB):
                    last = nc.tensor.matmul(b_aT[:, s * REP * S:(s + 1) * REP * S], v_s[g % KVH][:, s, :],
                                            pT[:, s, :], start=True, stop=True)
                last.then_inc(aT_done, 1)

            def project(n, g, t):
                gg = g % KVH
                need(pe, aT_lo, n + 1)
                if gg == 0:
                    need(pe, x1_ready, t)
                for h in range(REP):
                    for a, b in PASSES:
                        last = nc.tensor.matmul(b_o[:, 0:D], aT[a][:, h, :, :], wo_s[b][:, gg * REP + h, :],
                                                start=(gg == 0 and h == 0 and (a, b) == PASSES[0]),
                                                stop=(gg == KVH - 1 and h == REP - 1 and (a, b) == PASSES[-1]))
                last.then_inc(o_done, 1)

            normed_x_T(0, 0)
            pe.wait_ge(w_lo, QUERY_SPLITS[0])
            queries(0, 0, 0, 0)
            pe.wait_ge(w_lo, KV_SPLITS)
            keys_values(0, 0, 0, 0)
            pe.wait_ge(w_lo, QUERY_SPLITS[1])
            queries(1, 1, 0, 0)
            keys_values(1, 1, 0, 0)

            def pair(i, first, last):
                for u in range(2 * KVH):
                    p, g = divmod(u, KVH)
                    t, n = 2 * i + p, 8 * i + u
                    end = last and p == 1
                    t2, p2 = t + (g >= 2), (p if g < 2 else 1 - p)
                    if g == 2 and not end:
                        need(pe, x_lo, t + 2)
                    if g == 2 and end:
                        pe.wait_ge(early_read, 1)
                    if g == 3 and not (first and p == 0):
                        need(pe, yT_lo, t)
                    if g == 0 and not first:
                        need(pe, lg_copied, t - 1)
                    if g == 1 and not first:
                        need(pe, rk_read, t - 1)
                    heads_T(n, g)
                    if first and u == 2:
                        pe.wait_ge(wo_lo, WO_SPLITS)
                    if not (first and u < 2):
                        project(n - 2, g - 2, t if g >= 2 else t - 1)
                    scores(n, g)
                    if g == 0 and not first:
                        ranks(t - 2)
                    if g == 2 and not (first and p == 0):
                        tokens_T(t - 1, 1 - p)
                    if g == 3 and not (first and p == 0):
                        router(t - 1, 1 - p)
                    if g == 1 and not end:
                        normed_x_T(t + 1, 1 - p)
                    if g == 1 and end:
                        pe.wait_ge(seen_ready, TILES - PAD_TILES + 1)
                        nc.tensor.matmul(b_kT[:, D:D + E], ones[:], seen[:], start=True, stop=True).then_inc(early_done, 1)
                    if not (first and u < 1):
                        probs_T(n - 1, g - 1)
                    if first and u < 2:
                        pe.wait_ge(w_lo, QUERY_SPLITS[u + 2])
                    if not (end and g >= 2):
                        queries(n + 2, g + 2, t2, p2)
                    if not (first and u < 1):
                        attend(n - 1, g - 1)
                    if not (end and g >= 2):
                        keys_values(n + 2, g + 2, t2, p2)

            def tokens_T(t, p):
                need(pe, y_normed, t + 1)
                for c in range(DC):
                    last = nc.tensor.transpose(b_kT[:, D + c * P:D + (c + 1) * P], y_n[p][:, c * P:(c + 1) * P], ident[:])
                last.then_inc(yT_done, 1)

            def router(t, p):
                if isinstance(t, int) and t == 0:
                    pe.wait_ge(wr_lo, 1)
                need(pe, yT_lo, t + 1)
                for c in range(DC):
                    for a in (HI, LO):
                        last = nc.tensor.matmul(b_kT[:, D:D + 2 * E], yT[p][a][:, c, :],
                                                wr_both[:, c, :, :].rearrange("p a e -> p (a e)"),
                                                start=(c == 0 and a == HI), stop=(c == DC - 1 and a == LO))
                last.then_inc(lg_done, 1)

            def ranks(t):
                need(pe, mask_ready, t + 1)
                need(pe, seen_ready, t + 1)
                nc.tensor.matmul(b_kT[:, D:D + E], below[:], mask[:], start=True, stop=False)
                nc.tensor.matmul(b_kT[:, D:D + E], ones[:], seen[:], start=False, stop=True).then_inc(rk_done, 1)

            walk(pe, pair)
            pe.wait_ge(lg_copied, TILES - 1)
            ranks(TILES - 2)
            project(4 * TILES - 2, 2, TILES - 1)
            probs_T(4 * TILES - 1, 3)
            attend(4 * TILES - 1, 3)
            project(4 * TILES - 1, 3, TILES - 1)
            pe.wait_ge(rk_read, TILES - 1)
            tokens_T(TILES - 1, 1)
            router(TILES - 1, 1)
            pe.wait_ge(lg_copied, TILES)
            ranks(TILES - 1)
            pe.wait_ge(seen_ready, TILES + 1)
            nc.tensor.matmul(b_count[:, 0:E], ones[:], seen[:], start=True, stop=True).then_inc(count_done, 1)
            pe.wait_ge(rk_read, TILES)

            def slot_T(m, i, p):
                pe.wait_ge(ld_slot[p], 16 * (i + 1))
                for c in range(DC):
                    last = nc.tensor.transpose(b_sT[p][:, c * P:(c + 1) * P], s_in[p][:, c * P:(c + 1) * P], ident[:])
                last.then_inc(sT_done, 1)

            expert = [pe.alloc_register(f"expert{q}") for q in range(QUAD)]
            expert_down = [pe.alloc_register(f"expert_down{r}") for r in range(3)]

            def keep_experts():
                for r in range(3):
                    pe.reg_mov(expert_down[r], expert[QUAD - 3 + r])

            def load_experts(k):
                pe.reg_load(expert, slot_expert[0:1, bass.ds(QUAD * k, QUAD)])

            def slot_gate_up(m, p, of):
                e = pe.snap(of, min_val=0, max_val=E - 1)
                need(pe, sT_lo, m + 1)
                for c in range(DC):
                    for a, b in PASSES:
                        last = nc.tensor.matmul(b_sg[p][:, 0:2 * F], sT[p][a][:, c, :],
                                                wg_s[b][:, c, bass.ds(e * (2 * F) + 2 * FS, 2 * F)],
                                                start=(c == 0 and (a, b) == PASSES[0]),
                                                stop=(c == DC - 1 and (a, b) == PASSES[-1]))
                last.then_inc(sg_done, 1)

            def slot_hidden_T(m, p):
                need(pe, s_hid_ready, m + 1)
                for c in range(EFC):
                    last = nc.tensor.transpose(b_shT[p][:, c * P:(c + 1) * P], s_hid[p][:, c * P:(c + 1) * P], ident[:])
                last.then_inc(shT_done, 1)

            def slot_down(m, p, of):
                e = pe.snap(of, min_val=0, max_val=E - 1)
                need(pe, shT_lo, m + 1)
                out, hT, w = b_sy[p][:, 0:D], s_hT[p], [part[:, bass.ds(e * EFC + FC, EFC), :] for part in wd_s]
                for a, b in PASSES:
                    nc.tensor.matmul(out, hT[a][:, 0, :], w[b][:, 0, :], start=((a, b) == PASSES[0]), stop=False)
                rows = AGAIN + REST
                nc.tensor.matmul(out, hT[LO][0:rows, 1, :], w[HI][0:rows, 1, :], start=False, stop=False)
                last = nc.tensor.matmul(out, hT[HI][0:REST, 1, :], w[LO][0:REST, 1, :], start=False, stop=True)
                last.then_inc(sy_done, 1)

            pe.wait_ge(table_ready, 1)
            load_experts(0)
            for p in range(2):
                slot_T(p, 0, p)
            pe.wait_ge(wg_lo_done, len(WG_PIECES))
            pe.wait_ge(s_pad_done, 1)

            def slots(k, first, last):
                for q in range(QUAD):
                    r, p = divmod(q, 2)
                    m, i = QUAD * k + q, QUAD // 2 * k + r
                    slot_gate_up(m, p, expert[q])
                    if q == QUAD - 1:
                        keep_experts()
                        if not last:
                            load_experts(k + 1)
                    if not (first and q == 0):
                        slot_hidden_T(m - 1, 1 - p)
                    if not (last and q >= QUAD - 2):
                        slot_T(m + 2, i + 1, p)
                    if first and q == 2:
                        pe.wait_ge(wd_lo_done, len(WD_PIECES))
                    if not (first and q < 2):
                        slot_down(m - 2, p, expert_down[(q + 1) % QUAD] if q in (0, 1, QUAD - 1) else expert[q - 2])

            def gate_up(t, i, p):
                pe.wait_ge(ld_yT[p], 16 * (i + 1))
                need(pe, hid_ready, t - 1)
                for j, o in enumerate((b_gate[p], b_up[p])):
                    for c in range(DC):
                        for a, b in PASSES:
                            last = nc.tensor.matmul(o[:, 0:FS], yT[p][a][:, c, :], wg_s[b][:, c, j * FS:(j + 1) * FS],
                                                    start=(c == 0 and (a, b) == PASSES[0]),
                                                    stop=(c == DC - 1 and (a, b) == PASSES[-1]))
                last.then_inc(gu_done, 1)

            walk(pe, slots, SLOTS // QUAD, start=1)
            slot_hidden_T(SLOTS - 1, 1)
            slot_down(SLOTS - 2, 0, expert_down[1])
            pe.wait_ge(s_hid_ready, SLOTS - 1)
            pe.wait_ge(shT_lo, SLOTS - 1)
            gate_up(0, 0, 0)
            slot_down(SLOTS - 1, 1, expert_down[2])

            pe.wait_ge(s_hid_ready, SLOTS)
            pe.wait_ge(shT_lo, SLOTS)
            pe.wait_ge(pad_done, 1)

            def hidden_T(t, p):
                need(pe, hid_ready, t + 1)
                need(pe, hT_lo, t)
                for c in range(FC):
                    last = nc.tensor.transpose(b_hT[:, c * P:(c + 1) * P], hid[p][:, c * P:(c + 1) * P], ident[:])
                last.then_inc(hT_done, 1)

            def down(t, p):
                need(pe, hT_lo, t + 1)
                need(pe, out_ready, t - 1)
                for c in range(FC):
                    rows = min(P, FS - c * P)
                    for a, b in PASSES:
                        last = nc.tensor.matmul(b_y[p][:, 0:D], hT[a][0:rows, c, :], wd_s[b][0:rows, c, :],
                                                start=(c == 0 and (a, b) == PASSES[0]),
                                                stop=(c == FC - 1 and (a, b) == PASSES[-1]))
                last.then_inc(y_done, 1)

            def pair3(i, first, last):
                for p in range(2):
                    t = 2 * i + p
                    if first and p == 0:
                        pe.wait_ge(s_out_ready, SLOTS)
                        continue
                    gate_up(t, i, p)
                    if not first:
                        down(t - 2, p)
                    if not (first and p == 0):
                        hidden_T(t - 1, 1 - p)

            walk(pe, pair3, start=2)
            down(TILES - 2, 0)
            hidden_T(TILES - 1, 1)
            down(TILES - 1, 1)


def kernel(x, ctx_2048, pos_BxS2, itok_BxS_4096_4607, g_xattn, g_ffn, L0_xattn_Wq, L0_xattn_Wk, L0_xattn_Wv,
           L0_xattn_Wo, L0_xattn_q_norm_w, L0_xattn_k_norm_w, L0_ffn_w_router, L0_ffn_w_gate, L0_ffn_w_up,
           L0_ffn_w_down, L0_ffn_ws_gate, L0_ffn_ws_up, L0_ffn_ws_down):
    import numpy as np
    import concourse.bacc as bacc
    from concourse.bass_utils import run_bass_kernel_spmd as run

    def arr(a):
        return np.asarray(a)

    def chunked(w):
        return w.reshape(DC, P, -1).transpose(1, 0, 2)

    wk, wv = arr(L0_xattn_Wk).T, arr(L0_xattn_Wv).T
    wkv = np.stack([wk.reshape(D, KVH, HD), wv.reshape(D, KVH, HD)], 2)
    gate, up, down = arr(L0_ffn_w_gate), arr(L0_ffn_w_up), arr(L0_ffn_w_down)
    gu = [arr(L0_ffn_ws_gate), arr(L0_ffn_ws_up)]
    gu += [w[e] for e in range(E) for w in (gate, up)]
    gap = np.zeros((AGAIN - REST, D), down.dtype)
    dn = [arr(L0_ffn_ws_down)] + [np.concatenate([w, gap, w[P:F]], 0) for w in down]
    dn = [np.concatenate([w, np.zeros((-w.shape[0] % P, D), w.dtype)], 0).reshape(-1, P, D) for w in dn]
    inv_freq = (np.float32(1.0) / np.float32(10000.0) ** (np.arange(0, HD, 2, dtype=np.float32) / np.float32(HD)))
    ins = {
        "x": arr(x).reshape(TILES, P, D),
        "ctxT": arr(ctx_2048).reshape(TILES, P, DC, P).transpose(0, 3, 2, 1),
        "posx": arr(itok_BxS_4096_4607).reshape(TILES, P).T,
        "posc": arr(pos_BxS2).reshape(TILES, P).T,
        "invf": np.broadcast_to(inv_freq.astype(np.float32), (P, HALF)),
        "g_xattn": arr(g_xattn), "g_ffn": arr(g_ffn),
        "q_w": arr(L0_xattn_q_norm_w), "k_w": arr(L0_xattn_k_norm_w),
        "wq": chunked(arr(L0_xattn_Wq).T),
        "wkv": chunked(wkv.reshape(D, KVH * 2 * HD)).reshape(P, DC, KVH, 2 * HD),
        "wo": arr(L0_xattn_Wo).T.reshape(H, P, D).transpose(1, 0, 2),
        "wr": chunked(arr(L0_ffn_w_router)),
        "wg": chunked(np.concatenate(gu, 1)),
        "wd": np.concatenate(dn, 0).transpose(1, 0, 2),
    }
    nc = bacc.Bacc("TRN2", target_bir_lowering=False, num_devices=1)
    arrays, aps = {}, []
    for name, a in ins.items():
        arrays[f"in_{name}"] = np.ascontiguousarray(a)
        aps.append(nc.dram_tensor(f"in_{name}", a.shape, mybir.dt.from_np(a.dtype), kind="ExternalInput").ap())
    out = nc.dram_tensor("out", (TILES, P, D), F32, kind="ExternalOutput").ap()
    flamingo(nc, *aps, out)
    got = run(nc, [arrays], core_ids=[0]).results[0]["out"]
    return got.reshape(B, S, D)
```
